# Optimizing a Trainium2 kernel written in Bass

```python
import numpy as np
import jax
import jax.numpy as jnp

def _softmax(x, axis=-1):
    return jax.nn.softmax(x, axis=axis)

def _gelu(x):
    return jax.nn.gelu(x, approximate=True)

def _silu(x):
    return jax.nn.silu(x)

def _sigmoid(x):
    return jax.nn.sigmoid(x)

def _layernorm(x, axis=-1, eps=1e-05):
    m = jnp.mean(x, axis=axis, keepdims=True)
    v = jnp.var(x, axis=axis, keepdims=True)
    return (x - m) / jnp.sqrt(v + eps)

def _scatter_add(tgt, idx, src, axis=0):
    return tgt.at[idx].add(src)

def _segment_sum(src, seg, n):
    return jax.ops.segment_sum(src, seg, n)
kernel_name = 'mk_perceiver_d4_seqx_r4_c9b012'

def setup_inputs(seed: int=0):
    np.random.seed(seed)
    _w = jnp.asarray

    def _rec_inputs():
        import jax
        import jax.numpy as jnp
        _rk = jax.random.key(seed)
        x = -0.0002928 + 1 * jax.random.normal(jax.random.fold_in(_rk, 1), (32, 32, 256), jnp.float32)
        _lenS = 32 - jax.random.randint(jax.random.fold_in(_rk, 7), (32,), 0, max(1, 32 // 4) + 1, jnp.int32)
        _lenS2 = 257 - jax.random.randint(jax.random.fold_in(_rk, 8), (32,), 0, max(1, 257 // 4) + 1, jnp.int32)
        _ctx_768P = jax.random.normal(jax.random.fold_in(_rk, 11), (32, 16, 192), jnp.float32)
        _ctx_768c = jax.random.dirichlet(jax.random.fold_in(_rk, 511), 0.3 * jnp.ones((16,), jnp.float32), (32, 257))
        _ctx_768t = jnp.einsum('bsk,bkd->bsd', _ctx_768c, _ctx_768P)
        _ctx_768t = _ctx_768t * jax.lax.rsqrt(jnp.mean(jnp.square(_ctx_768t)) + 1e-12) * 0.953939
        ctx_768 = 2.09791e-05 + 1.00001 * (_ctx_768t + 0.3 * jax.random.normal(jax.random.fold_in(_rk, 611), (32, 257, 192), jnp.float32))
        return (x, ctx_768)
    x, ctx_768 = _rec_inputs()

    def _L0_xattn_setup():
        import jax, jax.numpy as jnp
        import numpy as np
        EMBED_DIM = 256
        Q_DIM = 256
        KV_DIM = 192
        NUM_HEADS = 16
        HEAD_DIM = EMBED_DIM // NUM_HEADS
        SCALE = NUM_HEADS ** (-0.5)

        def _linear_params(key, in_dim, out_dim):
            kw, kb = jax.random.split(key)
            bound = 1.0 / np.sqrt(in_dim)
            W = jax.random.uniform(kw, (in_dim, out_dim), minval=-bound, maxval=bound, dtype=jnp.float32)
            b = jax.random.uniform(kb, (out_dim,), minval=-bound, maxval=bound, dtype=jnp.float32)
            return (W, b)
        key = jax.random.key(seed)
        ks = jax.random.split(key, 8)
        B, N1, N2 = (2, 512, 512)
        query = jax.random.normal(ks[0], (B, N1, Q_DIM), dtype=jnp.float32)
        k_in = jax.random.normal(ks[1], (B, N2, KV_DIM), dtype=jnp.float32)
        v_in = jax.random.normal(ks[2], (B, N2, KV_DIM), dtype=jnp.float32)
        Wq, bq = _linear_params(ks[3], Q_DIM, EMBED_DIM)
        Wk, bk = _linear_params(ks[4], KV_DIM, EMBED_DIM)
        Wv, bv = _linear_params(ks[5], KV_DIM, EMBED_DIM)
        Wo, bo = _linear_params(ks[6], EMBED_DIM, EMBED_DIM)
        return {'query': query, 'key': k_in, 'value': v_in, 'Wq': Wq, 'bq': bq, 'Wk': Wk, 'bk': bk, 'Wv': Wv, 'bv': bv, 'Wo': Wo, 'bo': bo}
    _L0_xattn_all = _L0_xattn_setup()
    _L0_xattn_in = {k: v for k, v in _L0_xattn_all.items() if k in ('Wq', 'bq', 'Wk', 'bk', 'Wv', 'bv', 'Wo', 'bo')}
    del _L0_xattn_all

    def _L0_attn_setup():
        import math
        import jax, jax.numpy as jnp
        import numpy as np
        B, S, D, H = (2, 512, 256, 16)
        HD = D // H
        LAMBDA_MAX = 0.5
        AMP_EPS = 1e-06

        def _amp_norm(t):
            a = jax.nn.softplus(t)
            return a / jnp.sqrt(jnp.mean(a * a, axis=-1, keepdims=True) + AMP_EPS)
        key = jax.random.key(seed)
        ks = jax.random.split(key, 8)
        x = jax.random.normal(ks[0], (B, S, D), jnp.float32)
        w = lambda k, std: std * jax.random.normal(k, (D, D), jnp.float32)
        return {'x': x, 'Wq': w(ks[1], 0.02), 'Wk': w(ks[2], 0.02), 'Wv': w(ks[3], 0.02), 'Wo': w(ks[4], 0.02), 'Wqp': w(ks[5], 0.005), 'Wkp': w(ks[6], 0.005), 'lambda_raw': jnp.full((H,), float(np.arctanh(0.5)), jnp.float32)}
    _L0_attn_all = _L0_attn_setup()
    _L0_attn_in = {k: v for k, v in _L0_attn_all.items() if k in ('Wq', 'Wk', 'Wv', 'Wo', 'Wqp', 'Wkp', 'lambda_raw')}
    del _L0_attn_all

    def _L0_ffn_setup():
        import jax, jax.numpy as jnp
        import numpy as np
        B, T, D = (4, 256, 256)
        E = 8
        K = 2
        H = 4 * D
        key = jax.random.key(seed)
        ks = jax.random.split(key, 7)
        s_in = 1.0 / np.sqrt(D)
        s_h = 1.0 / np.sqrt(H)
        return {'x': jax.random.normal(ks[0], (B, T, D), dtype=jnp.float32), 'gate_w': jax.random.uniform(ks[1], (D, E), jnp.float32, -s_in, s_in), 'gate_b': jax.random.uniform(ks[2], (E,), jnp.float32, -s_in, s_in), 'w1': jax.random.uniform(ks[3], (E, D, H), jnp.float32, -s_in, s_in), 'b1': jax.random.uniform(ks[4], (E, H), jnp.float32, -s_in, s_in), 'w2': jax.random.uniform(ks[5], (E, H, D), jnp.float32, -s_h, s_h), 'b2': jax.random.uniform(ks[6], (E, D), jnp.float32, -s_h, s_h)}
    _L0_ffn_all = _L0_ffn_setup()
    _L0_ffn_in = {k: v for k, v in _L0_ffn_all.items() if k in ('gate_w', 'gate_b', 'w1', 'b1', 'w2', 'b2')}
    del _L0_ffn_all

    def _L1_xattn_setup():
        import jax, jax.numpy as jnp
        import numpy as np
        NUM_HEADS = 16
        CLAMP = 10000.0
        key = jax.random.key(seed)
        ks = jax.random.split(key, 8)
        B, Nq, Nkv, Cq, Ckv = (4, 512, 512, 256, 192)
        s_q = 1.0 / np.sqrt(Cq)
        s_kv = 1.0 / np.sqrt(Ckv)
        return {'query': jax.random.normal(ks[0], (B, Nq, Cq), jnp.float32), 'key_value': jax.random.normal(ks[1], (B, Nkv, Ckv), jnp.float32), 'Wq': jax.random.normal(ks[2], (Cq, Cq), jnp.float32) * s_q, 'bq': jnp.zeros((Cq,), jnp.float32), 'Wk': jax.random.normal(ks[3], (Ckv, Cq), jnp.float32) * s_kv, 'bk': jnp.zeros((Cq,), jnp.float32), 'Wv': jax.random.normal(ks[4], (Ckv, Cq), jnp.float32) * s_kv, 'bv': jnp.zeros((Cq,), jnp.float32), 'Wo': jax.random.normal(ks[5], (Cq, Cq), jnp.float32) * s_q, 'bo': jnp.zeros((Cq,), jnp.float32)}
    _L1_xattn_all = _L1_xattn_setup()
    _L1_xattn_in = {k: v for k, v in _L1_xattn_all.items() if k in ('Wq', 'bq', 'Wk', 'bk', 'Wv', 'bv', 'Wo', 'bo')}
    del _L1_xattn_all

    def _L1_attn_setup():
        import jax, jax.numpy as jnp
        import numpy as np
        B, S, D, H = (4, 512, 256, 16)
        HD = D // H
        LN_EPS = 1e-05
        KERN_EPS = 1e-06

        def kernel_func(q, k):
            scores = jnp.einsum('bhqd,bhkd->bhqk', q, k) / jnp.sqrt(jnp.asarray(HD, q.dtype))
            w = jax.nn.relu(scores)
            return w / (jnp.sum(w, axis=-1, keepdims=True) + KERN_EPS)
        key = jax.random.key(seed)
        k1, k2, k3 = jax.random.split(key, 3)
        scale = 1.0 / np.sqrt(D)
        return {'x': jax.random.normal(k1, (B, S, D), dtype=jnp.float32), 'w_qkv': jax.random.normal(k2, (D, 3 * D), dtype=jnp.float32) * scale, 'w_out': jax.random.normal(k3, (D, D), dtype=jnp.float32) * scale, 'b_out': jnp.zeros((D,), dtype=jnp.float32), 'gamma': jnp.ones((D,), dtype=jnp.float32), 'beta': jnp.zeros((D,), dtype=jnp.float32)}
    _L1_attn_all = _L1_attn_setup()
    _L1_attn_in = {k: v for k, v in _L1_attn_all.items() if k in ('w_qkv', 'w_out', 'b_out', 'gamma', 'beta')}
    del _L1_attn_all

    def _L1_ffn_setup():
        import jax, jax.numpy as jnp
        import numpy as np
        N_EXPERTS = 16
        TOP_K = int(N_EXPERTS * 0.2)
        EPS = 1e-12
        key = jax.random.key(seed)
        ks = jax.random.split(key, 6)
        B, T, D, H, E = (4, 256, 256, 512, N_EXPERTS)
        x = jax.random.normal(ks[0], (B, T, D), dtype=jnp.float32)
        gate = jax.random.normal(ks[1], (D, E), dtype=jnp.float32)
        W1 = jax.random.normal(ks[2], (E, D, H), dtype=jnp.float32) * (1.0 / np.sqrt(D))
        b1 = jax.random.normal(ks[3], (E, H), dtype=jnp.float32) * 0.02
        W2 = jax.random.normal(ks[4], (E, H, D), dtype=jnp.float32) * (1.0 / np.sqrt(H))
        b2 = jax.random.normal(ks[5], (E, D), dtype=jnp.float32) * 0.02
        return {'x': x, 'gate': gate, 'W1': W1, 'b1': b1, 'W2': W2, 'b2': b2}
    _L1_ffn_all = _L1_ffn_setup()
    _L1_ffn_in = {k: v for k, v in _L1_ffn_all.items() if k in ('gate', 'W1', 'b1', 'W2', 'b2')}
    del _L1_ffn_all

    def _L2_xattn_setup():
        import jax, jax.numpy as jnp
        import numpy as np
        QUERY_DIM = 256
        CONTEXT_DIM = 192
        HEADS = 8
        DIM_HEAD = 64
        INNER = HEADS * DIM_HEAD
        key = jax.random.key(seed)
        ks = jax.random.split(key, 7)
        B, S, L = (8, 1024, 77)
        x = jax.random.normal(ks[0], (B, S, QUERY_DIM), dtype=jnp.float32)
        context = jax.random.normal(ks[1], (B, L, CONTEXT_DIM), dtype=jnp.float32)
        Wq = jax.random.normal(ks[2], (QUERY_DIM, INNER), dtype=jnp.float32) * QUERY_DIM ** (-0.5)
        Wk = jax.random.normal(ks[3], (CONTEXT_DIM, INNER), dtype=jnp.float32) * CONTEXT_DIM ** (-0.5)
        Wv = jax.random.normal(ks[4], (CONTEXT_DIM, INNER), dtype=jnp.float32) * CONTEXT_DIM ** (-0.5)
        Wo = jax.random.normal(ks[5], (INNER, QUERY_DIM), dtype=jnp.float32) * INNER ** (-0.5)
        bo = jax.random.normal(ks[6], (QUERY_DIM,), dtype=jnp.float32) * 0.01
        return {'x': x, 'context': context, 'Wq': Wq, 'Wk': Wk, 'Wv': Wv, 'Wo': Wo, 'bo': bo}
    _L2_xattn_all = _L2_xattn_setup()
    _L2_xattn_in = {k: v for k, v in _L2_xattn_all.items() if k in ('Wq', 'Wk', 'Wv', 'Wo', 'bo')}
    del _L2_xattn_all

    def _L2_attn_setup():
        import jax, jax.numpy as jnp
        import numpy as np
        EPS = 1e-05

        def _ln(x, g, b):
            m = jnp.mean(x, axis=-1, keepdims=True)
            v = jnp.mean((x - m) ** 2, axis=-1, keepdims=True)
            return (x - m) * jax.lax.rsqrt(v + EPS) * g + b

        def _forward(x, ln_attn_g, ln_attn_b, Wq, bq, Wk, bk, Wv, bv, ln_conv_g, ln_conv_b, conv_w, conv_b, ln_boom_g, ln_boom_b, Wb, bb, Wu, bu):
            B, S, D = x.shape
            K = conv_w.shape[-1]
            G = D // conv_w.shape[1]
            h = _ln(x, ln_conv_g, ln_conv_b)
            hc = jnp.transpose(h, (0, 2, 1))
            hc = jnp.pad(hc, ((0, 0), (0, 0), (K - 1, 0)))
            conv = jax.lax.conv_general_dilated(hc, conv_w, window_strides=(1,), padding='VALID', dimension_numbers=('NCH', 'OIH', 'NCH'), feature_group_count=G)
            conv = conv + conv_b[None, :, None]
            x = x + jnp.transpose(conv, (0, 2, 1))
            h = _ln(x, ln_attn_g, ln_attn_b)
            q = jnp.einsum('bsd,ed->bse', h, Wq) + bq
            k = jnp.einsum('bsd,ed->bse', h, Wk) + bk
            v = jnp.einsum('bsd,ed->bse', h, Wv) + bv
            scale = jnp.arange(1, S + 1, dtype=x.dtype)[None, :, None]
            pooled_q = jnp.cumsum(q, axis=1) / scale
            pooled_k = jnp.cumsum(pooled_q * k, axis=1) / scale
            x = x + pooled_k * v
            h = _ln(x, ln_boom_g, ln_boom_b)
            h = jax.nn.gelu(jnp.einsum('bsd,ed->bse', h, Wb) + bb, approximate=False)
            h = jnp.einsum('bse,de->bsd', h, Wu) + bu
            return x + h
        key = jax.random.key(seed)
        ks = jax.random.split(key, 8)
        B, S, D, K, G = (4, 512, 256, 4, 4)
        w = lambda k, shape: jax.random.normal(k, shape, jnp.float32) * 0.02
        return {'hidden_states': jax.random.normal(ks[0], (B, S, D), jnp.float32), 'attention_mask': jnp.ones((B, S), jnp.int32), 'ln_attn_g': jnp.ones((D,), jnp.float32), 'ln_attn_b': jnp.zeros((D,), jnp.float32), 'Wq': w(ks[1], (D, D)), 'bq': jnp.zeros((D,), jnp.float32), 'Wk': w(ks[2], (D, D)), 'bk': jnp.zeros((D,), jnp.float32), 'Wv': w(ks[3], (D, D)), 'bv': jnp.zeros((D,), jnp.float32), 'ln_conv_g': jnp.ones((D,), jnp.float32), 'ln_conv_b': jnp.zeros((D,), jnp.float32), 'conv_w': w(ks[4], (D, D // G, K)), 'conv_b': jnp.zeros((D,), jnp.float32), 'ln_boom_g': jnp.ones((D,), jnp.float32), 'ln_boom_b': jnp.zeros((D,), jnp.float32), 'Wb': w(ks[5], (4 * D, D)), 'bb': jnp.zeros((4 * D,), jnp.float32), 'Wu': w(ks[6], (D, 4 * D)), 'bu': jnp.zeros((D,), jnp.float32)}
    _L2_attn_all = _L2_attn_setup()
    _L2_attn_in = {k: v for k, v in _L2_attn_all.items() if k in ('attention_mask', 'ln_attn_g', 'ln_attn_b', 'Wq', 'bq', 'Wk', 'bk', 'Wv', 'bv', 'ln_conv_g', 'ln_conv_b', 'conv_w', 'conv_b', 'ln_boom_g', 'ln_boom_b', 'Wb', 'bb', 'Wu', 'bu')}
    del _L2_attn_all

    def _L2_ffn_setup():
        import jax, jax.numpy as jnp
        import numpy as np
        TOP_K = 2
        key = jax.random.key(seed)
        ks = jax.random.split(key, 6)
        B, S, D, E = (8, 1024, 256, 8)
        s = 1.0 / np.sqrt(D)
        return {'x': jax.random.normal(ks[0], (B, S, D), dtype=jnp.float32), 'Wr': jax.random.normal(ks[1], (D, E), dtype=jnp.float32) * s, 'br': jnp.zeros((E,), dtype=jnp.float32), 'W1': jax.random.normal(ks[2], (E, D, D), dtype=jnp.float32) * s, 'b1': jnp.zeros((E, D), dtype=jnp.float32), 'W2': jax.random.normal(ks[3], (E, D, D), dtype=jnp.float32) * s, 'b2': jnp.zeros((E, D), dtype=jnp.float32)}
    _L2_ffn_all = _L2_ffn_setup()
    _L2_ffn_in = {k: v for k, v in _L2_ffn_all.items() if k in ('Wr', 'br', 'W1', 'b1', 'W2', 'b2')}
    del _L2_ffn_all

    def _L3_xattn_setup():
        import jax, jax.numpy as jnp
        import numpy as np
        IMG_DIM, TXT_DIM, HID = (256, 192, 256)
        B, LQ, LK = (8, 512, 512)
        key = jax.random.key(seed)
        ks = jax.random.split(key, 8)
        s_img = 1.0 / np.sqrt(IMG_DIM)
        s_txt = 1.0 / np.sqrt(TXT_DIM)
        return {'image_features': jax.random.normal(ks[0], (B, LQ, IMG_DIM), jnp.float32), 'text_features': jax.random.normal(ks[1], (B, LK, TXT_DIM), jnp.float32), 'Wq': jax.random.uniform(ks[2], (IMG_DIM, HID), jnp.float32, -s_img, s_img), 'bq': jax.random.uniform(ks[3], (HID,), jnp.float32, -s_img, s_img), 'Wk': jax.random.uniform(ks[4], (TXT_DIM, HID), jnp.float32, -s_txt, s_txt), 'bk': jax.random.uniform(ks[5], (HID,), jnp.float32, -s_txt, s_txt), 'Wv': jax.random.uniform(ks[6], (TXT_DIM, HID), jnp.float32, -s_txt, s_txt), 'bv': jax.random.uniform(ks[7], (HID,), jnp.float32, -s_txt, s_txt)}
    _L3_xattn_all = _L3_xattn_setup()
    _L3_xattn_in = {k: v for k, v in _L3_xattn_all.items() if k in ('Wq', 'bq', 'Wk', 'bk', 'Wv', 'bv')}
    del _L3_xattn_all

    def _L3_attn_setup():
        import jax, jax.numpy as jnp
        import numpy as np
        B, L, D, H = (2, 512, 256, 16)
        Dh = D // H
        key = jax.random.key(seed)
        kx, kq, kk, kv, ko = jax.random.split(key, 5)
        scale = 1.0 / np.sqrt(D)
        return {'x': jax.random.normal(kx, (B, L, D), dtype=jnp.float32), 'Wq': jax.random.normal(kq, (D, H, Dh), dtype=jnp.float32) * scale, 'Wk': jax.random.normal(kk, (D, H, Dh), dtype=jnp.float32) * scale, 'Wv': jax.random.normal(kv, (D, H, Dh), dtype=jnp.float32) * scale, 'Wout': jax.random.normal(ko, (H, Dh, D), dtype=jnp.float32) * (1.0 / np.sqrt(D))}
    _L3_attn_all = _L3_attn_setup()
    _L3_attn_in = {k: v for k, v in _L3_attn_all.items() if k in ('Wq', 'Wk', 'Wv', 'Wout')}
    del _L3_attn_all

    def _L3_ffn_setup():
        import jax, jax.numpy as jnp
        import numpy as np
        D_MODEL = 256
        N_HEADS = 16
        N_KV = 4
        NUM_REP = N_HEADS // N_KV
        HEAD_DIM = D_MODEL // N_HEADS
        N_EXPERTS = 8
        TOP_K = 2
        CAP_FACTOR = 1.25
        EPS_NORM = 1e-06

        def _rmsnorm(x, w):
            var = jnp.mean(x * x, axis=-1, keepdims=True)
            return w * (x * jax.lax.rsqrt(var + EPS_NORM))

        def _gqa(x, qw, qb, kw, kb, vw, vb, ow, ob):
            B, S, D = x.shape
            q = (x @ qw + qb).reshape(B, S, N_HEADS, HEAD_DIM).transpose(0, 2, 1, 3)
            k = (x @ kw + kb).reshape(B, S, N_KV, HEAD_DIM).transpose(0, 2, 1, 3)
            v = (x @ vw + vb).reshape(B, S, N_KV, HEAD_DIM).transpose(0, 2, 1, 3)
            k = jnp.repeat(k, NUM_REP, axis=1)
            v = jnp.repeat(v, NUM_REP, axis=1)
            scores = jnp.einsum('bhqd,bhkd->bhqk', q, k) / np.sqrt(HEAD_DIM).astype(np.float32)
            attn = jax.nn.softmax(scores, axis=-1)
            out = jnp.einsum('bhqk,bhkd->bhqd', attn, v)
            out = out.transpose(0, 2, 1, 3).reshape(B, S, D)
            return out @ ow + ob

        def _moe(x, gate_w, w1, w2):
            B, S, D = x.shape
            T = B * S
            x_flat = x.reshape(T, D)
            capacity = int(CAP_FACTOR * T * TOP_K / N_EXPERTS)
            logits = x_flat @ gate_w
            probs = jax.nn.sigmoid(logits)
            _, sel = jax.lax.top_k(probs, TOP_K)
            w_topk = jnp.take_along_axis(probs, sel, axis=1)
            w_topk = w_topk / (jnp.sum(w_topk, axis=-1, keepdims=True) + 1e-06)
            flat_sel = sel.reshape(-1)
            em = jax.nn.one_hot(flat_sel, N_EXPERTS, dtype=jnp.int32)
            ranks = jnp.take_along_axis(jnp.cumsum(em, axis=0), flat_sel[:, None], axis=1)[:, 0] - 1
            valid = ranks < capacity
            slot = flat_sel * capacity + ranks
            scatter_idx = jnp.where(valid, slot, N_EXPERTS * capacity)
            x_rep = jnp.repeat(x_flat, TOP_K, axis=0)
            padded = jnp.zeros((N_EXPERTS * capacity + 1, D), x.dtype).at[scatter_idx].set(x_rep)
            padded_x = padded[:N_EXPERTS * capacity].reshape(N_EXPERTS, capacity, D)
            h = jax.nn.gelu(jnp.einsum('ecd,edf->ecf', padded_x, w1), approximate=False)
            out_padded = jnp.einsum('ecf,efd->ecd', h, w2).reshape(N_EXPERTS * capacity, D)
            gather_idx = jnp.where(valid, slot, 0)
            out_rep = jnp.where(valid[:, None], out_padded[gather_idx], 0.0)
            out_w = out_rep * w_topk.reshape(-1)[:, None]
            return out_w.reshape(T, TOP_K, D).sum(axis=1).reshape(B, S, D)
        key = jax.random.key(seed)
        ks = jax.random.split(key, 12)
        s = 0.02
        return {'x': jax.random.normal(ks[0], (4, 256, D_MODEL), jnp.float32), 'qw': jax.random.normal(ks[1], (D_MODEL, D_MODEL), jnp.float32) * s, 'qb': jnp.zeros((D_MODEL,), jnp.float32), 'kw': jax.random.normal(ks[2], (D_MODEL, N_KV * HEAD_DIM), jnp.float32) * s, 'kb': jnp.zeros((N_KV * HEAD_DIM,), jnp.float32), 'vw': jax.random.normal(ks[3], (D_MODEL, N_KV * HEAD_DIM), jnp.float32) * s, 'vb': jnp.zeros((N_KV * HEAD_DIM,), jnp.float32), 'ow': jax.random.normal(ks[4], (D_MODEL, D_MODEL), jnp.float32) * s, 'ob': jnp.zeros((D_MODEL,), jnp.float32), 'gate_w': jax.random.normal(ks[5], (D_MODEL, N_EXPERTS), jnp.float32) * s, 'w1': jax.random.normal(ks[6], (N_EXPERTS, D_MODEL, 512), jnp.float32) * s, 'w2': jax.random.normal(ks[7], (N_EXPERTS, 512, D_MODEL), jnp.float32) * s, 'norm1_w': jnp.ones((D_MODEL,), jnp.float32), 'norm2_w': jnp.ones((D_MODEL,), jnp.float32)}
    _L3_ffn_all = _L3_ffn_setup()
    _L3_ffn_in = {k: v for k, v in _L3_ffn_all.items() if k in ('qw', 'qb', 'kw', 'kb', 'vw', 'vb', 'ow', 'ob', 'gate_w', 'w1', 'w2', 'norm1_w', 'norm2_w')}
    del _L3_ffn_all
    return {'x': x, 'ctx_768': ctx_768, 'L0_xattn_Wq': _L0_xattn_in['Wq'], 'L0_xattn_bq': _L0_xattn_in['bq'], 'L0_xattn_Wk': _L0_xattn_in['Wk'], 'L0_xattn_bk': _L0_xattn_in['bk'], 'L0_xattn_Wv': _L0_xattn_in['Wv'], 'L0_xattn_bv': _L0_xattn_in['bv'], 'L0_xattn_Wo': _L0_xattn_in['Wo'], 'L0_xattn_bo': _L0_xattn_in['bo'], 'L0_attn_Wq': _L0_attn_in['Wq'], 'L0_attn_Wk': _L0_attn_in['Wk'], 'L0_attn_Wv': _L0_attn_in['Wv'], 'L0_attn_Wo': _L0_attn_in['Wo'], 'L0_attn_Wqp': _L0_attn_in['Wqp'], 'L0_attn_Wkp': _L0_attn_in['Wkp'], 'L0_attn_lambda_raw': _L0_attn_in['lambda_raw'], 'L0_ffn_gate_w': _L0_ffn_in['gate_w'], 'L0_ffn_gate_b': _L0_ffn_in['gate_b'], 'L0_ffn_w1': _L0_ffn_in['w1'], 'L0_ffn_b1': _L0_ffn_in['b1'], 'L0_ffn_w2': _L0_ffn_in['w2'], 'L0_ffn_b2': _L0_ffn_in['b2'], 'L1_xattn_Wq': _L1_xattn_in['Wq'], 'L1_xattn_bq': _L1_xattn_in['bq'], 'L1_xattn_Wk': _L1_xattn_in['Wk'], 'L1_xattn_bk': _L1_xattn_in['bk'], 'L1_xattn_Wv': _L1_xattn_in['Wv'], 'L1_xattn_bv': _L1_xattn_in['bv'], 'L1_xattn_Wo': _L1_xattn_in['Wo'], 'L1_xattn_bo': _L1_xattn_in['bo'], 'L1_attn_w_qkv': _L1_attn_in['w_qkv'], 'L1_attn_w_out': _L1_attn_in['w_out'], 'L1_attn_b_out': _L1_attn_in['b_out'], 'L1_attn_gamma': _L1_attn_in['gamma'], 'L1_attn_beta': _L1_attn_in['beta'], 'L1_ffn_gate': _L1_ffn_in['gate'], 'L1_ffn_W1': _L1_ffn_in['W1'], 'L1_ffn_b1': _L1_ffn_in['b1'], 'L1_ffn_W2': _L1_ffn_in['W2'], 'L1_ffn_b2': _L1_ffn_in['b2'], 'L2_xattn_Wq': _L2_xattn_in['Wq'], 'L2_xattn_Wk': _L2_xattn_in['Wk'], 'L2_xattn_Wv': _L2_xattn_in['Wv'], 'L2_xattn_Wo': _L2_xattn_in['Wo'], 'L2_xattn_bo': _L2_xattn_in['bo'], 'L2_attn_attention_mask': _L2_attn_in['attention_mask'], 'L2_attn_ln_attn_g': _L2_attn_in['ln_attn_g'], 'L2_attn_ln_attn_b': _L2_attn_in['ln_attn_b'], 'L2_attn_Wq': _L2_attn_in['Wq'], 'L2_attn_bq': _L2_attn_in['bq'], 'L2_attn_Wk': _L2_attn_in['Wk'], 'L2_attn_bk': _L2_attn_in['bk'], 'L2_attn_Wv': _L2_attn_in['Wv'], 'L2_attn_bv': _L2_attn_in['bv'], 'L2_attn_ln_conv_g': _L2_attn_in['ln_conv_g'], 'L2_attn_ln_conv_b': _L2_attn_in['ln_conv_b'], 'L2_attn_conv_w': _L2_attn_in['conv_w'], 'L2_attn_conv_b': _L2_attn_in['conv_b'], 'L2_attn_ln_boom_g': _L2_attn_in['ln_boom_g'], 'L2_attn_ln_boom_b': _L2_attn_in['ln_boom_b'], 'L2_attn_Wb': _L2_attn_in['Wb'], 'L2_attn_bb': _L2_attn_in['bb'], 'L2_attn_Wu': _L2_attn_in['Wu'], 'L2_attn_bu': _L2_attn_in['bu'], 'L2_ffn_Wr': _L2_ffn_in['Wr'], 'L2_ffn_br': _L2_ffn_in['br'], 'L2_ffn_W1': _L2_ffn_in['W1'], 'L2_ffn_b1': _L2_ffn_in['b1'], 'L2_ffn_W2': _L2_ffn_in['W2'], 'L2_ffn_b2': _L2_ffn_in['b2'], 'L3_xattn_Wq': _L3_xattn_in['Wq'], 'L3_xattn_bq': _L3_xattn_in['bq'], 'L3_xattn_Wk': _L3_xattn_in['Wk'], 'L3_xattn_bk': _L3_xattn_in['bk'], 'L3_xattn_Wv': _L3_xattn_in['Wv'], 'L3_xattn_bv': _L3_xattn_in['bv'], 'L3_attn_Wq': _L3_attn_in['Wq'], 'L3_attn_Wk': _L3_attn_in['Wk'], 'L3_attn_Wv': _L3_attn_in['Wv'], 'L3_attn_Wout': _L3_attn_in['Wout'], 'L3_ffn_qw': _L3_ffn_in['qw'], 'L3_ffn_qb': _L3_ffn_in['qb'], 'L3_ffn_kw': _L3_ffn_in['kw'], 'L3_ffn_kb': _L3_ffn_in['kb'], 'L3_ffn_vw': _L3_ffn_in['vw'], 'L3_ffn_vb': _L3_ffn_in['vb'], 'L3_ffn_ow': _L3_ffn_in['ow'], 'L3_ffn_ob': _L3_ffn_in['ob'], 'L3_ffn_gate_w': _L3_ffn_in['gate_w'], 'L3_ffn_w1': _L3_ffn_in['w1'], 'L3_ffn_w2': _L3_ffn_in['w2'], 'L3_ffn_norm1_w': _L3_ffn_in['norm1_w'], 'L3_ffn_norm2_w': _L3_ffn_in['norm2_w']}

def reference(x, ctx_768, L0_xattn_Wq, L0_xattn_bq, L0_xattn_Wk, L0_xattn_bk, L0_xattn_Wv, L0_xattn_bv, L0_xattn_Wo, L0_xattn_bo, L0_attn_Wq, L0_attn_Wk, L0_attn_Wv, L0_attn_Wo, L0_attn_Wqp, L0_attn_Wkp, L0_attn_lambda_raw, L0_ffn_gate_w, L0_ffn_gate_b, L0_ffn_w1, L0_ffn_b1, L0_ffn_w2, L0_ffn_b2, L1_xattn_Wq, L1_xattn_bq, L1_xattn_Wk, L1_xattn_bk, L1_xattn_Wv, L1_xattn_bv, L1_xattn_Wo, L1_xattn_bo, L1_attn_w_qkv, L1_attn_w_out, L1_attn_b_out, L1_attn_gamma, L1_attn_beta, L1_ffn_gate, L1_ffn_W1, L1_ffn_b1, L1_ffn_W2, L1_ffn_b2, L2_xattn_Wq, L2_xattn_Wk, L2_xattn_Wv, L2_xattn_Wo, L2_xattn_bo, L2_attn_attention_mask, L2_attn_ln_attn_g, L2_attn_ln_attn_b, L2_attn_Wq, L2_attn_bq, L2_attn_Wk, L2_attn_bk, L2_attn_Wv, L2_attn_bv, L2_attn_ln_conv_g, L2_attn_ln_conv_b, L2_attn_conv_w, L2_attn_conv_b, L2_attn_ln_boom_g, L2_attn_ln_boom_b, L2_attn_Wb, L2_attn_bb, L2_attn_Wu, L2_attn_bu, L2_ffn_Wr, L2_ffn_br, L2_ffn_W1, L2_ffn_b1, L2_ffn_W2, L2_ffn_b2, L3_xattn_Wq, L3_xattn_bq, L3_xattn_Wk, L3_xattn_bk, L3_xattn_Wv, L3_xattn_bv, L3_attn_Wq, L3_attn_Wk, L3_attn_Wv, L3_attn_Wout, L3_ffn_qw, L3_ffn_qb, L3_ffn_kw, L3_ffn_kb, L3_ffn_vw, L3_ffn_vb, L3_ffn_ow, L3_ffn_ob, L3_ffn_gate_w, L3_ffn_w1, L3_ffn_w2, L3_ffn_norm1_w, L3_ffn_norm2_w):
    import jax
    import jax.numpy as jnp

    def _L0_xattn_ref(query, key, value, Wq, bq, Wk, bk, Wv, bv, Wo, bo):
        import jax, jax.numpy as jnp
        import numpy as np
        EMBED_DIM = 256
        Q_DIM = 256
        KV_DIM = 192
        NUM_HEADS = 16
        HEAD_DIM = EMBED_DIM // NUM_HEADS
        SCALE = NUM_HEADS ** (-0.5)

        def _linear_params(key, in_dim, out_dim):
            kw, kb = jax.random.split(key)
            bound = 1.0 / np.sqrt(in_dim)
            W = jax.random.uniform(kw, (in_dim, out_dim), minval=-bound, maxval=bound, dtype=jnp.float32)
            b = jax.random.uniform(kb, (out_dim,), minval=-bound, maxval=bound, dtype=jnp.float32)
            return (W, b)
        B, N1, _ = query.shape
        N2 = key.shape[1]
        Q = (query @ Wq + bq).reshape(B, N1, NUM_HEADS, HEAD_DIM).transpose(0, 2, 1, 3)
        K = (key @ Wk + bk).reshape(B, N2, NUM_HEADS, HEAD_DIM).transpose(0, 2, 1, 3)
        V = (value @ Wv + bv).reshape(B, N2, NUM_HEADS, HEAD_DIM).transpose(0, 2, 1, 3)
        att = jnp.einsum('bhqd,bhkd->bhqk', Q, K) * SCALE
        att = jax.nn.softmax(att, axis=-1)
        out = jnp.einsum('bhqk,bhkd->bhqd', att, V)
        out = out.transpose(0, 2, 1, 3).reshape(B, N1, EMBED_DIM)
        return out @ Wo + bo

    def _L0_attn_ref(x, Wq, Wk, Wv, Wo, Wqp, Wkp, lambda_raw):
        import math
        import jax, jax.numpy as jnp
        import numpy as np
        B, S, D, H = (2, 512, 256, 16)
        HD = D // H
        LAMBDA_MAX = 0.5
        AMP_EPS = 1e-06

        def _amp_norm(t):
            a = jax.nn.softplus(t)
            return a / jnp.sqrt(jnp.mean(a * a, axis=-1, keepdims=True) + AMP_EPS)
        b, s, d = x.shape
        split = lambda t: t.reshape(b, s, H, HD)
        q = split(x @ Wq)
        k = split(x @ Wk)
        v = split(x @ Wv)
        scale = 1.0 / math.sqrt(HD)
        scores_dot = jnp.einsum('bihd,bjhd->bhij', q, k) * scale
        q_amp = _amp_norm(q)
        k_amp = _amp_norm(k)
        q_phi = math.pi * jnp.tanh(split(x @ Wqp))
        k_phi = math.pi * jnp.tanh(split(x @ Wkp))
        q_cos = q_amp * jnp.cos(q_phi)
        q_sin = q_amp * jnp.sin(q_phi)
        k_cos = k_amp * jnp.cos(k_phi)
        k_sin = k_amp * jnp.sin(k_phi)
        scores_phase = (jnp.einsum('bihd,bjhd->bhij', q_cos, k_cos) + jnp.einsum('bihd,bjhd->bhij', q_sin, k_sin)) * scale
        lam = (LAMBDA_MAX * jnp.tanh(lambda_raw))[None, :, None, None]
        scores = scores_dot + lam * scores_phase
        causal = jnp.tril(jnp.ones((s, s), bool))
        scores = jnp.where(causal[None, None], scores, -jnp.inf)
        attn = jax.nn.softmax(scores, axis=-1)
        out = jnp.einsum('bhij,bjhd->bihd', attn, v).reshape(b, s, d)
        return out @ Wo

    def _L0_ffn_ref(x, gate_w, gate_b, w1, b1, w2, b2):
        import jax, jax.numpy as jnp
        import numpy as np
        B, T, D = (4, 256, 256)
        E = 8
        K = 2
        H = 4 * D
        b, t, d = x.shape
        xf = x.reshape(-1, d)
        logits = xf @ gate_w + gate_b
        top_w, top_idx = jax.lax.top_k(logits, K)
        top_w = jax.nn.softmax(top_w, axis=1).astype(x.dtype)
        n = xf.shape[0]
        comb = jnp.zeros((n, E), x.dtype).at[jnp.arange(n)[:, None], top_idx].add(top_w)
        h = jax.nn.gelu(jnp.einsum('nd,edh->enh', xf, w1) + b1[:, None, :], approximate=False)
        y = jnp.einsum('enh,ehd->end', h, w2) + b2[:, None, :]
        out = jnp.einsum('ne,end->nd', comb, y)
        return out.reshape(b, t, d)

    def _L1_xattn_ref(query, key_value, Wq, bq, Wk, bk, Wv, bv, Wo, bo):
        import jax, jax.numpy as jnp
        import numpy as np
        NUM_HEADS = 16
        CLAMP = 10000.0
        B, Nq, Cq = query.shape
        Nkv = key_value.shape[1]
        H = NUM_HEADS
        D = Cq // H
        scale = D ** (-0.5)
        q = (query @ Wq + bq).reshape(B, Nq, H, D).transpose(0, 2, 1, 3)
        k = (key_value @ Wk + bk).reshape(B, Nkv, H, D).transpose(0, 2, 1, 3)
        v = (key_value @ Wv + bv).reshape(B, Nkv, H, D).transpose(0, 2, 1, 3)
        attn = jnp.einsum('bhqd,bhkd->bhqk', q, k) * scale
        attn = jnp.clip(attn, -CLAMP, CLAMP)
        attn = jax.nn.softmax(attn, axis=-1)
        attn = jnp.where(jnp.any(jnp.isnan(attn)), jnp.asarray(1.0 / Nkv, attn.dtype), attn)
        x = jnp.einsum('bhqk,bhkd->bqhd', attn, v).reshape(B, Nq, Cq)
        return x @ Wo + bo

    def _L1_attn_ref(x, w_qkv, w_out, b_out, gamma, beta):
        import jax, jax.numpy as jnp
        import numpy as np
        B, S, D, H = (4, 512, 256, 16)
        HD = D // H
        LN_EPS = 1e-05
        KERN_EPS = 1e-06

        def kernel_func(q, k):
            scores = jnp.einsum('bhqd,bhkd->bhqk', q, k) / jnp.sqrt(jnp.asarray(HD, q.dtype))
            w = jax.nn.relu(scores)
            return w / (jnp.sum(w, axis=-1, keepdims=True) + KERN_EPS)
        Bx, Sx, _ = x.shape
        qkv = (x @ w_qkv).reshape(Bx, Sx, H, 3 * HD)
        q, k, v = jnp.split(qkv, 3, axis=-1)
        q = q.transpose(0, 2, 1, 3)
        k = k.transpose(0, 2, 1, 3)
        v = v.transpose(0, 2, 1, 3)
        attn = kernel_func(q, k)
        out = jnp.einsum('bhqk,bhkd->bhqd', attn, v)
        out = out.transpose(0, 2, 1, 3).reshape(Bx, Sx, D)
        out = out @ w_out + b_out
        y = x + out
        mu = jnp.mean(y, axis=-1, keepdims=True)
        var = jnp.var(y, axis=-1, keepdims=True)
        return (y - mu) * jax.lax.rsqrt(var + LN_EPS) * gamma + beta

    def _L1_ffn_ref(x, gate, W1, b1, W2, b2):
        import jax, jax.numpy as jnp
        import numpy as np
        N_EXPERTS = 16
        TOP_K = int(N_EXPERTS * 0.2)
        EPS = 1e-12
        raw_gate = jax.nn.softmax(jnp.einsum('btd,de->bte', x, gate), axis=-1)
        _, topk_idx = jax.lax.top_k(raw_gate, TOP_K)
        mask = jax.nn.one_hot(topk_idx, raw_gate.shape[-1], dtype=raw_gate.dtype).sum(axis=2)
        gate_topk = mask * raw_gate
        gate_topk = gate_topk / jnp.maximum(jnp.sum(jnp.abs(gate_topk), axis=-1, keepdims=True), EPS)
        hidden = jax.nn.relu(jnp.einsum('btd,edh->bteh', x, W1) + b1)
        expert_out = jnp.einsum('bteh,ehd->bted', hidden, W2) + b2
        return jnp.einsum('bte,bted->btd', gate_topk, expert_out)

    def _L2_xattn_ref(x, context, Wq, Wk, Wv, Wo, bo):
        import jax, jax.numpy as jnp
        import numpy as np
        QUERY_DIM = 256
        CONTEXT_DIM = 192
        HEADS = 8
        DIM_HEAD = 64
        INNER = HEADS * DIM_HEAD
        B, S, _ = x.shape
        L = context.shape[1]
        scale = DIM_HEAD ** (-0.5)
        q = (x @ Wq).reshape(B, S, HEADS, DIM_HEAD).transpose(0, 2, 1, 3)
        k = (context @ Wk).reshape(B, L, HEADS, DIM_HEAD).transpose(0, 2, 1, 3)
        v = (context @ Wv).reshape(B, L, HEADS, DIM_HEAD).transpose(0, 2, 1, 3)
        attn = jnp.einsum('bhsd,bhld->bhsl', q, k) * scale
        attn = jax.nn.softmax(attn, axis=-1)
        out = jnp.einsum('bhsl,bhld->bhsd', attn, v)
        out = out.transpose(0, 2, 1, 3).reshape(B, S, INNER)
        return out @ Wo + bo

    def _L2_attn_ref(hidden_states, attention_mask, ln_attn_g, ln_attn_b, Wq, bq, Wk, bk, Wv, bv, ln_conv_g, ln_conv_b, conv_w, conv_b, ln_boom_g, ln_boom_b, Wb, bb, Wu, bu):
        import jax, jax.numpy as jnp
        import numpy as np
        EPS = 1e-05

        def _ln(x, g, b):
            m = jnp.mean(x, axis=-1, keepdims=True)
            v = jnp.mean((x - m) ** 2, axis=-1, keepdims=True)
            return (x - m) * jax.lax.rsqrt(v + EPS) * g + b

        def _forward(x, ln_attn_g, ln_attn_b, Wq, bq, Wk, bk, Wv, bv, ln_conv_g, ln_conv_b, conv_w, conv_b, ln_boom_g, ln_boom_b, Wb, bb, Wu, bu):
            B, S, D = x.shape
            K = conv_w.shape[-1]
            G = D // conv_w.shape[1]
            h = _ln(x, ln_conv_g, ln_conv_b)
            hc = jnp.transpose(h, (0, 2, 1))
            hc = jnp.pad(hc, ((0, 0), (0, 0), (K - 1, 0)))
            conv = jax.lax.conv_general_dilated(hc, conv_w, window_strides=(1,), padding='VALID', dimension_numbers=('NCH', 'OIH', 'NCH'), feature_group_count=G)
            conv = conv + conv_b[None, :, None]
            x = x + jnp.transpose(conv, (0, 2, 1))
            h = _ln(x, ln_attn_g, ln_attn_b)
            q = jnp.einsum('bsd,ed->bse', h, Wq) + bq
            k = jnp.einsum('bsd,ed->bse', h, Wk) + bk
            v = jnp.einsum('bsd,ed->bse', h, Wv) + bv
            scale = jnp.arange(1, S + 1, dtype=x.dtype)[None, :, None]
            pooled_q = jnp.cumsum(q, axis=1) / scale
            pooled_k = jnp.cumsum(pooled_q * k, axis=1) / scale
            x = x + pooled_k * v
            h = _ln(x, ln_boom_g, ln_boom_b)
            h = jax.nn.gelu(jnp.einsum('bsd,ed->bse', h, Wb) + bb, approximate=False)
            h = jnp.einsum('bse,de->bsd', h, Wu) + bu
            return x + h
        return _forward(hidden_states, ln_attn_g, ln_attn_b, Wq, bq, Wk, bk, Wv, bv, ln_conv_g, ln_conv_b, conv_w, conv_b, ln_boom_g, ln_boom_b, Wb, bb, Wu, bu)

    def _L2_ffn_ref(x, Wr, br, W1, b1, W2, b2):
        import jax, jax.numpy as jnp
        import numpy as np
        TOP_K = 2
        k = TOP_K
        scores0 = x[:, 0, :] @ Wr + br
        _, idx = jax.lax.top_k(scores0, k)
        W1g, b1g = (W1[idx], b1[idx])
        W2g, b2g = (W2[idx], b2[idx])
        h = jnp.einsum('bsd,bkde->bkse', x, W1g) + b1g[:, :, None, :]
        h = jax.nn.gelu(h, approximate=False)
        o = jnp.einsum('bkse,bkef->bksf', h, W2g) + b2g[:, :, None, :]
        return jnp.sum(o, axis=1) / k

    def _L3_xattn_ref(image_features, text_features, Wq, bq, Wk, bk, Wv, bv):
        import jax, jax.numpy as jnp
        import numpy as np
        IMG_DIM, TXT_DIM, HID = (256, 192, 256)
        B, LQ, LK = (8, 512, 512)
        query = jnp.einsum('bqi,ih->bqh', image_features, Wq) + bq
        key = jnp.einsum('bkt,th->bkh', text_features, Wk) + bk
        value = jnp.einsum('bkt,th->bkh', text_features, Wv) + bv
        scale = 1.0 / jnp.sqrt(jnp.asarray(HID, query.dtype))
        scores = jnp.einsum('bqh,bkh->bqk', query, key) * scale
        weights = jax.nn.softmax(scores, axis=-1)
        attended = jnp.einsum('bqk,bkh->bqh', weights, value)
        return attended

    def _L3_attn_ref(x, Wq, Wk, Wv, Wout):
        import jax, jax.numpy as jnp
        import numpy as np
        B, L, D, H = (2, 512, 256, 16)
        Dh = D // H
        q = jnp.einsum('bld,dhe->blhe', x, Wq)
        k = jnp.einsum('bld,dhe->blhe', x, Wk)
        v = jnp.einsum('bld,dhe->blhe', x, Wv)
        a = jnp.einsum('bqhd,bkhd->bhqk', q, k) / Dh ** 0.5
        Lq = x.shape[1]
        mask = jnp.tril(jnp.ones((1, 1, Lq, Lq), dtype=jnp.bool_))
        NEG_INF = jnp.finfo(jnp.float32).min
        a = jnp.where(mask, a, NEG_INF)
        a = jax.nn.softmax(a, axis=-1)
        o = jnp.einsum('bhqk,bkhd->bqhd', a, v)
        return jnp.einsum('blhe,hed->bld', o, Wout)

    def _L3_ffn_ref(x, qw, qb, kw, kb, vw, vb, ow, ob, gate_w, w1, w2, norm1_w, norm2_w):
        import jax, jax.numpy as jnp
        import numpy as np
        D_MODEL = 256
        N_HEADS = 16
        N_KV = 4
        NUM_REP = N_HEADS // N_KV
        HEAD_DIM = D_MODEL // N_HEADS
        N_EXPERTS = 8
        TOP_K = 2
        CAP_FACTOR = 1.25
        EPS_NORM = 1e-06

        def _rmsnorm(x, w):
            var = jnp.mean(x * x, axis=-1, keepdims=True)
            return w * (x * jax.lax.rsqrt(var + EPS_NORM))

        def _gqa(x, qw, qb, kw, kb, vw, vb, ow, ob):
            B, S, D = x.shape
            q = (x @ qw + qb).reshape(B, S, N_HEADS, HEAD_DIM).transpose(0, 2, 1, 3)
            k = (x @ kw + kb).reshape(B, S, N_KV, HEAD_DIM).transpose(0, 2, 1, 3)
            v = (x @ vw + vb).reshape(B, S, N_KV, HEAD_DIM).transpose(0, 2, 1, 3)
            k = jnp.repeat(k, NUM_REP, axis=1)
            v = jnp.repeat(v, NUM_REP, axis=1)
            scores = jnp.einsum('bhqd,bhkd->bhqk', q, k) / np.sqrt(HEAD_DIM).astype(np.float32)
            attn = jax.nn.softmax(scores, axis=-1)
            out = jnp.einsum('bhqk,bhkd->bhqd', attn, v)
            out = out.transpose(0, 2, 1, 3).reshape(B, S, D)
            return out @ ow + ob

        def _moe(x, gate_w, w1, w2):
            B, S, D = x.shape
            T = B * S
            x_flat = x.reshape(T, D)
            capacity = int(CAP_FACTOR * T * TOP_K / N_EXPERTS)
            logits = x_flat @ gate_w
            probs = jax.nn.sigmoid(logits)
            _, sel = jax.lax.top_k(probs, TOP_K)
            w_topk = jnp.take_along_axis(probs, sel, axis=1)
            w_topk = w_topk / (jnp.sum(w_topk, axis=-1, keepdims=True) + 1e-06)
            flat_sel = sel.reshape(-1)
            em = jax.nn.one_hot(flat_sel, N_EXPERTS, dtype=jnp.int32)
            ranks = jnp.take_along_axis(jnp.cumsum(em, axis=0), flat_sel[:, None], axis=1)[:, 0] - 1
            valid = ranks < capacity
            slot = flat_sel * capacity + ranks
            scatter_idx = jnp.where(valid, slot, N_EXPERTS * capacity)
            x_rep = jnp.repeat(x_flat, TOP_K, axis=0)
            padded = jnp.zeros((N_EXPERTS * capacity + 1, D), x.dtype).at[scatter_idx].set(x_rep)
            padded_x = padded[:N_EXPERTS * capacity].reshape(N_EXPERTS, capacity, D)
            h = jax.nn.gelu(jnp.einsum('ecd,edf->ecf', padded_x, w1), approximate=False)
            out_padded = jnp.einsum('ecf,efd->ecd', h, w2).reshape(N_EXPERTS * capacity, D)
            gather_idx = jnp.where(valid, slot, 0)
            out_rep = jnp.where(valid[:, None], out_padded[gather_idx], 0.0)
            out_w = out_rep * w_topk.reshape(-1)[:, None]
            return out_w.reshape(T, TOP_K, D).sum(axis=1).reshape(B, S, D)
        src = x + _gqa(x, qw, qb, kw, kb, vw, vb, ow, ob)
        src = _rmsnorm(src, norm1_w)
        src = src + _moe(src, gate_w, w1, w2)
        return _rmsnorm(src, norm2_w)
    x = x + _L0_xattn_ref(_layernorm(x, axis=-1), ctx_768, ctx_768, L0_xattn_Wq, L0_xattn_bq, L0_xattn_Wk, L0_xattn_bk, L0_xattn_Wv, L0_xattn_bv, L0_xattn_Wo, L0_xattn_bo)
    x = x + _L0_attn_ref(_layernorm(x, axis=-1), L0_attn_Wq, L0_attn_Wk, L0_attn_Wv, L0_attn_Wo, L0_attn_Wqp, L0_attn_Wkp, L0_attn_lambda_raw)
    x = x + _L0_ffn_ref(_layernorm(x, axis=-1), L0_ffn_gate_w, L0_ffn_gate_b, L0_ffn_w1, L0_ffn_b1, L0_ffn_w2, L0_ffn_b2)
    x = x + _L1_xattn_ref(_layernorm(x, axis=-1), ctx_768, L1_xattn_Wq, L1_xattn_bq, L1_xattn_Wk, L1_xattn_bk, L1_xattn_Wv, L1_xattn_bv, L1_xattn_Wo, L1_xattn_bo)
    x = x + _L1_attn_ref(_layernorm(x, axis=-1), L1_attn_w_qkv, L1_attn_w_out, L1_attn_b_out, L1_attn_gamma, L1_attn_beta)
    x = x + _L1_ffn_ref(_layernorm(x, axis=-1), L1_ffn_gate, L1_ffn_W1, L1_ffn_b1, L1_ffn_W2, L1_ffn_b2)
    x = x + _L2_xattn_ref(_layernorm(x, axis=-1), ctx_768, L2_xattn_Wq, L2_xattn_Wk, L2_xattn_Wv, L2_xattn_Wo, L2_xattn_bo)
    x = x + _L2_attn_ref(_layernorm(x, axis=-1), L2_attn_attention_mask, L2_attn_ln_attn_g, L2_attn_ln_attn_b, L2_attn_Wq, L2_attn_bq, L2_attn_Wk, L2_attn_bk, L2_attn_Wv, L2_attn_bv, L2_attn_ln_conv_g, L2_attn_ln_conv_b, L2_attn_conv_w, L2_attn_conv_b, L2_attn_ln_boom_g, L2_attn_ln_boom_b, L2_attn_Wb, L2_attn_bb, L2_attn_Wu, L2_attn_bu)
    x = x + _L2_ffn_ref(_layernorm(x, axis=-1), L2_ffn_Wr, L2_ffn_br, L2_ffn_W1, L2_ffn_b1, L2_ffn_W2, L2_ffn_b2)
    x = x + _L3_xattn_ref(_layernorm(x, axis=-1), ctx_768, L3_xattn_Wq, L3_xattn_bq, L3_xattn_Wk, L3_xattn_bk, L3_xattn_Wv, L3_xattn_bv)
    x = x + _L3_attn_ref(_layernorm(x, axis=-1), L3_attn_Wq, L3_attn_Wk, L3_attn_Wv, L3_attn_Wout)
    x = x + _L3_ffn_ref(_layernorm(x, axis=-1), L3_ffn_qw, L3_ffn_qb, L3_ffn_kw, L3_ffn_kb, L3_ffn_vw, L3_ffn_vb, L3_ffn_ow, L3_ffn_ob, L3_ffn_gate_w, L3_ffn_w1, L3_ffn_w2, L3_ffn_norm1_w, L3_ffn_norm2_w)
    return x

_drawn_inputs = setup_inputs


def setup_inputs(seed=0):
    import zlib

    import numpy as np

    out = dict(_drawn_inputs(seed))
    spreads = {'L0_attn_lambda_raw': (0.5493061542510986, 0.6),
     'L1_xattn_bq': (0.0, 0.1),
     'L1_xattn_bk': (0.0, 2.0),
     'L1_xattn_bv': (0.0, 0.1),
     'L1_xattn_bo': (0.0, 0.1),
     'L1_attn_b_out': (0.0, 0.1),
     'L1_attn_gamma': (1.0, 0.2),
     'L1_attn_beta': (0.0, 0.1),
     'L2_attn_ln_attn_g': (1.0, 0.6),
     'L2_attn_ln_attn_b': (0.0, 0.8),
     'L2_attn_bq': (0.0, 0.8),
     'L2_attn_bk': (0.0, 0.8),
     'L2_attn_bv': (0.0, 0.8),
     'L2_attn_ln_conv_g': (1.0, 0.2),
     'L2_attn_ln_conv_b': (0.0, 0.307),
     'L2_attn_conv_b': (0.0, 0.1),
     'L2_attn_ln_boom_g': (1.0, 0.6),
     'L2_attn_ln_boom_b': (0.0, 2.0),
     'L2_attn_bb': (0.0, 2.0),
     'L2_attn_bu': (0.0, 0.8),
     'L2_ffn_br': (0.0, 0.8),
     'L2_ffn_b1': (0.0, 2.0),
     'L2_ffn_b2': (0.0, 2.0),
     'L3_ffn_qb': (0.0, 2.0),
     'L3_ffn_kb': (0.0, 2.0),
     'L3_ffn_vb': (0.0, 0.8),
     'L3_ffn_ob': (0.0, 1.023),
     'L3_ffn_norm1_w': (1.0, 0.6),
     'L3_ffn_norm2_w': (1.0, 0.6)}
    factors = {'L0_xattn_bq': 14.427,
     'L0_xattn_bk': 64.0,
     'L0_attn_Wq': 8.0,
     'L0_attn_Wk': 8.0,
     'L0_attn_Wqp': 28.561,
     'L0_attn_Wkp': 32.049,
     'L0_ffn_b1': 4.949,
     'L1_ffn_b1': 3.178,
     'L2_xattn_bo': 8.0,
     'L2_attn_Wq': 8.0,
     'L2_attn_Wk': 3.245,
     'L2_attn_Wv': 8.0,
     'L3_xattn_Wq': 5.254,
     'L3_xattn_bq': 64.0,
     'L3_xattn_Wk': 5.252,
     'L3_xattn_bk': 64.0,
     'L3_xattn_bv': 25.612,
     'L3_ffn_qw': 8.0,
     'L3_ffn_kw': 8.0,
     'L3_ffn_vw': 3.729,
     'L3_ffn_ow': 3.43,
     'L3_ffn_gate_w': 4.915,
     'L3_ffn_w1': 4.531,
     'L3_ffn_w2': 4.42,
     'L1_ffn_b2': 4.95,
     'L2_attn_Wb': 5.707,
     'L2_attn_Wu': 3.181,
     'L2_ffn_W1': 2.683,
     'L3_attn_Wq': 5.614,
     'L3_attn_Wk': 5.456}
    for name, (base, spread) in spreads.items():
        noise = np.random.default_rng([zlib.crc32(name.encode()), seed]).standard_normal(out[name].shape)
        drawn = base * np.exp(spread * noise) if base else spread * noise
        out[name] = jnp.asarray(drawn.astype(out[name].dtype))
    for name, factor in factors.items():
        out[name] = (out[name] * factor).astype(out[name].dtype)
    return out
```

```python
from collections import namedtuple
from contextlib import ExitStack, contextmanager

import numpy as np

import concourse.bass as bass
from concourse import mybir

F32 = mybir.dt.float32
ALU = mybir.AluOpType
ACT = mybir.ActivationFunctionType
AX = mybir.AxisListType
ds = bass.ds

P = 128
B, S, D = 32, 32, 256
T = B * S
NT = T // P
BT = P // S
DC = D // P
LK, DK = 257, 192
BANK = 512
LN_EPS = 1e-5
NEG = -1.0e30



def constants():
    p = np.arange(P)
    f = np.float32
    out = {}
    out["ident"] = np.eye(P, dtype=f)
    out["head8"] = (p[:, None] // 16 == np.arange(8)[None, :]).astype(f)
    out["half4"] = (2 * np.arange(2)[None, :, None] + p[:, None, None] // 64 == np.arange(4)).astype(f).reshape(P, 8)
    out["seq4"] = (p[:, None] // S == np.arange(BT)[None, :]).astype(f)
    out["causal"] = np.where(np.arange(S)[None, :] <= (p % S)[:, None], 0.0, NEG).astype(f)
    out["headmean"] = (p[:, None] // 16 == p[None, :] // 16).astype(f) / f(16)
    out["first"] = (p[:, None] == (p[None, :] // S) * S).astype(f)
    out["before"] = (p[:, None] < p[None, :]).astype(f)
    out["ones"] = np.ones((P, P), f)
    out["down8"] = np.tile(8 - np.arange(8), (P, 1)).astype(f)
    out["down16"] = np.tile(16 - np.arange(16), (P, 1)).astype(f)
    keep = (np.arange(T) % S != 0).astype(f)
    out["keep"] = np.tile(keep, (P, 1))
    out["rcount"] = np.tile((1.0 / (np.arange(T) % S + 1)).astype(f), (P, 1))
    return out


def chunks(w):
    k = -(-w.shape[0] // P) * P
    w = np.concatenate([w, np.zeros((k - w.shape[0],) + w.shape[1:], w.dtype)]) if k != w.shape[0] else w
    return w.reshape(k // P, P, -1).transpose(1, 0, 2)


def column(v):
    return v.reshape(-1, P).T


def row(v):
    return np.broadcast_to(v.reshape(1, -1), (P, v.size))


def wo_rows(w, ng, hd):
    w = w.reshape(ng, 4, hd, -1).transpose(0, 2, 1, 3).reshape(ng * hd, 4, -1)
    return np.concatenate([w, np.zeros((P - ng * hd,) + w.shape[1:], w.dtype)]) if ng * hd < P else w


def conv_blocks(w):
    g = w.shape[1]
    out = np.zeros((P, DC, w.shape[2], P), w.dtype)
    for c in range(DC):
        for j in range(P // g):
            o = c * P + j * g
            out[j * g:(j + 1) * g, c, :, j * g:(j + 1) * g] = w[o:o + g].transpose(1, 2, 0)
    return out


def packs(i):
    out = {}
    for n in ("L0", "L1", "L2", "L3"):
        g = lambda k: i[f"{n}_xattn_{k}"]
        f = [("wq", chunks(g("Wq"))), ("wk", chunks(g("Wk"))), ("wv", chunks(g("Wv")))]
        if n in ("L0", "L1"):
            f += [("wo", wo_rows(g("Wo"), 4, 16)), ("bq", column(g("bq"))), ("bk", column(g("bk"))),
                  ("bv", row(g("bv"))), ("bo", row(g("bo")))]
        elif n == "L2":
            f += [("wo", wo_rows(g("Wo"), 2, 64)), ("bo", row(g("bo")))]
        else:
            f += [("bq", column(g("bq"))), ("bk", column(g("bk"))), ("bv", row(g("bv")))]
        out[f"{n}_xattn"] = f
    g = lambda k: i[f"L0_attn_{k}"]
    lam = np.repeat(g("lambda_raw"), 16)
    out["L0_attn"] = [("wq", chunks(g("Wq"))), ("wk", chunks(g("Wk"))), ("wv", chunks(g("Wv"))),
                      ("wqp", chunks(g("Wqp"))), ("wkp", chunks(g("Wkp"))), ("wo", wo_rows(g("Wo"), 4, 16)),
                      ("lam", column(lam))]
    w = i["L1_attn_w_qkv"].reshape(D, 16, 3, 16)
    q, k, v = (w[:, :, j].reshape(D, D) for j in range(3))
    out["L1_attn"] = [("wq", chunks(q)), ("wk", chunks(k)), ("wv", chunks(v)), ("wo", wo_rows(i["L1_attn_w_out"], 4, 16)),
                      ("bo", row(i["L1_attn_b_out"])), ("gamma", row(i["L1_attn_gamma"])), ("beta", row(i["L1_attn_beta"]))]
    g = lambda k: i[f"L2_attn_{k}"]
    out["L2_attn"] = [("wq", chunks(g("Wq").T)), ("wk", chunks(g("Wk").T)), ("wv", chunks(g("Wv").T)),
                      ("conv", conv_blocks(g("conv_w")))] + \
                     [(a, column(g(b))) for a, b in (("bq", "bq"), ("bk", "bk"), ("bv", "bv"), ("cb", "conv_b"),
                                                     ("g1", "ln_conv_g"), ("b1", "ln_conv_b"), ("g2", "ln_attn_g"),
                                                     ("b2", "ln_attn_b"), ("g3", "ln_boom_g"), ("b3", "ln_boom_b"))]
    out["L2_boom"] = [("b1", column(g("bb"))), ("bo", row(g("bu")))]
    g = lambda k: i[f"L3_attn_{k}"]
    out["L3_attn"] = [("wq", chunks(g("Wq").reshape(D, D))), ("wk", chunks(g("Wk").reshape(D, D))),
                      ("wv", chunks(g("Wv").reshape(D, D))), ("wo", wo_rows(g("Wout").reshape(D, D), 4, 16))]
    g = lambda k: i[f"L3_ffn_{k}"]

    def heads(w):
        return np.repeat(w.reshape(-1, 4, 16), 4, axis=1).reshape(-1, D)

    out["L3_gqa"] = [("wq", chunks(g("qw"))), ("wk", chunks(heads(g("kw")))), ("wv", chunks(heads(g("vw")))),
                     ("wo", wo_rows(g("ow"), 4, 16)), ("bq", column(g("qb"))), ("bk", column(heads(g("kb")).reshape(-1))),
                     ("bv", row(heads(g("vb")).reshape(-1))), ("bo", row(g("ob"))),
                     ("gamma", row(g("norm1_w"))), ("gamma2", row(g("norm2_w")))]

    def moe(gate, bias, b1, b2):
        f = [("gate", chunks(gate))]
        if bias is not None:
            f.append(("gb", row(bias)))
        if b1 is not None:
            f.append(("b1", b1.reshape(b1.shape[0], -1, P).transpose(2, 0, 1)))
            f.append(("b2", np.concatenate([b2, np.zeros((P - b2.shape[0], D), b2.dtype)])))
        return f

    out["L0_ffn"] = moe(i["L0_ffn_gate_w"], i["L0_ffn_gate_b"], i["L0_ffn_b1"], i["L0_ffn_b2"])
    out["L1_ffn"] = moe(i["L1_ffn_gate"], None, i["L1_ffn_b1"], i["L1_ffn_b2"])
    out["L2_ffn"] = moe(i["L2_ffn_Wr"], i["L2_ffn_br"], i["L2_ffn_b1"], i["L2_ffn_b2"])
    out["L3_ffn"] = moe(i["L3_ffn_gate_w"], None, None, None)
    return out


def experts(w1, w2):
    return (np.stack([chunks(a) for a in w1]), np.stack([chunks(a) for a in w2]))


ORDER = ["L0_xattn", "L0_attn", "L0_ffn", "L1_xattn", "L1_attn", "L1_ffn",
         "L2_xattn", "L2_attn", "L2_boom", "L2_ffn", "L3_xattn", "L3_attn", "L3_gqa", "L3_ffn"]



class Core:
    pass


@contextmanager
def stage(k, names):
    k.stages += 1
    sems = {n: k.nc.alloc_semaphore(name=f"{n}_{k.stages}") for n in names.split()}
    with k.nc.Block() as block:
        yield block, namedtuple("Semaphores", sems)(**sems)
    k.nc.clear_and_free_semaphores(list(sems.values()))
    k.nc.all_engine_barrier(sem_only=True)


@contextmanager
def buffers(k, **shapes):
    with ExitStack() as ctx:
        k.buffers += 1
        made = {n: ctx.enter_context(k.nc.sbuf_tensor(f"{n}_{k.buffers}", list(s), F32)) for n, s in shapes.items()}
        yield namedtuple("Buffers", made)(**made)


def fetch_weights(k, sp):
    i = k.fetched
    if i < min(k.fetch_to, len(k.order)):
        k.fetched += 1
        name = k.order[i]
        width = k.packed[name].shape[1]
        sp.dma_start(k.store[:, i % 2, 0:width], k.packed[name]).then_inc(k.weights_loaded[i % 2], 16)


FIELDS = "wq wk wv wo bq bk bv bo wqp wkp lam gamma gamma2 beta conv cb g1 b1 g2 b2 g3 b3 gate gb"
Weights = namedtuple("Weights", "at " + FIELDS, defaults=[None] * len(FIELDS.split()))


def weights(k, name):
    i = k.order.index(name)
    views, at = {}, 0
    for field, shape in k.fields[name]:
        n = int(np.prod(shape[1:]))
        v = k.store[:, i % 2, at:at + n]
        if len(shape) == 3:
            v = v.rearrange("p (a b) -> p a b", a=shape[1])
        if len(shape) == 4:
            v = v.rearrange("p (a b c) -> p a b c", a=shape[1], b=shape[2])
        views[field] = v
        at += n
    return Weights(at=(k.weights_loaded[i % 2], 16 * (i // 2 + 1)), **views)


def spread(ap, n, axis):
    shape = list(ap.shape)
    return ap.unsqueeze(axis).broadcast_to(shape[:axis] + [n] + shape[axis:])


def load_inputs(k):
    nc = k.nc
    with stage(k, "loaded") as (block, s):
        @block.sync
        def _(sp):
            sp.dma_start(k.x[:], k.in_x).then_inc(s.loaded, 16)
            sp.dma_start(k.consts[:], k.in_const).then_inc(s.loaded, 16)
            fetch_weights(k, sp)
            fetch_weights(k, sp)
            sp.wait_ge(s.loaded, 32)


def store_output(k):
    with k.nc.Block() as block:
        @block.sync
        def _(sp):
            sp.dma_start(k.out, k.x[:]).then_inc(k.stored, 16)
            sp.wait_ge(k.stored, 16)


def normalize(k, src, dst, rms=False, gain=None, shift=None, eps=LN_EPS, w_at=None, add=None):
    nc = k.nc
    with stage(k, "stats_done aggr_done std_done rstd_done norm_done gained shifted") as (block, s), \
            buffers(k, stats=[P, NT, 6], mv=[P, NT, 2], std=[P, NT], rstd=[P, NT], sq=[P, 2, D], eps=[P, 1]) as b:
        @block.vector
        def _(dve):
            if w_at:
                dve.wait_ge(*w_at)
            nc.vector.memset(b.eps[:], eps).then_inc(s.stats_done, 1)
            for t in range(NT):
                if rms:
                    if t >= 2:
                        dve.wait_ge(s.stats_done, t)
                    nc.vector.tensor_tensor_reduce(b.sq[:, t % 2, :], src[:, t, :], src[:, t, :], 1.0 / D, 0.0,
                                                   ALU.mult, ALU.add, b.mv[:, t, 1:2]).then_inc(s.stats_done, 1)
                else:
                    nc.vector.bn_stats(b.stats[:, t, :], src[:, t, :]).then_inc(s.stats_done, 1)
            for t in range(NT):
                if not rms:
                    dve.wait_ge(s.stats_done, t + 2)
                    nc.vector.bn_aggr(b.mv[:, t, :], b.stats[:, t, :]).then_inc(s.aggr_done, 1)
            dve.wait_ge(s.std_done, 1)
            nc.vector.reciprocal(b.rstd[:], b.std[:]).then_inc(s.rstd_done, 1)
            dve.wait_ge(s.rstd_done, 1)
            for t in range(NT):
                if rms:
                    nc.vector.tensor_scalar(dst[:, t, :], src[:, t, :], b.rstd[:, t:t + 1], None,
                                            ALU.mult).then_inc(s.norm_done, 1)
                else:
                    nc.vector.tensor_scalar(dst[:, t, :], src[:, t, :], b.mv[:, t, 0:1], b.rstd[:, t:t + 1],
                                            ALU.subtract, ALU.mult).then_inc(s.norm_done, 1)
            if gain is not None:
                dve.wait_ge(s.norm_done, NT)
                nc.vector.tensor_tensor(dst[:], dst[:], spread(gain, NT, 1), ALU.mult).then_inc(s.gained, 1)
            if shift is not None:
                dve.wait_ge(s.gained, 1)
                nc.vector.tensor_tensor(dst[:], dst[:], spread(shift, NT, 1), ALU.add).then_inc(s.shifted, 1)
            if add is not None:
                if shift is not None:
                    dve.wait_ge(s.shifted, 1)
                elif gain is not None:
                    dve.wait_ge(s.gained, 1)
                nc.vector.tensor_tensor(add[:], add[:], dst[:], ALU.add)

        @block.sync
        def _(sp):
            fetch_weights(k, sp)

        @block.scalar
        def _(act):
            act.wait_ge(s.stats_done, NT + 1)
            if not rms:
                act.wait_ge(s.aggr_done, NT)
            nc.scalar.activation(b.std[:], b.mv[:, :, 1], ACT.Sqrt, bias=b.eps[:, 0:1]).then_inc(s.std_done, 1)


def transpose_tokens(k, src, dst, gain=None, shift=None, padded=None, w_at=None):
    nc = k.nc
    with stage(k, "turned copied") as (block, s):
        @block.tensor
        def _(pe):
            for q in range(2 * DC):
                c, half = q % DC, q // DC
                for t in range(4):
                    last = nc.tensor.transpose(k.ps[:, q, t * P:(t + 1) * P],
                                               src[:, half * 4 + t, c * P:(c + 1) * P], k.ident)
                last.then_inc(s.turned, 1)

        def copy(eng, which, q):
            c, half = q % DC, q // DC
            eng.wait_ge(s.turned, q + 1)
            if padded is not None:
                out = padded[:, c, half * 16:(half + 1) * 16, :]
                inp = k.ps[:, q, :].rearrange("p (b s) -> p b s", s=S)
            else:
                out, inp = dst[:, c, half * 512:(half + 1) * 512], k.ps[:, q, :]
            if which == "act":
                if gain is None:
                    nc.scalar.copy(out, inp)
                else:
                    nc.scalar.activation(out, inp, ACT.Identity, bias=shift[:, c:c + 1], scale=gain[:, c:c + 1])
            elif gain is None:
                nc.vector.tensor_copy(out, inp)
            else:
                nc.vector.tensor_scalar(out, inp, gain[:, c:c + 1], shift[:, c:c + 1], ALU.mult, ALU.add)

        @block.scalar
        def _(act):
            if w_at:
                act.wait_ge(*w_at)
            for q in (0, 2):
                copy(act, "act", q)

        @block.vector
        def _(dve):
            if w_at:
                dve.wait_ge(*w_at)
            for q in (1, 3):
                copy(dve, "dve", q)


def transpose_channels(k, src, dst, adds):
    nc = k.nc
    with stage(k, "turned") as (block, s):
        @block.tensor
        def _(pe):
            for t in range(NT):
                for c in range(DC):
                    last = nc.tensor.transpose(k.ps[:, t // 2, (t % 2) * D + c * P:(t % 2) * D + (c + 1) * P],
                                               src[:, c, t * P:(t + 1) * P], k.ident)
                if t % 2:
                    last.then_inc(s.turned, 1)

        @block.vector
        def _(dve):
            for q in range(NT // 2):
                dve.wait_ge(s.turned, q + 1)
                nc.vector.tensor_tensor(dst[:, 2 * q:2 * q + 2, :], adds[:, 2 * q:2 * q + 2, :],
                                        k.ps[:, q, :].rearrange("p (t d) -> p t d", d=D), ALU.add)


def project(k, src, jobs, w_at, token_major=()):
    nc = k.nc
    units = []
    for dst, w, bias, scale in jobs:
        for m in range(w.shape[2] // P):
            for half in range(2):
                units.append(("channel", dst, w, bias, scale, m, half))
    for dst, w, r in token_major:
        for q in range(NT // 2):
            units.append(("token", dst, w, r, None, None, q))
    owner, rank, count = [], [], {"act": 0, "dve": 0}
    for n, (kind, _, _, bias, scale, _, _) in enumerate(units):
        able = bias is None or (kind == "channel" and scale == 1.0)
        owner.append("act" if n % 2 == 0 and able else "dve")
        rank.append(count[owner[n]])
        count[owner[n]] += 1
    with stage(k, "product_done taken_act taken_dve") as (block, s):
        @block.tensor
        def _(pe):
            pe.wait_ge(*w_at)
            for n, (kind, dst, w, bias, scale, m, q) in enumerate(units):
                if n >= 8:
                    pe.wait_ge(s.taken_act if owner[n - 8] == "act" else s.taken_dve, rank[n - 8] + 1)
                if kind == "channel":
                    for c in range(DC):
                        last = nc.tensor.matmul(k.ps[:, n % 8, :], w[:, c, m * P:(m + 1) * P],
                                                src[:, c, q * 512:(q + 1) * 512], start=c == 0, stop=c == DC - 1)
                else:
                    for t in range(2):
                        for c in range(DC):
                            at = (2 * q + t) * P
                            last = nc.tensor.matmul(k.ps[:, n % 8, t * D:(t + 1) * D], src[:, c, at:at + P], w[:, c, :],
                                                    start=c == 0, stop=c == DC - 1)
                last.then_inc(s.product_done, 1)

        @block.scalar
        def _(act):
            act.wait_ge(*w_at)
            for n, (kind, dst, w, bias, scale, m, q) in enumerate(units):
                if owner[n] == "dve":
                    continue
                act.wait_ge(s.product_done, n + 1)
                bank = k.ps[:, n % 8, :]
                if kind == "token":
                    nc.scalar.copy(dst[:, 2 * q:2 * q + 2, :],
                                   bank.rearrange("p (t d) -> p t d", d=D)).then_inc(s.taken_act, 1)
                elif bias is None:
                    nc.scalar.mul(dst[:, m, q * 512:(q + 1) * 512], bank, scale).then_inc(s.taken_act, 1)
                else:
                    nc.scalar.activation(dst[:, m, q * 512:(q + 1) * 512], bank, ACT.Identity,
                                         bias=bias[:, m:m + 1]).then_inc(s.taken_act, 1)

        @block.vector
        def _(dve):
            dve.wait_ge(*w_at)
            for n, (kind, dst, w, bias, scale, m, q) in enumerate(units):
                if owner[n] == "act":
                    continue
                dve.wait_ge(s.product_done, n + 1)
                bank = k.ps[:, n % 8, :]
                if kind == "token":
                    out, inp = dst[:, 2 * q:2 * q + 2, :], bank.rearrange("p (t d) -> p t d", d=D)
                    if bias is None:
                        nc.vector.tensor_copy(out, inp).then_inc(s.taken_dve, 1)
                    else:
                        nc.vector.tensor_tensor(out, inp, spread(bias, 2, 1), ALU.add).then_inc(s.taken_dve, 1)
                elif bias is None:
                    nc.vector.tensor_scalar(dst[:, m, q * 512:(q + 1) * 512], bank, scale, None,
                                            ALU.mult).then_inc(s.taken_dve, 1)
                else:
                    nc.vector.tensor_scalar(dst[:, m, q * 512:(q + 1) * 512], bank, bias[:, m:m + 1], scale,
                                            ALU.add, ALU.mult).then_inc(s.taken_dve, 1)


def cross_attention(k, w, qt, heads, hd, clamp=None):
    nc = k.nc
    inner = heads * hd
    ng, kc = heads // 4, inner // P
    gc = max(1, 4 * hd // P)
    gw = 4 * hd
    nh = 8 if hd == 16 else 4
    TAIL = 2 * P
    if hd == 16:
        KB, VB, SB, TB, TTB, OB, OTB = [0, 1], [(2, 0), (2, 256)], 4, [0, 1], 2, 3, 3
    else:
        KB, VB, SB, TB, TTB, OB, OTB = [0, 1, 2, 3], [(4, 0), (5, 0)], 6, [0, 1], 4, 2, 3
    names = ("tail_loaded ctx_loaded0 ctx_loaded1 tail_done tail_ready tail_placed cleared keys_done values_done "
             "keys_ready values_ready spread_ready scores_done clamped max_ready probs_ready turned_done "
             "turned_act turned_dve rsum_ready pv_done o_ready ot_done ot_ready y_done y_added x_ready")
    with stage(k, names) as (block, s), \
            buffers(k, c0=[P, 2, LK], c1=[DK - P, 2, LK], t0=[P, B], t1=[DK - P, B], vtail=[B, inner],
                    vt=[ng, B, inner], key=[P, 2, kc, LK], val=[P, 2, 2, inner], qx=[P, 2, kc, nh, S],
                    p=[P, 2, ng, LK], nmax=[P, 2, ng], sums=[P, 2, ng], rsum=[P, 2, ng],
                    pt=[P, 2, ng * P], ptt=[ng, P], o=[P, P], ot=[ng * hd, 4, P],
                    sc=[P, ng if clamp else 1, LK if clamp else 1]) as b:
        ctx_loaded = [s.ctx_loaded0, s.ctx_loaded1]

        @block.sync
        def _(sp):
            sp.dma_start(b.t0[:], k.ctx_t0).then_inc(s.tail_loaded, 16)
            sp.dma_start(b.t1[:], k.ctx_t1).then_inc(s.tail_loaded, 16)

            def load(n, par):
                sp.dma_start(b.c0[:, par, :], k.ctx0[ds(n, 1)].rearrange("a p l -> (a p) l")).then_inc(ctx_loaded[par], 16)
                sp.dma_start(b.c1[:, par, :], k.ctx1[ds(n, 1)].rearrange("a p l -> (a p) l")).then_inc(ctx_loaded[par], 16)

            load(0, 0)
            load(1, 1)
            sp.wait_ge(s.tail_ready, 1)
            sp.wait_ge(s.cleared, 1)
            for g in range(ng):
                sp.dma_start(b.vt[g:g + 1, :, g * gw:(g + 1) * gw],
                             b.vtail[:, g * gw:(g + 1) * gw]).then_inc(s.tail_placed, 16)

            def body(it, last):
                for j in range(BT):
                    if last and j >= 2:
                        break
                    n = it * BT + j
                    sp.wait_ge(s.values_done, n + 1)
                    load(n + 2, j % 2)

            with sp.Fori(0, NT - 1) as it:
                body(it, False)
            body(NT - 1, True)

        @block.tensor
        def _(pe):
            pe.wait_ge(*w.at)
            pe.wait_ge(s.tail_loaded, 32)
            for c, t in ((0, b.t0), (1, b.t1)):
                kr = P if c == 0 else DK - P
                last = nc.tensor.matmul(k.ps[0:B, 7, 0:inner], t[:], w.wv[0:kr, c, :], start=c == 0, stop=c == 1)
            last.then_inc(s.tail_done, 1)

            def keys_values(m, par, turn, first=False):
                pe.wait_ge(ctx_loaded[par], turn)
                for j in range(kc):
                    if KB[j] == OB and not first:
                        pe.wait_ge(s.o_ready, m)
                    for c, ct in ((0, b.c0), (1, b.c1)):
                        kr = P if c == 0 else DK - P
                        last = nc.tensor.matmul(k.ps[:, KB[j], 0:LK], w.wk[0:kr, c, j * P:(j + 1) * P],
                                                ct[0:kr, par, :], start=c == 0, stop=c == 1)
                last.then_inc(s.keys_done, 1)
                for r in range(2):
                    bank, at = VB[r]
                    for c, ct in ((0, b.c0), (1, b.c1)):
                        kr = P if c == 0 else DK - P
                        last = nc.tensor.matmul(k.ps[:, bank, at:at + inner], ct[0:kr, par, r * P:(r + 1) * P],
                                                w.wv[0:kr, c, :], start=c == 0, stop=c == 1)
                last.then_inc(s.values_done, 1)

            def scores(n, par):
                pe.wait_ge(s.keys_ready, n + 1)
                pe.wait_ge(s.spread_ready, n + 1)
                for g in range(ng):
                    for c in range(gc):
                        chunk = (g * gw) // P + c
                        h0 = ((g * gw) % P) // hd
                        last = nc.tensor.matmul(k.ps[:, SB + g, 0:LK], b.qx[:, par, chunk, h0:h0 + 4, :],
                                                b.key[:, par, chunk, :], start=c == 0, stop=c == gc - 1)
                last.then_inc(s.scores_done, 1)

            def turn_probs(n, par, final):
                pe.wait_ge(s.probs_ready, n + 1)
                if not final:
                    pe.wait_ge(s.keys_ready, n + 2)
                    pe.wait_ge(s.values_ready, n + 2)
                for r in range(2):
                    for g in range(ng):
                        last = nc.tensor.transpose(k.ps[:, TB[r], g * P:(g + 1) * P],
                                                   b.p[:, par, g, r * P:(r + 1) * P], k.ident)
                    last.then_inc(s.turned_done, 1)
                nc.tensor.transpose(k.ps[0:ng, TTB, 0:P], b.p[:, par, :, TAIL], k.ident).then_inc(s.turned_done, 1)

            def probs_values(n, par):
                pe.wait_ge(s.turned_act, 2 * n + 2)
                pe.wait_ge(s.turned_dve, n + 1)
                nc.tensor.matmul(k.ps[:, OB, 0:inner], b.ptt[:], b.vt[:, ds(n, 1), :].rearrange("g a c -> g (a c)"),
                                 start=True, stop=False)
                for g in range(ng):
                    for r in range(2):
                        last = nc.tensor.matmul(k.ps[:, OB, g * gw:(g + 1) * gw], b.pt[:, r, g * P:(g + 1) * P],
                                                b.val[:, par, r, g * gw:(g + 1) * gw], start=False,
                                                stop=(g == ng - 1 and r == 1))
                last.then_inc(s.pv_done, 1)

            def turn_outputs(n):
                pe.wait_ge(s.o_ready, n + 2)
                nc.tensor.transpose(k.ps[:, OTB, 0:P], b.o[:], k.ident).then_inc(s.ot_done, 1)

            def body(it, last):
                for j in range(BT):
                    n = it * BT + j
                    final = last and j == BT - 1
                    if not final:
                        keys_values(n + 1, (j + 1) % 2, it * 64 + 32 * ((j + 1) // 2 + 1))
                    if j > 0:
                        if not final and OTB in KB:
                            pe.wait_ge(s.keys_ready, n + 2)
                        turn_outputs(n - 1)
                    turn_probs(n, j % 2, final)
                    if not final:
                        scores(n + 1, (j + 1) % 2)
                    if j > 0:
                        pe.wait_ge(s.ot_ready, n)
                    probs_values(n, j % 2)
                turn_outputs(it * BT + BT - 1)
                pe.wait_ge(s.ot_ready, it * BT + BT)
                for h in range(4):
                    mm = nc.tensor.matmul(k.ps[:, OTB, 0:D], b.ot[:, h, :], w.wo[0:ng * hd, h, :],
                                          start=h == 0, stop=h == 3)
                mm.then_inc(s.y_done, 1)
                if not last:
                    pe.wait_ge(s.y_added, it + 1)

            keys_values(0, 0, 32, first=True)
            pe.wait_ge(s.tail_ready, 1)
            scores(0, 0)
            pe.wait_ge(s.values_ready, 1)
            pe.wait_ge(s.tail_placed, 16 * ng)
            with pe.Fori(0, NT - 1) as it:
                body(it, False)
            body(NT - 1, True)

        @block.scalar
        def _(act):
            act.wait_ge(*w.at)

            def take_keys(n, par):
                act.wait_ge(s.keys_done, n + 1)
                for j in range(kc):
                    if w.bk is None:
                        last = nc.scalar.copy(b.key[:, par, j, :], k.ps[:, KB[j], 0:LK])
                    else:
                        last = nc.scalar.activation(b.key[:, par, j, :], k.ps[:, KB[j], 0:LK], ACT.Identity,
                                                    bias=w.bk[:, j:j + 1])
                last.then_inc(s.keys_ready, 1)

            def exponentials(n, par):
                act.wait_ge(s.max_ready, n + 1)
                for g in range(ng):
                    score = b.sc[:, g, :] if clamp else k.ps[:, SB + g, 0:LK]
                    last = nc.scalar.activation(b.p[:, par, g, :], score, ACT.Exp, bias=b.nmax[:, par, g:g + 1],
                                                accum_out=b.sums[:, par, g:g + 1])
                last.then_inc(s.probs_ready, 1)

            def take_turned_outputs(n, j):
                act.wait_ge(s.ot_done, n + 1)
                nc.scalar.copy(b.ot[:, :, j * S:(j + 1) * S],
                               k.ps[0:ng * hd, OTB, 0:P].rearrange("p (h q) -> p h q", q=S)).then_inc(s.ot_ready, 1)

            def body(it, last):
                for j in range(BT):
                    n = it * BT + j
                    final = last and j == BT - 1
                    if not final:
                        take_keys(n + 1, (j + 1) % 2)
                    if j > 0:
                        take_turned_outputs(n - 1, j - 1)
                    act.wait_ge(s.turned_done, 3 * n + 1)
                    nc.scalar.copy(b.pt[:, 0, :], k.ps[:, TB[0], 0:ng * P]).then_inc(s.turned_act, 1)
                    act.wait_ge(s.turned_done, 3 * n + 3)
                    nc.scalar.copy(b.ptt[:], k.ps[0:ng, TTB, 0:P]).then_inc(s.turned_act, 1)
                    if not final:
                        exponentials(n + 1, (j + 1) % 2)
                take_turned_outputs(it * BT + BT - 1, BT - 1)

            take_keys(0, 0)
            exponentials(0, 0)
            with act.Fori(0, NT - 1) as it:
                body(it, False)
            body(NT - 1, True)

        @block.gpsimd
        def _(pool):
            nc.gpsimd.memset(b.vt[:], 0.0).then_inc(s.cleared, 1)
            nc.gpsimd.memset(b.o[:], 0.0).then_inc(s.cleared, 1)

            def spread_queries(n, par):
                for c in range(kc):
                    m = k.head8 if hd == 16 else k.half4[:, c % 2, :]
                    q = spread(qt[:, c, ds(n * S, S)], nh, 1)
                    last = nc.gpsimd.tensor_tensor(b.qx[:, par, c, :, :], q, spread(m, S, 2), ALU.mult)
                last.then_inc(s.spread_ready, 1)

            spread_queries(0, 0)
            spread_queries(1, 1)

            def body(it, last):
                for j in range(BT):
                    if last and j >= 2:
                        break
                    n = it * BT + j
                    pool.wait_ge(s.scores_done, n + 1)
                    spread_queries(n + 2, j % 2)

            with pool.Fori(0, NT - 1) as it:
                body(it, False)
            body(NT - 1, True)

        @block.vector
        def _(dve):
            dve.wait_ge(*w.at)
            dve.wait_ge(s.cleared, 2)
            dve.sem_inc(s.o_ready, 1)
            dve.wait_ge(s.tail_done, 1)
            if w.bv is None:
                nc.vector.tensor_copy(b.vtail[:], k.ps[0:B, 7, 0:inner]).then_inc(s.tail_ready, 1)
            else:
                nc.vector.tensor_tensor(b.vtail[:], k.ps[0:B, 7, 0:inner], w.bv[0:B, :], ALU.add).then_inc(s.tail_ready, 1)

            outputs = b.o[:, 0:ng * hd].rearrange("p (g d) -> p g d", d=hd)

            def take_values(n, par):
                dve.wait_ge(s.values_done, n + 1)
                if VB[0][0] == VB[1][0]:
                    src, dst = k.ps[:, VB[0][0], :].rearrange("p (r c) -> p r c", r=2), b.val[:, par, :, :]
                else:
                    src, dst = k.ps[:, VB[0][0]:VB[0][0] + 2, 0:inner], b.val[:, par, :, :]
                if w.bv is None:
                    nc.vector.tensor_copy(dst, src).then_inc(s.values_ready, 1)
                else:
                    nc.vector.tensor_tensor(dst, src, spread(w.bv, 2, 1), ALU.add).then_inc(s.values_ready, 1)

            def maxima(n, par):
                dve.wait_ge(s.scores_done, n + 1)
                score = k.ps[:, SB:SB + ng, 0:LK]
                if clamp:
                    nc.vector.tensor_scalar(b.sc[:], score, clamp, -clamp, ALU.min, ALU.max).then_inc(s.clamped, 1)
                    dve.wait_ge(s.clamped, n + 1)
                    score = b.sc[:]
                nc.vector.tensor_reduce(b.nmax[:, par, :], score, AX.X, ALU.max, negate=True).then_inc(s.max_ready, 1)

            def body(it, last):
                for j in range(BT):
                    n = it * BT + j
                    par = j % 2
                    final = last and j == BT - 1
                    if not final:
                        take_values(n + 1, 1 - par)
                    dve.wait_ge(s.turned_done, 3 * n + 2)
                    nc.vector.tensor_copy(b.pt[:, 1, :], k.ps[:, TB[1], 0:ng * P]).then_inc(s.turned_dve, 1)
                    dve.wait_ge(s.probs_ready, n + 1)
                    nc.vector.reciprocal(b.rsum[:, par, :], b.sums[:, par, :]).then_inc(s.rsum_ready, 1)
                    if not final:
                        maxima(n + 1, 1 - par)
                    dve.wait_ge(s.rsum_ready, n + 1)
                    dve.wait_ge(s.pv_done, n + 1)
                    for h in range(4):
                        rows = slice(h * S, (h + 1) * S)
                        own = k.ps[rows, OB, 0:inner].rearrange("p (g h d) -> p g h d", h=4, d=hd)[:, :, h, :]
                        o = nc.vector.tensor_tensor(outputs[rows, :, :], own, spread(b.rsum[rows, par, :], hd, 2), ALU.mult)
                    o.then_inc(s.o_ready, 1)
                dve.wait_ge(s.y_done, it + 1)
                tile = k.x[:, ds(it, 1), :].rearrange("p a d -> p (a d)")
                nc.vector.tensor_tensor(tile, tile, k.ps[:, OTB, 0:D], ALU.add).then_inc(s.y_added, 1)
                dve.wait_ge(s.y_added, it + 1)
                nc.vector.tensor_tensor(tile, tile, w.bo, ALU.add).then_inc(s.x_ready, 1)

            take_values(0, 0)
            maxima(0, 0)
            with dve.Fori(0, NT - 1) as it:
                body(it, False)
            body(NT - 1, True)


def self_attention(k, w, qt, kt, v, into, causal=False, relu=False, scale=0.25, more=()):
    nc = k.nc
    sets = [(qt, kt), *more]
    HD, NG, GW = 16, 4, 64
    SB, PB, OB, TB, YB = 0, 1, 2, 4, 5
    names = ("cleared spread_ready more_ready vspread_ready scores_done masked max_ready shifted probs_ready "
             "sums_ready rsum_ready turned_done turned_ready pv_done o_ready ot_done ot_ready y_done y_added")
    with stage(k, names) as (block, s), \
            buffers(k, qx=[P, len(sets), DC, BT, 8, S], vx=[P, NG, BT, GW], sc=[P, NG, BT, S], p=[P, NG, BT, S],
                    m=[P, NG, BT], sums=[P, NG, BT], rsum=[P, NG, BT], pt=[P, NG, P], o=[P, BT, P],
                    ot=[NG * HD, 4, P]) as b:

        def score_bank():
            return k.ps[:, SB, :].rearrange("p (g b l) -> p g b l", g=NG, b=BT)

        @block.tensor
        def _(pe):
            def scores(i):
                pe.wait_ge(s.spread_ready, i + 1)
                if more:
                    pe.wait_ge(s.more_ready, i + 1)
                for g in range(NG):
                    c, h0 = g // 2, 4 * (g % 2)
                    for b_ in range(BT):
                        at = (g * BT + b_) * S
                        for m, (_, keys) in enumerate(sets):
                            last = nc.tensor.matmul(k.ps[:, SB, at:at + S], b.qx[:, m, c, b_, h0:h0 + 4, :],
                                                    keys[:, c, ds(i * P + b_ * S, S)], start=m == 0,
                                                    stop=m == len(sets) - 1)
                last.then_inc(s.scores_done, 1)

            def body(i, last):
                pe.wait_ge(s.probs_ready, i + 1)
                for g in range(NG):
                    mm = nc.tensor.transpose(k.ps[:, PB, g * P:(g + 1) * P],
                                             b.p[:, g, :, :].rearrange("p b l -> p (b l)"), k.ident)
                mm.then_inc(s.turned_done, 1)
                if not last:
                    scores(i + 1)
                pe.wait_ge(s.turned_ready, i + 1)
                pe.wait_ge(s.vspread_ready, i + 1)
                for g in range(NG):
                    mm = nc.tensor.matmul(k.ps[:, OB + g // 2, (g % 2) * 256:(g % 2) * 256 + 256], b.pt[:, g, :],
                                          b.vx[:, g, :, :].rearrange("p b c -> p (b c)"), start=True, stop=True)
                mm.then_inc(s.pv_done, 1)
                pe.wait_ge(s.o_ready, i + 1)
                for b_ in range(BT):
                    mm = nc.tensor.transpose(k.ps[:, TB, b_ * P:(b_ + 1) * P], b.o[:, b_, :], k.ident)
                mm.then_inc(s.ot_done, 1)
                pe.wait_ge(s.ot_ready, i + 1)
                for h in range(4):
                    mm = nc.tensor.matmul(k.ps[:, YB, 0:D], b.ot[:, h, :], w.wo[0:NG * HD, h, :],
                                          start=h == 0, stop=h == 3)
                mm.then_inc(s.y_done, 1)
                if not last:
                    pe.wait_ge(s.y_added, i + 1)

            pe.wait_ge(*w.at)
            scores(0)
            with pe.Fori(0, NT - 1) as i:
                body(i, False)
            body(NT - 1, True)

        @block.scalar
        def _(act):
            def probs(i):
                if relu:
                    act.wait_ge(s.scores_done, i + 1)
                    nc.scalar.activation(b.p[:], score_bank(), ACT.Relu, scale=scale).then_inc(s.probs_ready, 1)
                else:
                    act.wait_ge(s.shifted, i + 1)
                    nc.scalar.activation(b.p[:], b.sc[:], ACT.Exp, scale=scale).then_inc(s.probs_ready, 1)

            def body(i, last):
                act.wait_ge(s.turned_done, i + 1)
                nc.scalar.copy(b.pt[:], k.ps[:, PB, :].rearrange("p (g c) -> p g c", g=NG)).then_inc(s.turned_ready, 1)
                if not last:
                    act.wait_ge(s.sums_ready, i + 1)
                    probs(i + 1)
                act.wait_ge(s.ot_done, i + 1)
                nc.scalar.copy(b.ot[:].rearrange("p h (b q) -> p h b q", b=BT),
                               k.ps[0:NG * HD, TB, :].rearrange("p (b h q) -> p h b q", b=BT, h=4)).then_inc(s.ot_ready, 1)

            probs(0)
            with act.Fori(0, NT - 1) as i:
                body(i, False)
            body(NT - 1, True)

        @block.gpsimd
        def _(pool):
            nc.gpsimd.memset(b.o[:], 0.0).then_inc(s.cleared, 1)

            def spread_queries(i):
                for c in range(DC):
                    for b_ in range(BT):
                        last = nc.gpsimd.tensor_tensor(b.qx[:, 0, c, b_, :, :], spread(qt[:, c, ds(i * P + b_ * S, S)], 8, 1),
                                                       spread(k.head8, S, 2), ALU.mult)
                last.then_inc(s.spread_ready, 1)

            def spread_values(i):
                for g in range(NG):
                    vg = v[:, ds(i, 1), g * GW:(g + 1) * GW].rearrange("p a c -> p (a c)")
                    last = nc.gpsimd.tensor_tensor(b.vx[:, g, :, :], spread(vg, BT, 1), spread(k.seq4, GW, 2), ALU.mult)
                last.then_inc(s.vspread_ready, 1)

            spread_queries(0)
            spread_values(0)
            with pool.Fori(0, NT - 1) as i:
                pool.wait_ge(s.scores_done, i + 1)
                spread_queries(i + 1)
                pool.wait_ge(s.pv_done, i + 1)
                spread_values(i + 1)

        @block.vector
        def _(dve):
            def spread_more(i):
                for m in range(1, len(sets)):
                    for c in range(DC):
                        for b_ in range(BT):
                            last = nc.vector.tensor_tensor(b.qx[:, m, c, b_, :, :],
                                                           spread(sets[m][0][:, c, ds(i * P + b_ * S, S)], 8, 1),
                                                           spread(k.head8, S, 2), ALU.mult)
                if more:
                    last.then_inc(s.more_ready, 1)

            def shift(i):
                dve.wait_ge(s.scores_done, i + 1)
                if relu:
                    return
                src = score_bank()
                if causal:
                    flat = b.sc[:].rearrange("p g b l -> p (g b) l")
                    nc.vector.tensor_tensor(flat, src.rearrange("p g b l -> p (g b) l"), spread(k.causal, NG * BT, 1),
                                            ALU.add).then_inc(s.masked, 1)
                    dve.wait_ge(s.masked, i + 1)
                    src = b.sc[:]
                nc.vector.tensor_reduce(b.m[:], src, AX.X, ALU.max).then_inc(s.max_ready, 1)
                dve.wait_ge(s.max_ready, i + 1)
                nc.vector.tensor_tensor(b.sc[:], src, spread(b.m[:], S, 3), ALU.subtract).then_inc(s.shifted, 1)

            def sums(i):
                dve.wait_ge(s.probs_ready, i + 1)
                if relu:
                    nc.vector.tensor_reduce(b.sums[:], b.p[:], AX.X, ALU.add).then_inc(s.masked, 1)
                    dve.wait_ge(s.masked, i + 1)
                    nc.vector.tensor_scalar(b.sums[:], b.sums[:], 1e-6, None, ALU.add).then_inc(s.sums_ready, 1)
                else:
                    nc.vector.tensor_reduce(b.sums[:], b.p[:], AX.X, ALU.add).then_inc(s.sums_ready, 1)
                dve.wait_ge(s.sums_ready, i + 1)
                nc.vector.reciprocal(b.rsum[:], b.sums[:]).then_inc(s.rsum_ready, 1)

            def body(i, last):
                sums(i)
                if not last:
                    if more:
                        spread_more(i + 1)
                    shift(i + 1)
                dve.wait_ge(s.rsum_ready, i + 1)
                dve.wait_ge(s.pv_done, i + 1)
                for h in range(4):
                    rows = slice(h * S, (h + 1) * S)
                    own = k.ps[rows, OB:OB + 2, :].rearrange("p a (g b h d) -> p (a g) b h d", g=2, b=BT, h=4)[:, :, :, h, :]
                    out = b.o[rows, :, 0:NG * HD].rearrange("p b (g d) -> p g b d", g=NG)
                    o = nc.vector.tensor_tensor(out, own, spread(b.rsum[rows, :, :], HD, 3), ALU.mult)
                o.then_inc(s.o_ready, 1)
                dve.wait_ge(s.y_done, i + 1)
                tile = into[:, ds(i, 1), :].rearrange("p a d -> p (a d)")
                nc.vector.tensor_tensor(tile, tile, k.ps[:, YB, 0:D], ALU.add).then_inc(s.y_added, 1)
                if w.bo is not None:
                    dve.wait_ge(s.y_added, i + 1)
                    nc.vector.tensor_tensor(tile, tile, w.bo, ALU.add)

            dve.wait_ge(*w.at)
            dve.wait_ge(s.cleared, 1)
            if more:
                spread_more(0)
            shift(0)
            with dve.Fori(0, NT - 1) as i:
                body(i, False)
            body(NT - 1, True)


def phase_features(k, w, qk, ph, amp, sn, cs):
    nc = k.nc
    PI = float(np.float32(np.pi))
    names = ("abs_done exp_done plus_done rest_done ln_done sum_done amp_done square_done mean_done root_done "
             "recip_done norm_done tanh_done fold_done sin_done cos_done lam_tanh lam_done const_done sq_ready q_sin")
    with stage(k, names) as (block, s), \
            buffers(k, f=[P, 2, DC, T], eps=[P, 1], half=[P, 1], lam=[P, 2, DC]) as b:
        @block.vector
        def _(dve):
            nc.vector.memset(b.eps[:], 1e-6).then_inc(s.const_done, 1)
            nc.vector.memset(b.half[:], PI / 2).then_inc(s.const_done, 1)
            for u in range(2):
                nc.vector.scalar_tensor_tensor(amp[:, u], qk[:, u], -1.0, qk[:, u], ALU.mult, ALU.max).then_inc(s.abs_done, 1)
            for u in range(2):
                dve.wait_ge(s.exp_done, u + 1)
                nc.vector.tensor_scalar(b.f[:, u], amp[:, u], 1.0, None, ALU.add).then_inc(s.plus_done, 1)
                dve.wait_ge(s.plus_done, u + 1)
                nc.vector.scalar_tensor_tensor(amp[:, u], b.f[:, u], -1.0, amp[:, u], ALU.add,
                                               ALU.subtract).then_inc(s.rest_done, 1)
            for u in range(2):
                dve.wait_ge(s.ln_done, u + 1)
                nc.vector.scalar_tensor_tensor(b.f[:, u], qk[:, u], 0.0, b.f[:, u], ALU.max, ALU.add).then_inc(s.sum_done, 1)
                dve.wait_ge(s.sum_done, u + 1)
                dve.wait_ge(s.rest_done, u + 1)
                nc.vector.tensor_tensor(amp[:, u], b.f[:, u], amp[:, u], ALU.subtract).then_inc(s.amp_done, 1)
                dve.wait_ge(s.amp_done, u + 1)
                nc.vector.tensor_tensor(b.f[:, u], amp[:, u], amp[:, u], ALU.mult).then_inc(s.square_done, 1)
            dve.wait_ge(s.lam_tanh, 1)
            nc.vector.tensor_scalar(b.lam[:, 1], b.lam[:, 0], 0.5, None, ALU.mult).then_inc(s.lam_done, 1)
            for u in range(2):
                dve.wait_ge(s.root_done, 4 * (u + 1))
                nc.vector.reciprocal(b.f[:, u], b.f[:, u]).then_inc(s.recip_done, 1)
                dve.wait_ge(s.recip_done, u + 1)
                nc.vector.tensor_tensor(amp[:, u], amp[:, u], b.f[:, u], ALU.mult).then_inc(s.norm_done, 1)
            for u in range(2):
                dve.wait_ge(s.tanh_done, u + 1)
                dve.wait_ge(s.norm_done, u + 1)
                nc.vector.scalar_tensor_tensor(b.f[:, u], ph[:, u], -1.0, ph[:, u], ALU.mult, ALU.max).then_inc(s.fold_done, 1)
            dve.wait_ge(s.lam_done, 1)
            for u in range(2):
                for done, t in ((s.sin_done, sn), (s.cos_done, cs)):
                    dve.wait_ge(done, u + 1)
                    if u == 0:
                        for c in range(DC):
                            nc.vector.scalar_tensor_tensor(t[:, u, c], t[:, u, c], b.lam[:, 1, c:c + 1], amp[:, u, c],
                                                           ALU.mult, ALU.mult)
                    else:
                        nc.vector.tensor_tensor(t[:, u], t[:, u], amp[:, u], ALU.mult)

        @block.scalar
        def _(act):
            for u in range(2):
                act.wait_ge(s.abs_done, u + 1)
                nc.scalar.activation(amp[:, u], amp[:, u], ACT.Exp, scale=-1.0).then_inc(s.exp_done, 1)
            for u in range(2):
                act.wait_ge(s.plus_done, u + 1)
                act.wait_ge(s.rest_done, u + 1)
                nc.scalar.activation(b.f[:, u], b.f[:, u], ACT.Ln).then_inc(s.ln_done, 1)
            act.wait_ge(*w.at)
            nc.scalar.activation(b.lam[:, 0], w.lam, ACT.Tanh).then_inc(s.lam_tanh, 1)
            for u in range(2):
                nc.scalar.activation(ph[:, u], ph[:, u], ACT.Tanh).then_inc(s.tanh_done, 1)
            act.wait_ge(s.const_done, 2)
            for u in range(2):
                for q in range(4):
                    act.wait_ge(s.mean_done, 4 * u + q + 1)
                    nc.scalar.activation(b.f[:, u, q // 2, (q % 2) * 512:(q % 2) * 512 + 512], k.ps[:, 4 * u + q, :],
                                         ACT.Sqrt, bias=b.eps[:, 0:1]).then_inc(s.root_done, 1)
            act.wait_ge(s.tanh_done, 2)
            for u in range(2):
                nc.scalar.activation(sn[:, u], ph[:, u], ACT.Sin, scale=PI).then_inc(s.sin_done, 1)
            for u in range(2):
                act.wait_ge(s.fold_done, u + 1)
                nc.scalar.activation(cs[:, u], b.f[:, u], ACT.Sin, bias=b.half[:, 0:1], scale=-PI).then_inc(s.cos_done, 1)

        @block.tensor
        def _(pe):
            for u in range(2):
                pe.wait_ge(s.square_done, u + 1)
                for q in range(4):
                    nc.tensor.matmul(k.ps[:, 4 * u + q, :], k.headmean, b.f[:, u, q // 2, (q % 2) * 512:(q % 2) * 512 + 512],
                                     start=True, stop=True).then_inc(s.mean_done, 1)


def gate(k, w, n_exp, top, kind, comb, comb_t):
    nc = k.nc
    E = n_exp
    CAP = int(1.25 * T * top / E)
    W = NT * E
    down = k.down8 if E == 8 else k.down16
    mm_name = "logits_done step exp_done mask_ready spread_done comb_ready turned"
    with stage(k, mm_name) as (block, s), \
            buffers(k, l=[P, NT, E], r=[P, NT, E], eq=[P, NT, E], pick=[P, NT, E], mask=[P, NT, E], pr=[P, NT, E],
                    m=[P, NT], m1=[P, NT], sm=[P, NT], rs=[P, NT]) as b:

        @block.tensor
        def _(pe):
            pe.wait_ge(*w.at)
            for t in range(NT):
                for c in range(DC):
                    mm = nc.tensor.matmul(k.ps[:, 0, t * E:(t + 1) * E], k.ht[:, c, t * P:(t + 1) * P], w.gate[:, c, :],
                                          start=c == 0, stop=c == DC - 1)
            mm.then_inc(s.logits_done, 1)
            if kind in ("sequence", "capacity"):
                pe.wait_ge(s.mask_ready, 1)
                flat = b.mask[:].rearrange("p t e -> p (t e)")
                if kind == "sequence":
                    mm = nc.tensor.matmul(k.ps[:, 1, 0:W], k.first, flat, start=True, stop=True)
                else:
                    mm = nc.tensor.matmul(k.ps[:, 1, 0:W], k.before, flat, start=True, stop=False)
                    for t in range(NT - 1):
                        mm = nc.tensor.matmul(k.ps[:, 1, (t + 1) * E:W], k.ones, spread(b.mask[:, t, :], NT - 1 - t, 1),
                                              start=False, stop=t == NT - 2)
                mm.then_inc(s.spread_done, 1)
            if comb_t is not None:
                pe.wait_ge(s.comb_ready, 1)
                for t in range(NT):
                    mm = nc.tensor.transpose(k.ps[0:E, 2 + t // 4, (t % 4) * P:(t % 4 + 1) * P], comb[:, t, :], k.ident)
                mm.then_inc(s.turned, 1)

        @block.scalar
        def _(act):
            if kind != "sequence":
                act.wait_ge(s.step, EXP_AT[kind])
                nc.scalar.activation(b.pr[:], b.pr[:], ACT.Exp,
                                     scale=-1.0 if kind == "capacity" else 1.0).then_inc(s.exp_done, 1)
            if comb_t is not None:
                act.wait_ge(s.turned, 1)
                nc.scalar.copy(comb_t[:].rearrange("e (a n) -> e a n", a=2), k.ps[0:E, 2:4, :])

        @block.vector
        def _(dve):
            steps = [0]

            def step(ins):
                steps[0] += 1
                ins.then_inc(s.step, 1)
                dve.wait_ge(s.step, steps[0])

            def over_experts(a):
                return spread(a[:], E, 2)

            dve.wait_ge(*w.at)
            dve.wait_ge(s.logits_done, 1)
            logits = k.ps[:, 0, 0:W].rearrange("p (t e) -> p t e", e=E)
            if w.gb is None:
                step(nc.vector.tensor_copy(b.l[:], logits))
            else:
                step(nc.vector.tensor_tensor(b.l[:], logits, spread(w.gb, NT, 1), ALU.add))
            if kind == "capacity":
                step(nc.vector.tensor_copy(b.pr[:], b.l[:]))
            elif kind != "sequence":
                step(nc.vector.tensor_reduce(b.m1[:], b.l[:], AX.X, ALU.max))
                step(nc.vector.tensor_tensor(b.pr[:], b.l[:], over_experts(b.m1), ALU.subtract))
            step(nc.vector.tensor_copy(b.r[:], b.l[:]))
            for n in range(top):
                step(nc.vector.tensor_reduce(b.m[:], b.r[:], AX.X, ALU.max))
                step(nc.vector.tensor_tensor(b.eq[:], b.r[:], over_experts(b.m), ALU.is_equal))
                step(nc.vector.tensor_tensor(b.eq[:], b.eq[:], spread(down, NT, 1), ALU.mult))
                step(nc.vector.tensor_reduce(b.m[:], b.eq[:], AX.X, ALU.max))
                step(nc.vector.tensor_tensor(b.pick[:], b.eq[:], over_experts(b.m), ALU.is_equal))
                if n == 0:
                    step(nc.vector.tensor_copy(b.mask[:], b.pick[:]))
                else:
                    step(nc.vector.tensor_tensor(b.mask[:], b.mask[:], b.pick[:], ALU.add))
                if n < top - 1:
                    step(nc.vector.scalar_tensor_tensor(b.r[:], b.pick[:], NEG, b.r[:], ALU.mult, ALU.add))
            if kind == "sequence":
                dve.sem_inc(s.mask_ready, 1)
                dve.wait_ge(s.spread_done, 1)
                chosen = k.ps[:, 1, 0:W].rearrange("p (t e) -> p t e", e=E)
                nc.vector.tensor_scalar(comb[:], chosen, 1.0 / top, None, ALU.mult).then_inc(s.comb_ready, 1)
                return
            dve.wait_ge(s.exp_done, 1)
            if kind == "capacity":
                dve.sem_inc(s.mask_ready, 1)
                step(nc.vector.tensor_scalar(b.pr[:], b.pr[:], 1.0, None, ALU.add))
                step(nc.vector.reciprocal(b.pr[:], b.pr[:]))
            if kind == "masked":
                step(nc.vector.tensor_reduce(b.sm[:], b.pr[:], AX.X, ALU.add))
                step(nc.vector.reciprocal(b.rs[:], b.sm[:]))
                step(nc.vector.tensor_tensor(b.pr[:], b.pr[:], over_experts(b.rs), ALU.mult))
            step(nc.vector.tensor_tensor(b.pr[:], b.pr[:], b.mask[:], ALU.mult))
            step(nc.vector.tensor_reduce(b.sm[:], b.pr[:], AX.X, ALU.add))
            if kind == "masked":
                step(nc.vector.tensor_scalar(b.sm[:], b.sm[:], 1e-12, None, ALU.max))
            if kind == "capacity":
                step(nc.vector.tensor_scalar(b.sm[:], b.sm[:], 1e-6, None, ALU.add))
            step(nc.vector.reciprocal(b.rs[:], b.sm[:]))
            if kind == "capacity":
                step(nc.vector.tensor_tensor(b.pr[:], b.pr[:], over_experts(b.rs), ALU.mult))
                dve.wait_ge(s.spread_done, 1)
                ranks = k.ps[:, 1, 0:W].rearrange("p (t e) -> p t e", e=E)
                step(nc.vector.tensor_scalar(b.eq[:], ranks, float(CAP), None, ALU.is_lt))
                nc.vector.tensor_tensor(comb[:], b.pr[:], b.eq[:], ALU.mult).then_inc(s.comb_ready, 1)
            else:
                nc.vector.tensor_tensor(comb[:], b.pr[:], over_experts(b.rs), ALU.mult).then_inc(s.comb_ready, 1)


EXP_AT = {"softmax": 3, "masked": 3, "capacity": 2}


def ffn(k, w, n_exp, hid, w1, w2, func, comb, comb_t, into, b1=None, row_bias=None, also=None):
    nc = k.nc
    HC = hid // P
    HB = min(4, HC)
    names = "w1_loaded0 w1_loaded1 w2_loaded0 w2_loaded1 h_done g_ready y_done y_free bias_done bias_added bias_placed also_added"
    with stage(k, names) as (block, s), \
            buffers(k, w1=[P, 2, DC, hid], w2=[P, 2, HC, D], g=[P, 2, HC, 512], bias=[P, 2, HC]) as b:
        w1_loaded, w2_loaded = [s.w1_loaded0, s.w1_loaded1], [s.w2_loaded0, s.w2_loaded1]

        @block.sync
        def _(sp):
            def load(e, par):
                sp.dma_start(b.w1[:, par], w1[ds(e, 1)].rearrange("a p c n -> (a p) c n")).then_inc(w1_loaded[par], 16)
                sp.dma_start(b.w2[:, par], w2[ds(e, 1)].rearrange("a p c n -> (a p) c n")).then_inc(w2_loaded[par], 16)

            load(0, 0)
            fetch_weights(k, sp)
            if n_exp > 1:
                load(1, 1)
                with sp.Fori(0, n_exp // 2 - 1) as it:
                    for par in range(2):
                        sp.wait_ge(s.y_done, 16 * it + 8 * (par + 1))
                        load(2 * it + par + 2, par)

        @block.tensor
        def _(pe):
            def hidden(n, par_e, par_n, half, turn, first=False):
                if half == 0:
                    pe.wait_ge(w1_loaded[par_e], turn)
                for h in range(HC):
                    if not (first and h < HB):
                        pe.wait_ge(s.g_ready, n * HC + h - HB + 1)
                    for c in range(DC):
                        mm = nc.tensor.matmul(k.ps[:, h % HB, :], b.w1[:, par_e, c, h * P:(h + 1) * P],
                                              k.ht[:, c, half * 512:(half + 1) * 512], start=c == 0, stop=c == DC - 1)
                    mm.then_inc(s.h_done, 1)

            def outputs(n, par_e, par_n, half, turn):
                if half == 0:
                    pe.wait_ge(w2_loaded[par_e], turn)
                pe.wait_ge(s.g_ready, (n + 1) * HC)
                for t in range(4):
                    pe.wait_ge(s.y_free, 4 * n + t + 1)
                    for h in range(HC):
                        mm = nc.tensor.matmul(k.ps[:, 4 + t, 0:D], b.g[:, par_n, h, t * P:(t + 1) * P],
                                              b.w2[:, par_e, h, :], start=h == 0, stop=h == HC - 1)
                    mm.then_inc(s.y_done, 1)

            if comb_t is not None:
                for t in range(NT):
                    mm = nc.tensor.matmul(k.ps[:, 4 + t // 2, (t % 2) * D:(t % 2 + 1) * D], comb_t[:, t * P:(t + 1) * P],
                                          w.b2[0:n_exp, :], start=True, stop=True)
                mm.then_inc(s.bias_done, 1)
            hidden(0, 0, 0, 0, 16, first=True)
            if n_exp > 1:
                def body(it, last):
                    for j in range(4):
                        n = 4 * it + j
                        if not (last and j == 3):
                            m = (j + 1) % 4
                            turn = it * 16 + (32 if j == 3 else 16)
                            hidden(n + 1, m // 2, m % 2, m % 2, turn)
                        outputs(n, j // 2, j % 2, j % 2, it * 16 + 16)

                if n_exp > 2:
                    with pe.Fori(0, n_exp // 2 - 1) as it:
                        body(it, False)
                body(n_exp // 2 - 1, True)
            else:
                hidden(1, 0, 1, 1, 16)
                outputs(0, 0, 0, 0, 16)
                outputs(1, 0, 1, 1, 16)

        @block.scalar
        def _(act):
            def values(n, e, par_n, half, par_e):
                if b1 is not None and half == 0 and n_exp == 1:
                    act.wait_ge(*w.at)
                if b1 is not None and half == 0:
                    nc.scalar.copy(b.bias[:, par_e, :], b1[:, ds(e * HC, HC)]).then_inc(s.bias_placed, 1)
                    act.wait_ge(s.bias_placed, e + 1)
                for h in range(HC):
                    act.wait_ge(s.h_done, n * HC + h + 1)
                    out, inp = b.g[:, par_n, h, :], k.ps[:, h % HB, :]
                    if b1 is None:
                        nc.scalar.activation(out, inp, func).then_inc(s.g_ready, 1)
                    else:
                        nc.scalar.activation(out, inp, func, bias=b.bias[:, par_e, h:h + 1]).then_inc(s.g_ready, 1)

            if n_exp > 1:
                with act.Fori(0, n_exp // 2) as it:
                    for j in range(4):
                        values(4 * it + j, 2 * it + j // 2, j % 2, j % 2, j // 2)
            else:
                values(0, 0, 0, 0, 0)
                values(1, 0, 1, 1, 0)

        @block.vector
        def _(dve):
            if comb_t is not None:
                dve.wait_ge(s.bias_done, 1)
                nc.vector.tensor_tensor(into[:], into[:], k.ps[:, 4:8, :].rearrange("p a (t d) -> p (a t) d", d=D),
                                        ALU.add).then_inc(s.bias_added, 1)
                dve.wait_ge(s.bias_added, 1)
            if also is not None:
                nc.vector.tensor_tensor(into[:], into[:], also[:], ALU.add).then_inc(s.also_added, 1)
                dve.wait_ge(s.also_added, 1)
            if row_bias is not None:
                dve.wait_ge(*w.at)
                nc.vector.tensor_tensor(into[:], into[:], spread(row_bias, NT, 1), ALU.add).then_inc(s.bias_added, 1)
                dve.wait_ge(s.bias_added, 1)
            dve.sem_inc(s.y_free, 4)

            def add(n, e, half):
                for t in range(4):
                    dve.wait_ge(s.y_done, 4 * n + t + 1)
                    tile = into[:, half * 4 + t, :]
                    if comb is None:
                        nc.vector.tensor_tensor(tile, tile, k.ps[:, 4 + t, 0:D], ALU.add).then_inc(s.y_free, 1)
                    else:
                        share = comb[:, half * 4 + t, ds(e, 1)]
                        nc.vector.scalar_tensor_tensor(tile, k.ps[:, 4 + t, 0:D], share, tile, ALU.mult,
                                                       ALU.add).then_inc(s.y_free, 1)

            if n_exp > 1:
                with dve.Fori(0, n_exp // 2) as it:
                    for j in range(4):
                        add(4 * it + j, 2 * it + j // 2, j % 2)
            else:
                add(0, 0, 0)
                add(1, 0, 1)


def clear(k, view):
    nc = k.nc
    with stage(k, "cleared") as (block, s):
        @block.gpsimd
        def _(pool):
            for c in range(view.shape[1]):
                nc.gpsimd.memset(view[:, c], 0.0).then_inc(s.cleared, 1)


def convolve(k, w, hp, ct):
    nc = k.nc
    taps = w.conv.shape[2]
    with stage(k, "conv_done") as (block, s):
        @block.tensor
        def _(pe):
            pe.wait_ge(*w.at)
            for m in range(DC):
                for half in range(2):
                    for j in range(taps):
                        mm = nc.tensor.matmul(k.ps[:, 2 * m + half, :], w.conv[:, m, j, :],
                                              hp[:, m, half * 16:(half + 1) * 16, j:j + S], start=j == 0, stop=j == taps - 1)
                    mm.then_inc(s.conv_done, 1)

        @block.scalar
        def _(act):
            for q in (0, 2):
                act.wait_ge(s.conv_done, q + 1)
                nc.scalar.activation(ct[:, q // 2, 0:512], k.ps[:, q, :], ACT.Identity, bias=w.cb[:, q // 2:q // 2 + 1])

        @block.vector
        def _(dve):
            for q in (1, 3):
                dve.wait_ge(s.conv_done, q + 1)
                nc.vector.tensor_scalar(ct[:, q // 2, 512:1024], k.ps[:, q, :], w.cb[:, q // 2:q // 2 + 1], None, ALU.add)


def pool_keys(k, q, key, v):
    nc = k.nc
    names = "q_sums q_means q_keys k_sums k_means"
    with stage(k, names) as (block, s), buffers(k, acc=[P, DC, T]) as b:
        @block.vector
        def _(dve):
            for c in range(DC):
                nc.vector.tensor_tensor_scan(b.acc[:, c, :], k.keep, q[:, c, :], 0.0, ALU.mult, ALU.add).then_inc(s.q_sums, 1)
            for c in range(DC):
                dve.wait_ge(s.q_sums, c + 1)
                nc.vector.tensor_tensor(q[:, c, :], b.acc[:, c, :], k.rcount, ALU.mult).then_inc(s.q_means, 1)
            for c in range(DC):
                dve.wait_ge(s.q_means, c + 1)
                nc.vector.tensor_tensor(key[:, c, :], q[:, c, :], key[:, c, :], ALU.mult).then_inc(s.q_keys, 1)
            for c in range(DC):
                dve.wait_ge(s.q_keys, c + 1)
                nc.vector.tensor_tensor_scan(b.acc[:, c, :], k.keep, key[:, c, :], 0.0, ALU.mult, ALU.add).then_inc(s.k_sums, 1)
            for c in range(DC):
                dve.wait_ge(s.k_sums, c + 1)
                nc.vector.tensor_tensor(key[:, c, :], b.acc[:, c, :], k.rcount, ALU.mult).then_inc(s.k_means, 1)
            for c in range(DC):
                dve.wait_ge(s.k_means, c + 1)
                nc.vector.tensor_tensor(v[:, c, :], key[:, c, :], v[:, c, :], ALU.mult)


def wide_cross_attention(k, w, qt):
    nc = k.nc
    SB, PB, OB = 6, 7, 4
    names = ("tail_loaded tail_done tail_ready tail_placed ctx_loaded0 ctx_loaded1 ctx_loaded2 ctx_loaded3 keys_done "
             "keys_ready values_done values_ready q_placed scores_done max_ready probs_ready tail_spread turned_done "
             "turned_ready rsum_ready o_done x_ready")
    with stage(k, names) as (block, s), \
            buffers(k, c0=[P, BT, LK], c1=[DK - P, BT, LK], t0=[P, B], t1=[DK - P, B], vtail=[B, D], vt=[BT, NT, D],
                    key=[P, BT, DC, LK], val=[P, BT, 2, D], q=[P, DC, P], p=[P, LK], pb=[P, BT], nmax=[P, 1],
                    sums=[P, 1], rsum=[P, 1], pt=[P, 2, P], ptt=[BT, P]) as b:
        ctx_loaded = [s.ctx_loaded0, s.ctx_loaded1, s.ctx_loaded2, s.ctx_loaded3]
        parts = ((0, b.c0, P), (1, b.c1, DK - P))

        @block.sync
        def _(sp):
            sp.dma_start(b.t0[:], k.ctx_t0).then_inc(s.tail_loaded, 16)
            sp.dma_start(b.t1[:], k.ctx_t1).then_inc(s.tail_loaded, 16)

            def load(i, j):
                n = i * BT + j
                sp.dma_start(b.c0[:, j, :], k.ctx0[ds(n, 1)].rearrange("a p l -> (a p) l")).then_inc(ctx_loaded[j], 16)
                sp.dma_start(b.c1[:, j, :], k.ctx1[ds(n, 1)].rearrange("a p l -> (a p) l")).then_inc(ctx_loaded[j], 16)

            for j in range(BT):
                load(0, j)
            sp.wait_ge(s.tail_ready, 1)
            for j in range(BT):
                sp.dma_start(b.vt[j:j + 1, :, :], b.vtail[j:B:BT, :]).then_inc(s.tail_placed, 16)
            with sp.Fori(0, NT - 1) as i:
                for j in range(BT):
                    sp.wait_ge(s.values_done, i * BT + j + 1)
                    load(i + 1, j)

        @block.gpsimd
        def _(pool):
            def place(i):
                nc.gpsimd.tensor_copy(b.q[:], qt[:, :, ds(i * P, P)]).then_inc(s.q_placed, 1)

            place(0)
            with pool.Fori(0, NT - 1) as i:
                pool.wait_ge(s.scores_done, i + 1)
                place(i + 1)

        @block.tensor
        def _(pe):
            pe.wait_ge(*w.at)
            pe.wait_ge(s.tail_loaded, 32)
            for c, t, kr in ((0, b.t0, P), (1, b.t1, DK - P)):
                mm = nc.tensor.matmul(k.ps[0:B, 7, 0:D], t[:], w.wv[0:kr, c, :], start=c == 0, stop=c == 1)
            mm.then_inc(s.tail_done, 1)

            def keys(i, first=False):
                for j in range(BT):
                    pe.wait_ge(ctx_loaded[j], 32 * (i + 1))
                    if not (first and j < 2):
                        pe.wait_ge(s.keys_ready, i * BT + j - 1)
                    for m in range(DC):
                        for c, ct, kr in parts:
                            mm = nc.tensor.matmul(k.ps[:, 2 * (j % 2) + m, 0:LK], w.wk[0:kr, c, m * P:(m + 1) * P],
                                                  ct[0:kr, j, :], start=c == 0, stop=c == 1)
                    mm.then_inc(s.keys_done, 1)

            def values(i, first=False):
                for j in range(BT):
                    if not (first and j < 2):
                        pe.wait_ge(s.values_ready, i * BT + j - 1)
                    if j == 1 and not first:
                        pe.wait_ge(s.x_ready, i)
                    bank = 5 - j % 2
                    for r in range(2):
                        for c, ct, kr in parts:
                            mm = nc.tensor.matmul(k.ps[:, bank, r * D:(r + 1) * D], ct[0:kr, j, r * P:(r + 1) * P],
                                                  w.wv[0:kr, c, :], start=c == 0, stop=c == 1)
                    mm.then_inc(s.values_done, 1)

            def body(i, last):
                pe.wait_ge(s.keys_ready, (i + 1) * BT)
                pe.wait_ge(s.q_placed, i + 1)
                for j in range(BT):
                    for c in range(DC):
                        mm = nc.tensor.matmul(k.ps[j * S:(j + 1) * S, SB, 0:LK], b.q[:, c, j * S:(j + 1) * S],
                                              b.key[:, j, c, :], start=c == 0, stop=c == DC - 1)
                mm.then_inc(s.scores_done, 1)
                if not last:
                    keys(i + 1)
                pe.wait_ge(s.tail_spread, i + 1)
                for r in range(2):
                    nc.tensor.transpose(k.ps[:, PB, r * P:(r + 1) * P], b.p[:, r * P:(r + 1) * P], k.ident)
                nc.tensor.transpose(k.ps[0:BT, PB, 2 * P:3 * P], b.pb[:], k.ident).then_inc(s.turned_done, 1)
                pe.wait_ge(s.turned_ready, i + 1)
                pe.wait_ge(s.values_ready, (i + 1) * BT)
                nc.tensor.matmul(k.ps[:, OB, 0:D], b.ptt[:], b.vt[:, ds(i, 1), :].rearrange("g a c -> g (a c)"),
                                 start=True, stop=False, skip_group_check=True)
                for j in range(BT):
                    for r in range(2):
                        mm = nc.tensor.matmul(k.ps[j * S:(j + 1) * S, OB, 0:D], b.pt[:, r, j * S:(j + 1) * S],
                                              b.val[:, j, r, :], start=False, stop=r == 1, skip_group_check=True)
                mm.then_inc(s.o_done, 1)
                if not last:
                    values(i + 1)

            pe.wait_ge(s.tail_ready, 1)
            keys(0, first=True)
            values(0, first=True)
            pe.wait_ge(s.tail_placed, 16 * BT)
            with pe.Fori(0, NT - 1) as i:
                body(i, False)
            body(NT - 1, True)

        @block.scalar
        def _(act):
            act.wait_ge(*w.at)

            def take_keys(i):
                for j in range(BT):
                    act.wait_ge(s.keys_done, i * BT + j + 1)
                    for m in range(DC):
                        last = nc.scalar.activation(b.key[:, j, m, :], k.ps[:, 2 * (j % 2) + m, 0:LK], ACT.Identity,
                                                    bias=w.bk[:, m:m + 1])
                    last.then_inc(s.keys_ready, 1)

            def body(i, last):
                act.wait_ge(s.max_ready, i + 1)
                nc.scalar.activation(b.p[:], k.ps[:, SB, 0:LK], ACT.Exp, bias=b.nmax[:, 0:1],
                                     accum_out=b.sums[:, 0:1]).then_inc(s.probs_ready, 1)
                if not last:
                    take_keys(i + 1)

            take_keys(0)
            with act.Fori(0, NT - 1) as i:
                body(i, False)
            body(NT - 1, True)

        @block.vector
        def _(dve):
            dve.wait_ge(*w.at)
            dve.wait_ge(s.tail_done, 1)
            nc.vector.tensor_tensor(b.vtail[:], k.ps[0:B, 7, 0:D], w.bv[0:B, :], ALU.add).then_inc(s.tail_ready, 1)

            def take_values(i):
                for j in range(BT):
                    dve.wait_ge(s.values_done, i * BT + j + 1)
                    nc.vector.tensor_tensor(b.val[:, j, :, :], k.ps[:, 5 - j % 2, :].rearrange("p (r c) -> p r c", r=2),
                                            spread(w.bv, 2, 1), ALU.add).then_inc(s.values_ready, 1)

            def body(i, last):
                dve.wait_ge(s.scores_done, i + 1)
                nc.vector.tensor_reduce(b.nmax[:], k.ps[:, SB, 0:LK], AX.X, ALU.max, negate=True).then_inc(s.max_ready, 1)
                dve.wait_ge(s.probs_ready, i + 1)
                nc.vector.tensor_scalar(b.pb[:], k.seq4, b.p[:, 2 * P:LK], None, ALU.mult).then_inc(s.tail_spread, 1)
                nc.vector.reciprocal(b.rsum[:], b.sums[:]).then_inc(s.rsum_ready, 1)
                dve.wait_ge(s.turned_done, i + 1)
                nc.vector.tensor_copy(b.pt[:], k.ps[:, PB, 0:2 * P].rearrange("p (r c) -> p r c", r=2))
                nc.vector.tensor_copy(b.ptt[:], k.ps[0:BT, PB, 2 * P:3 * P]).then_inc(s.turned_ready, 1)
                dve.wait_ge(s.rsum_ready, i + 1)
                dve.wait_ge(s.o_done, i + 1)
                tile = k.x[:, ds(i, 1), :].rearrange("p a d -> p (a d)")
                nc.vector.scalar_tensor_tensor(tile, k.ps[:, OB, 0:D], b.rsum[:, 0:1], tile, ALU.mult,
                                               ALU.add).then_inc(s.x_ready, 1)
                if not last:
                    take_values(i + 1)

            take_values(0)
            with dve.Fori(0, NT - 1) as i:
                body(i, False)
            body(NT - 1, True)


def build(nc, args, packed, fields, order):
    k = Core()
    k.nc, k.stages, k.buffers = nc, 0, 0
    k.packed, k.fields, k.order = packed, fields, order
    k.in_x, k.out = args["x"], args["out_0"]
    k.in_const = args["const"]
    k.ctx0, k.ctx1, k.ctx_t0, k.ctx_t1 = (args[n] for n in ("ctx0", "ctx1", "ctx_t0", "ctx_t1"))
    k.args = args
    with ExitStack() as ctx:
        def sb(name, *shape):
            return ctx.enter_context(nc.sbuf_tensor(f"{name}_sb", list(shape), F32))

        k.x = sb("x", P, NT, D)
        k.z = sb("z", P, NT, D)
        k.ht = sb("ht", P, DC, T)
        k.store = sb("store", P, 2, max(int(a.shape[1]) for a in packed.values()))
        k.consts = sb("consts", P, int(k.in_const.shape[1]))
        made, at = constants(), 0
        for name, a in made.items():
            made[name] = k.consts[:, at:at + a.shape[1]]
            at += a.shape[1]
        k.ident, k.head8, k.seq4, k.causal, k.headmean, k.first = (
            made[n] for n in ("ident", "head8", "seq4", "causal", "headmean", "first"))
        k.before, k.ones, k.down8, k.down16, k.keep, k.rcount = (
            made[n] for n in ("before", "ones", "down8", "down16", "keep", "rcount"))
        k.half4 = made["half4"].rearrange("p (c h) -> p c h", c=2)
        k.ps = ctx.enter_context(nc.psum_tensor("ps", [P, 8, BANK], F32))
        k.weights_loaded = [ctx.enter_context(nc.semaphore(f"weights_loaded{h}")) for h in range(2)]
        k.stored = ctx.enter_context(nc.semaphore("stored"))
        k.fetched, k.fetch_to = 0, 2
        load_inputs(k)

        def begin(name):
            k.fetch_to = order.index(name) + 2
            return weights(k, name)

        for name in order:
            w = begin(name)
            if name in ("L0_xattn", "L1_xattn", "L2_xattn"):
                heads, hd = (8, 64) if name == "L2_xattn" else (16, 16)
                with buffers(k, qt=[P, heads * hd // P, T]) as b:
                    normalize(k, k.x, k.z)
                    transpose_tokens(k, k.z, k.ht)
                    project(k, k.ht, [(b.qt, w.wq, w.bq, 0.25 if hd == 16 else 0.125)], w.at)
                    cross_attention(k, w, b.qt, heads, hd, clamp=1.0e4 if name == "L1_xattn" else None)
            if name in ("L1_attn", "L3_attn", "L3_gqa"):
                with buffers(k, qt=[P, DC, T], kt=[P, DC, T], v=[P, NT, D]) as b:
                    normalize(k, k.x, k.z)
                    transpose_tokens(k, k.z, k.ht)
                    project(k, k.ht, [(b.qt, w.wq, w.bq, 1.0), (b.kt, w.wk, w.bk, 1.0)], w.at, [(b.v, w.wv, w.bv)])
                    self_attention(k, w, b.qt, b.kt, b.v, k.x if name == "L3_attn" else k.z,
                                   causal=name == "L3_attn", relu=name == "L1_attn")
                if name == "L1_attn":
                    normalize(k, k.z, k.z, gain=w.gamma, shift=w.beta, w_at=w.at, add=k.x)
            if name == "L0_attn":
                with buffers(k, qk=[P, 2, DC, T], v=[P, NT, D], sn=[P, 2, DC, T], cs=[P, 2, DC, T]) as b:
                    normalize(k, k.x, k.z)
                    transpose_tokens(k, k.z, k.ht)
                    with buffers(k, ph=[P, 2, DC, T], amp=[P, 2, DC, T]) as f:
                        project(k, k.ht, [(b.qk[:, 0], w.wq, None, 1.0), (b.qk[:, 1], w.wk, None, 1.0),
                                          (f.ph[:, 0], w.wqp, None, 1.0), (f.ph[:, 1], w.wkp, None, 1.0)], w.at,
                                [(b.v, w.wv, None)])
                        phase_features(k, w, b.qk, f.ph, f.amp, b.sn, b.cs)
                    self_attention(k, w, b.qk[:, 0], b.qk[:, 1], b.v, k.x, causal=True,
                                   more=[(b.sn[:, 0], b.sn[:, 1]), (b.cs[:, 0], b.cs[:, 1])])
            if name in ("L0_ffn", "L1_ffn", "L2_ffn", "L3_ffn"):
                n_exp, hid, top, kind, func = {
                    "L0_ffn": (8, 1024, 2, "softmax", ACT.Gelu), "L1_ffn": (16, 512, 3, "masked", ACT.Relu),
                    "L2_ffn": (8, 256, 2, "sequence", ACT.Gelu), "L3_ffn": (8, 512, 2, "capacity", ACT.Gelu)}[name]
                biased = name != "L3_ffn"
                if biased:
                    normalize(k, k.x, k.z)
                else:
                    normalize(k, k.z, k.z, rms=True, gain=gains[0], eps=1e-6, w_at=gains[2])
                transpose_tokens(k, k.z, k.ht)
                with ExitStack() as c2:
                    b = c2.enter_context(buffers(k, comb=[P, NT, n_exp]))
                    comb_t = c2.enter_context(buffers(k, t=[n_exp, T])).t if biased else None
                    gate(k, w, n_exp, top, kind, b.comb, comb_t)
                    ffn(k, w, n_exp, hid, args[f"{name}_w1"], args[f"{name}_w2"], func, b.comb, comb_t,
                        k.x if biased else k.z, b1=w.b1.rearrange("p e h -> p (e h)") if biased else None)
                if not biased:
                    normalize(k, k.z, k.z, rms=True, gain=gains[1], eps=1e-6, add=k.x)
            if name == "L3_gqa":
                gains = (w.gamma, w.gamma2, w.at)
            if name == "L3_xattn":
                with buffers(k, qt=[P, DC, T]) as b:
                    normalize(k, k.x, k.z)
                    transpose_tokens(k, k.z, k.ht)
                    project(k, k.ht, [(b.qt, w.wq, w.bq, 1.0 / 16)], w.at)
                    wide_cross_attention(k, w, b.qt)
            if name == "L2_attn":
                pad = w.conv.shape[2] - 1
                with buffers(k, hn=[P, NT, D]) as b:
                    normalize(k, k.x, k.z)
                    normalize(k, k.z, b.hn)
                    with buffers(k, hp=[P, DC, B, S + pad], ct=[P, DC, T]) as f:
                        clear(k, f.hp[:, :, :, 0:pad])
                        transpose_tokens(k, b.hn, None, w.g1, w.b1, padded=f.hp[:, :, :, pad:], w_at=w.at)
                        convolve(k, w, f.hp, f.ct)
                        transpose_channels(k, f.ct, k.z, k.z)
                    normalize(k, k.z, b.hn)
                    transpose_tokens(k, b.hn, k.ht, w.g2, w.b2, w_at=w.at)
                    with buffers(k, q=[P, DC, T], key=[P, DC, T], v=[P, DC, T]) as f:
                        project(k, k.ht, [(f.q, w.wq, w.bq, 1.0), (f.key, w.wk, w.bk, 1.0), (f.v, w.wv, w.bv, 1.0)], w.at)
                        pool_keys(k, f.q, f.key, f.v)
                        transpose_channels(k, f.v, k.z, k.z)
                    normalize(k, k.z, b.hn)
                    transpose_tokens(k, b.hn, k.ht, w.g3, w.b3, w_at=w.at)
            if name == "L2_boom":
                ffn(k, w, 1, 1024, args["L2_boom_w1"], args["L2_boom_w2"], ACT.Gelu, None, None, k.x,
                    b1=w.b1, row_bias=w.bo, also=k.z)
        store_output(k)


def unlay(y):
    return np.ascontiguousarray(y.transpose(1, 0, 2)).reshape(B, S, D)


def kernel(**inputs):
    import concourse.bacc as _bacc
    from concourse.bass_utils import run_bass_kernel_spmd as _run

    nc = _bacc.Bacc("TRN2", target_bir_lowering=False, num_devices=1)
    i = {n: np.asarray(a) for n, a in inputs.items()}
    arrays = {"x": i["x"].reshape(NT, P, D).transpose(1, 0, 2)}
    ctx = i["ctx_768"].transpose(0, 2, 1)
    arrays["ctx0"], arrays["ctx1"] = ctx[:, 0:P, :], ctx[:, P:DK, :]
    arrays["ctx_t0"], arrays["ctx_t1"] = ctx[:, 0:P, LK - 1].T, ctx[:, P:DK, LK - 1].T
    arrays["const"] = np.concatenate(list(constants().values()), axis=1)
    order = ORDER
    fields = {}
    for name, parts in packs(i).items():
        if name in order:
            fields[name] = [(f, a.shape) for f, a in parts]
            arrays[f"w_{name}"] = np.concatenate([a.reshape(P, -1) for _, a in parts], axis=1)
    for name, a, c in (("L0_ffn", "w1", "w2"), ("L1_ffn", "W1", "W2"), ("L2_ffn", "W1", "W2"), ("L3_ffn", "w1", "w2")):
        if name in order:
            arrays[f"{name}_w1"], arrays[f"{name}_w2"] = experts(i[f"{name}_{a}"], i[f"{name}_{c}"])
    if "L2_boom" in order:
        arrays["L2_boom_w1"], arrays["L2_boom_w2"] = experts(i["L2_attn_Wb"].T[None], i["L2_attn_Wu"].T[None])
    arrays = {n: np.ascontiguousarray(a) for n, a in arrays.items()}
    args = {n: nc.dram_tensor(f"in_{n}", a.shape, mybir.dt.from_np(a.dtype), kind="ExternalInput").ap()
            for n, a in arrays.items()}
    args["out_0"] = nc.dram_tensor("out_0", (P, NT, D), F32, kind="ExternalOutput").ap()
    build(nc, args, {n: args[f"w_{n}"] for n in order}, fields, order)
    r = _run(nc, [{f"in_{n}": a for n, a in arrays.items()}], core_ids=[0])
    return unlay(r.results[0]["out_0"])
```

```python
from collections import namedtuple
from contextlib import ExitStack, contextmanager

import numpy as np

import concourse.bass as bass
from concourse import mybir

F32, F32R = mybir.dt.float32, mybir.dt.float32r
ALU = mybir.AluOpType
ACT = mybir.ActivationFunctionType
AX = mybir.AxisListType
ds = bass.ds

P = 128
B, S, D = 32, 32, 256
T = B * S
NT = T // P
BT = P // S
DC = D // P
LK, DK = 257, 192
LP = LK + LK % 2
BANK = 512
LN_EPS = 1e-5
NEG = -1.0e30



def constants():
    p = np.arange(P)
    f = np.float32
    out = {}
    out["ident"] = np.eye(P, dtype=f)
    out["head8"] = (p[:, None] // 16 == np.arange(8)[None, :]).astype(f)
    out["half4"] = (2 * np.arange(2)[None, :, None] + p[:, None, None] // 64 == np.arange(4)).astype(f).reshape(P, 8)
    out["seq4"] = (p[:, None] // S == np.arange(BT)[None, :]).astype(f)
    out["causal"] = np.where(np.arange(S)[None, :] <= (p % S)[:, None], 0.0, NEG).astype(f)
    out["headmean"] = (p[:, None] // 16 == p[None, :] // 16).astype(f) / f(16)
    out["first"] = (p[:, None] == (p[None, :] // S) * S).astype(f)
    out["before"] = (p[:, None] < p[None, :]).astype(f)
    out["ones"] = np.ones((P, P), f)
    out["down8"] = np.tile(8 - np.arange(8), (P, 1)).astype(f)
    out["down16"] = np.tile(16 - np.arange(16), (P, 1)).astype(f)
    keep = (np.arange(T) % S != 0).astype(f)
    out["keep"] = np.tile(keep, (P, 1))
    out["rcount"] = np.tile((1.0 / (np.arange(T) % S + 1)).astype(f), (P, 1))
    return out


def stacked(w):
    return np.stack([w[0:P], np.concatenate([w[P:], w[P:]])], axis=1)


def chunks(w):
    k = -(-w.shape[0] // P) * P
    w = np.concatenate([w, np.zeros((k - w.shape[0],) + w.shape[1:], w.dtype)]) if k != w.shape[0] else w
    return w.reshape(k // P, P, -1).transpose(1, 0, 2)


def column(v):
    return v.reshape(-1, P).T


def row(v):
    return np.broadcast_to(v.reshape(1, -1), (P, v.size))


def wo_rows(w, ng, hd):
    w = w.reshape(ng, 4, hd, -1).transpose(0, 2, 1, 3).reshape(ng * hd, 4, -1)
    return np.concatenate([w, np.zeros((P - ng * hd,) + w.shape[1:], w.dtype)]) if ng * hd < P else w


def conv_blocks(w):
    g = w.shape[1]
    out = np.zeros((P, DC, w.shape[2], P), w.dtype)
    for c in range(DC):
        for j in range(P // g):
            o = c * P + j * g
            out[j * g:(j + 1) * g, c, :, j * g:(j + 1) * g] = w[o:o + g].transpose(1, 2, 0)
    return out


def packs(i):
    out = {}
    for n in ("L0", "L1", "L2", "L3"):
        g = lambda k: i[f"{n}_xattn_{k}"]
        f = [("wq", chunks(g("Wq"))), ("wk", stacked(g("Wk"))), ("wv", stacked(g("Wv")))]
        if n in ("L0", "L1"):
            f += [("wo", wo_rows(g("Wo"), 4, 16)), ("bq", column(g("bq"))), ("bk", column(g("bk"))),
                  ("bv", row(g("bv"))), ("bo", row(g("bo")))]
        elif n == "L2":
            f += [("wo", wo_rows(g("Wo"), 2, 64)), ("bo", row(g("bo")))]
        else:
            f += [("bq", column(g("bq"))), ("bk", column(g("bk"))), ("bv", row(g("bv")))]
        out[f"{n}_xattn"] = f
    g = lambda k: i[f"L0_attn_{k}"]
    lam = np.repeat(g("lambda_raw"), 16)
    out["L0_attn"] = [("wq", chunks(g("Wq"))), ("wk", chunks(g("Wk"))), ("wv", chunks(g("Wv"))),
                      ("wqp", chunks(g("Wqp"))), ("wkp", chunks(g("Wkp"))), ("wo", wo_rows(g("Wo"), 4, 16)),
                      ("lam", column(lam))]
    w = i["L1_attn_w_qkv"].reshape(D, 16, 3, 16)
    q, k, v = (w[:, :, j].reshape(D, D) for j in range(3))
    out["L1_attn"] = [("wq", chunks(q)), ("wk", chunks(k)), ("wv", chunks(v)), ("wo", wo_rows(i["L1_attn_w_out"], 4, 16)),
                      ("bo", row(i["L1_attn_b_out"])), ("gamma", row(i["L1_attn_gamma"])), ("beta", row(i["L1_attn_beta"]))]
    g = lambda k: i[f"L2_attn_{k}"]
    out["L2_attn"] = [("wq", chunks(g("Wq").T)), ("wk", chunks(g("Wk").T)), ("wv", chunks(g("Wv").T)),
                      ("conv", conv_blocks(g("conv_w")))] + \
                     [(a, column(g(b))) for a, b in (("bq", "bq"), ("bk", "bk"), ("bv", "bv"), ("cb", "conv_b"),
                                                     ("g1", "ln_conv_g"), ("b1", "ln_conv_b"), ("g2", "ln_attn_g"),
                                                     ("b2", "ln_attn_b"), ("g3", "ln_boom_g"), ("b3", "ln_boom_b"))]
    out["L2_boom"] = [("b1", column(g("bb"))), ("bo", row(g("bu")))]
    g = lambda k: i[f"L3_attn_{k}"]
    out["L3_attn"] = [("wq", chunks(g("Wq").reshape(D, D))), ("wk", chunks(g("Wk").reshape(D, D))),
                      ("wv", chunks(g("Wv").reshape(D, D))), ("wo", wo_rows(g("Wout").reshape(D, D), 4, 16))]
    g = lambda k: i[f"L3_ffn_{k}"]

    def heads(w):
        return np.repeat(w.reshape(-1, 4, 16), 4, axis=1).reshape(-1, D)

    out["L3_gqa"] = [("wq", chunks(g("qw"))), ("wk", chunks(heads(g("kw")))), ("wv", chunks(heads(g("vw")))),
                     ("wo", wo_rows(g("ow"), 4, 16)), ("bq", column(g("qb"))), ("bk", column(heads(g("kb")).reshape(-1))),
                     ("bv", row(heads(g("vb")).reshape(-1))), ("bo", row(g("ob"))),
                     ("gamma", row(g("norm1_w"))), ("gamma2", row(g("norm2_w")))]

    def moe(gate, bias, b1, b2):
        f = [("gate", chunks(gate))]
        if bias is not None:
            f.append(("gb", row(bias)))
        if b1 is not None:
            f.append(("b1", b1.reshape(b1.shape[0], -1, P).transpose(2, 0, 1)))
            f.append(("b2", np.concatenate([b2, np.zeros((P - b2.shape[0], D), b2.dtype)])))
        return f

    out["L0_ffn"] = moe(i["L0_ffn_gate_w"], i["L0_ffn_gate_b"], i["L0_ffn_b1"], i["L0_ffn_b2"])
    out["L1_ffn"] = moe(i["L1_ffn_gate"], None, i["L1_ffn_b1"], i["L1_ffn_b2"])
    out["L2_ffn"] = moe(i["L2_ffn_Wr"], i["L2_ffn_br"], i["L2_ffn_b1"], i["L2_ffn_b2"])
    out["L3_ffn"] = moe(i["L3_ffn_gate_w"], None, None, None)
    return out


def experts(w1, w2):
    return (np.stack([chunks(a) for a in w1]), np.stack([chunks(a) for a in w2]))


ORDER = ["L0_xattn", "L0_attn", "L0_ffn", "L1_xattn", "L1_attn", "L1_ffn",
         "L2_xattn", "L2_attn", "L2_boom", "L2_ffn", "L3_xattn", "L3_attn", "L3_gqa", "L3_ffn"]



class Core:
    pass


@contextmanager
def stage(k, names):
    k.stages += 1
    sems = {n: k.nc.alloc_semaphore(name=f"{n}_{k.stages}") for n in names.split()}
    with k.nc.Block() as block:
        yield block, namedtuple("Semaphores", sems)(**sems)
    k.nc.clear_and_free_semaphores(list(sems.values()))
    k.nc.all_engine_barrier(sem_only=True)


@contextmanager
def buffers(k, dtype=F32, **shapes):
    with ExitStack() as ctx:
        k.buffers += 1
        made = {n: ctx.enter_context(k.nc.sbuf_tensor(f"{n}_{k.buffers}", list(s), dtype)) for n, s in shapes.items()}
        yield namedtuple("Buffers", made)(**made)


def fetch_weights(k, sp):
    i = k.fetched
    if i < min(k.fetch_to, len(k.order)):
        k.fetched += 1
        name = k.order[i]
        width = k.packed[name].shape[1]
        sp.dma_start(k.store[:, i % 2, 0:width], k.packed[name]).then_inc(k.weights_loaded[i % 2], 16)


FIELDS = "wq wk wv wo bq bk bv bo wqp wkp lam gamma gamma2 beta conv cb g1 b1 g2 b2 g3 b3 gate gb"
Weights = namedtuple("Weights", "at " + FIELDS, defaults=[None] * len(FIELDS.split()))


def weights(k, name):
    i = k.order.index(name)
    views, at = {}, 0
    for field, shape in k.fields[name]:
        n = int(np.prod(shape[1:]))
        v = k.store[:, i % 2, at:at + n]
        if len(shape) == 3:
            v = v.rearrange("p (a b) -> p a b", a=shape[1])
        if len(shape) == 4:
            v = v.rearrange("p (a b c) -> p a b c", a=shape[1], b=shape[2])
        views[field] = v
        at += n
    return Weights(at=(k.weights_loaded[i % 2], 16 * (i // 2 + 1)), **views)


def spread(ap, n, axis):
    shape = list(ap.shape)
    return ap.unsqueeze(axis).broadcast_to(shape[:axis] + [n] + shape[axis:])


def load_inputs(k):
    nc = k.nc
    with stage(k, "loaded") as (block, s):
        @block.sync
        def _(sp):
            sp.dma_start(k.x[:], k.in_x).then_inc(s.loaded, 16)
            sp.dma_start(k.consts[:], k.in_const).then_inc(s.loaded, 16)
            fetch_weights(k, sp)
            fetch_weights(k, sp)
            sp.wait_ge(s.loaded, 32)


def store_output(k):
    with k.nc.Block() as block:
        @block.sync
        def _(sp):
            sp.dma_start(k.out, k.x[:]).then_inc(k.stored, 16)
            sp.wait_ge(k.stored, 16)


def normalize(k, src, dst, rms=False, gain=None, shift=None, eps=LN_EPS, w_at=None, add=None):
    nc = k.nc
    with stage(k, "stats_done aggr_done std_done rstd_done norm_done gained shifted") as (block, s), \
            buffers(k, stats=[P, NT, 6], mv=[P, NT, 2], std=[P, NT], rstd=[P, NT], sq=[P, 2, D], eps=[P, 1]) as b:
        @block.vector
        def _(dve):
            if w_at:
                dve.wait_ge(*w_at)
            nc.vector.memset(b.eps[:], eps).then_inc(s.stats_done, 1)
            for t in range(NT):
                if rms:
                    if t >= 2:
                        dve.wait_ge(s.stats_done, t)
                    nc.vector.tensor_tensor_reduce(b.sq[:, t % 2, :], src[:, t, :], src[:, t, :], 1.0 / D, 0.0,
                                                   ALU.mult, ALU.add, b.mv[:, t, 1:2]).then_inc(s.stats_done, 1)
                else:
                    nc.vector.bn_stats(b.stats[:, t, :], src[:, t, :]).then_inc(s.stats_done, 1)
            for t in range(NT):
                if not rms:
                    dve.wait_ge(s.stats_done, t + 2)
                    nc.vector.bn_aggr(b.mv[:, t, :], b.stats[:, t, :]).then_inc(s.aggr_done, 1)
            dve.wait_ge(s.std_done, 1)
            nc.vector.reciprocal(b.rstd[:], b.std[:]).then_inc(s.rstd_done, 1)
            dve.wait_ge(s.rstd_done, 1)
            for t in range(NT):
                if rms:
                    nc.vector.tensor_scalar(dst[:, t, :], src[:, t, :], b.rstd[:, t:t + 1], None,
                                            ALU.mult).then_inc(s.norm_done, 1)
                else:
                    nc.vector.tensor_scalar(dst[:, t, :], src[:, t, :], b.mv[:, t, 0:1], b.rstd[:, t:t + 1],
                                            ALU.subtract, ALU.mult).then_inc(s.norm_done, 1)
            if gain is not None:
                dve.wait_ge(s.norm_done, NT)
                nc.vector.tensor_tensor(dst[:], dst[:], spread(gain, NT, 1), ALU.mult).then_inc(s.gained, 1)
            if shift is not None:
                dve.wait_ge(s.gained, 1)
                nc.vector.tensor_tensor(dst[:], dst[:], spread(shift, NT, 1), ALU.add).then_inc(s.shifted, 1)
            if add is not None:
                if shift is not None:
                    dve.wait_ge(s.shifted, 1)
                elif gain is not None:
                    dve.wait_ge(s.gained, 1)
                nc.vector.tensor_tensor(add[:], add[:], dst[:], ALU.add)

        @block.sync
        def _(sp):
            fetch_weights(k, sp)

        @block.scalar
        def _(act):
            act.wait_ge(s.stats_done, NT + 1)
            if not rms:
                act.wait_ge(s.aggr_done, NT)
            nc.scalar.activation(b.std[:], b.mv[:, :, 1], ACT.Sqrt, bias=b.eps[:, 0:1]).then_inc(s.std_done, 1)


def transpose_tokens(k, src, dst, gain=None, shift=None, padded=None, w_at=None):
    nc = k.nc
    with stage(k, "turned copied") as (block, s):
        @block.tensor
        def _(pe):
            for q in range(2 * DC):
                c, half = q % DC, q // DC
                for t in range(4):
                    last = nc.tensor.transpose(k.ps[:, q, t * P:(t + 1) * P],
                                               src[:, half * 4 + t, c * P:(c + 1) * P], k.ident)
                last.then_inc(s.turned, 1)

        def copy(eng, which, q):
            c, half = q % DC, q // DC
            eng.wait_ge(s.turned, q + 1)
            if padded is not None:
                out = padded[:, c, half * 16:(half + 1) * 16, :]
                inp = k.ps[:, q, :].rearrange("p (b s) -> p b s", s=S)
            else:
                out, inp = dst[:, c, half * 512:(half + 1) * 512], k.ps[:, q, :]
            if which == "act":
                if gain is None:
                    nc.scalar.copy(out, inp)
                else:
                    nc.scalar.activation(out, inp, ACT.Identity, bias=shift[:, c:c + 1], scale=gain[:, c:c + 1])
            elif gain is None:
                nc.vector.tensor_copy(out, inp)
            else:
                nc.vector.tensor_scalar(out, inp, gain[:, c:c + 1], shift[:, c:c + 1], ALU.mult, ALU.add)

        @block.scalar
        def _(act):
            if w_at:
                act.wait_ge(*w_at)
            for q in (0, 2):
                copy(act, "act", q)

        @block.vector
        def _(dve):
            if w_at:
                dve.wait_ge(*w_at)
            for q in (1, 3):
                copy(dve, "dve", q)


def transpose_channels(k, src, dst, adds):
    nc = k.nc
    with stage(k, "turned") as (block, s):
        @block.tensor
        def _(pe):
            for t in range(NT):
                for c in range(DC):
                    last = nc.tensor.transpose(k.ps[:, t // 2, (t % 2) * D + c * P:(t % 2) * D + (c + 1) * P],
                                               src[:, c, t * P:(t + 1) * P], k.ident)
                if t % 2:
                    last.then_inc(s.turned, 1)

        @block.vector
        def _(dve):
            for q in range(NT // 2):
                dve.wait_ge(s.turned, q + 1)
                nc.vector.tensor_tensor(dst[:, 2 * q:2 * q + 2, :], adds[:, 2 * q:2 * q + 2, :],
                                        k.ps[:, q, :].rearrange("p (t d) -> p t d", d=D), ALU.add)


def project(k, src, jobs, w_at, token_major=()):
    nc = k.nc
    units = []
    for dst, w, bias, scale in jobs:
        for m in range(w.shape[2] // P):
            for half in range(2):
                units.append(("channel", dst, w, bias, scale, m, half))
    for dst, w, r in token_major:
        for q in range(NT // 2):
            units.append(("token", dst, w, r, None, None, q))
    owner, rank, count = [], [], {"act": 0, "dve": 0}
    for n, (kind, _, _, bias, scale, _, _) in enumerate(units):
        able = bias is None or (kind == "channel" and scale == 1.0)
        owner.append("act" if n % 2 == 0 and able else "dve")
        rank.append(count[owner[n]])
        count[owner[n]] += 1
    with stage(k, "product_done taken_act taken_dve") as (block, s):
        @block.tensor
        def _(pe):
            pe.wait_ge(*w_at)
            for n, (kind, dst, w, bias, scale, m, q) in enumerate(units):
                if n >= 8:
                    pe.wait_ge(s.taken_act if owner[n - 8] == "act" else s.taken_dve, rank[n - 8] + 1)
                if kind == "channel":
                    for c in range(DC):
                        last = nc.tensor.matmul(k.ps[:, n % 8, :], w[:, c, m * P:(m + 1) * P],
                                                src[:, c, q * 512:(q + 1) * 512], start=c == 0, stop=c == DC - 1)
                else:
                    for t in range(2):
                        for c in range(DC):
                            at = (2 * q + t) * P
                            last = nc.tensor.matmul(k.ps[:, n % 8, t * D:(t + 1) * D], src[:, c, at:at + P], w[:, c, :],
                                                    start=c == 0, stop=c == DC - 1)
                last.then_inc(s.product_done, 1)

        @block.scalar
        def _(act):
            act.wait_ge(*w_at)
            for n, (kind, dst, w, bias, scale, m, q) in enumerate(units):
                if owner[n] == "dve":
                    continue
                act.wait_ge(s.product_done, n + 1)
                bank = k.ps[:, n % 8, :]
                if kind == "token":
                    nc.scalar.copy(dst[:, 2 * q:2 * q + 2, :],
                                   bank.rearrange("p (t d) -> p t d", d=D)).then_inc(s.taken_act, 1)
                elif bias is None:
                    nc.scalar.mul(dst[:, m, q * 512:(q + 1) * 512], bank, scale).then_inc(s.taken_act, 1)
                else:
                    nc.scalar.activation(dst[:, m, q * 512:(q + 1) * 512], bank, ACT.Identity,
                                         bias=bias[:, m:m + 1]).then_inc(s.taken_act, 1)

        @block.vector
        def _(dve):
            dve.wait_ge(*w_at)
            for n, (kind, dst, w, bias, scale, m, q) in enumerate(units):
                if owner[n] == "act":
                    continue
                dve.wait_ge(s.product_done, n + 1)
                bank = k.ps[:, n % 8, :]
                if kind == "token":
                    out, inp = dst[:, 2 * q:2 * q + 2, :], bank.rearrange("p (t d) -> p t d", d=D)
                    if bias is None:
                        nc.vector.tensor_copy(out, inp).then_inc(s.taken_dve, 1)
                    else:
                        nc.vector.tensor_tensor(out, inp, spread(bias, 2, 1), ALU.add).then_inc(s.taken_dve, 1)
                elif bias is None:
                    nc.vector.tensor_scalar(dst[:, m, q * 512:(q + 1) * 512], bank, scale, None,
                                            ALU.mult).then_inc(s.taken_dve, 1)
                else:
                    nc.vector.tensor_scalar(dst[:, m, q * 512:(q + 1) * 512], bank, bias[:, m:m + 1], scale,
                                            ALU.add, ALU.mult).then_inc(s.taken_dve, 1)


def cross_attention(k, w, qt, heads, hd, clamp=None):
    nc = k.nc
    inner = heads * hd
    ng, kc = heads // 4, inner // P
    gc = max(1, 4 * hd // P)
    gw = 4 * hd
    nh = 8 if hd == 16 else 4
    TAIL = 2 * P
    if hd == 16:
        KB, VB, SB, TB, OB, OTB = [0, 1], [(2, 0), (2, 256)], 4, [0, 1], 3, 3
    else:
        KB, VB, SB, TB, OB, OTB = [0, 1, 2, 3], [(4, 0), (5, 0)], 6, [0, 1], 2, 3
    TT, YT = slice(3 * P, 4 * P), slice(P, P + D)
    names = ("tail_loaded ctx_loaded0 ctx_loaded1 w_hi w_split ctx_hi ctx_low ctx_split tail_done tail_ready tail_placed cleared keys_done values_done "
             "keys_ready values_ready spread_ready scores_done clamped max_ready probs_ready turned_done "
             "tail_turned turned_act turned_dve rsum_ready pv_done o_ready ot_done ot_ready y_done y_added x_ready")
    with stage(k, names) as (block, s), \
            buffers(k, c=[P, 2, 2, LP], t0=[P, B], t1=[DK - P, B], vtail=[B, inner],
                    vt=[ng, B, inner], key=[P, 2, kc, LK], val=[P, 2, 2, inner], qx=[P, 2, kc, nh, S],
                    p=[P, 2, ng, LK], nmax=[P, 2, ng], sums=[P, 2, ng], rsum=[P, 2, ng],
                    pt=[P, 2, ng * P], ptt=[ng, P], o=[P, P], ot=[ng * hd, 4, P],
                    sc=[P, ng if clamp else 1, LK if clamp else 1]) as b, \
            buffers(k, F32R, w=[P, 2, 2, 2 * inner], c=[P, 2, 2, LP], clo=[P, 2, LP]) as r:
        ctx_loaded = [s.ctx_loaded0, s.ctx_loaded1]

        def factors(par, at, rows):
            whi, wlo = r.w[:, 0, :, at], r.w[:, 1, :, at]
            return ((whi[:, 0], r.c[:, par, 0, rows]), (whi[:, 0], r.clo[:, par, rows]), (wlo[:, 0], r.c[:, par, 0, rows]),
                    (whi[:, 1], r.c[:, par, 1, rows]), (wlo[0:DK - P, 1], r.c[0:DK - P, par, 1, rows]))

        @block.sync
        def _(sp):
            sp.dma_start(b.t0[:], k.ctx_t0).then_inc(s.tail_loaded, 16)
            sp.dma_start(b.t1[:], k.ctx_t1).then_inc(s.tail_loaded, 16)

            def load(n, par):
                sp.dma_start(b.c[:, par], k.ctx[ds(n, 1)].rearrange("a p c l -> (a p) c l")).then_inc(ctx_loaded[par], 16)

            load(0, 0)
            load(1, 1)
            sp.wait_ge(s.tail_ready, 1)
            sp.wait_ge(s.cleared, 1)
            for g in range(ng):
                sp.dma_start(b.vt[g:g + 1, :, g * gw:(g + 1) * gw],
                             b.vtail[:, g * gw:(g + 1) * gw]).then_inc(s.tail_placed, 16)

            def body(it, last):
                for j in range(BT):
                    if last and j >= 2:
                        break
                    n = it * BT + j
                    sp.wait_ge(s.ctx_low, n + 1)
                    sp.wait_ge(s.ctx_split, n + 1)
                    load(n + 2, j % 2)

            with sp.Fori(0, NT - 1) as it:
                body(it, False)
            body(NT - 1, True)

        @block.tensor
        def _(pe):
            pe.wait_ge(*w.at)
            pe.wait_ge(s.tail_loaded, 32)
            for c, t in ((0, b.t0), (1, b.t1)):
                kr = P if c == 0 else DK - P
                last = nc.tensor.matmul(k.ps[0:B, 7, 0:inner], t[:], w.wv[0:kr, c, :], start=c == 0, stop=c == 1)
            last.then_inc(s.tail_done, 1)
            pe.wait_ge(s.w_split, 2)

            def keys_values(m, par, first=False):
                pe.wait_ge(s.ctx_low, m + 1)
                pe.wait_ge(s.ctx_split, m + 1)
                for j in range(kc):
                    if KB[j] == OB and not first:
                        pe.wait_ge(s.o_ready, m)
                    for t, (wp, cp) in enumerate(factors(par, slice(j * P, (j + 1) * P), slice(0, LP))):
                        last = nc.tensor.matmul(k.ps[:, KB[j], 0:LP], wp, cp, start=t == 0, stop=t == 4)
                last.then_inc(s.keys_done, 1)
                for half in range(2):
                    bank, at = VB[half]
                    for t, (wp, cp) in enumerate(factors(par, slice(inner, 2 * inner), slice(half * P, (half + 1) * P))):
                        last = nc.tensor.matmul(k.ps[:, bank, at:at + inner], cp, wp, start=t == 0, stop=t == 4)
                last.then_inc(s.values_done, 1)

            def scores(n, par):
                pe.wait_ge(s.keys_ready, n + 1)
                pe.wait_ge(s.spread_ready, n + 1)
                for g in range(ng):
                    for c in range(gc):
                        chunk = (g * gw) // P + c
                        h0 = ((g * gw) % P) // hd
                        last = nc.tensor.matmul(k.ps[:, SB + g, 0:LK], b.qx[:, par, chunk, h0:h0 + 4, :],
                                                b.key[:, par, chunk, :], start=c == 0, stop=c == gc - 1)
                last.then_inc(s.scores_done, 1)

            def turn_last_column(n, par):
                pe.wait_ge(s.probs_ready, n + 1)
                nc.tensor.transpose(k.ps[0:ng, OTB, TT], b.p[:, par, :, TAIL], k.ident).then_inc(s.tail_turned, 1)

            def turn_probs(n, par, final):
                if not final:
                    pe.wait_ge(s.keys_ready, n + 2)
                for half in range(2):
                    for g in range(ng):
                        last = nc.tensor.transpose(k.ps[:, TB[half], g * P:(g + 1) * P],
                                                   b.p[:, par, g, half * P:(half + 1) * P], k.ident)
                    last.then_inc(s.turned_done, 1)

            def probs_values(n, par):
                pe.wait_ge(s.turned_act, 2 * n + 2)
                pe.wait_ge(s.turned_dve, n + 1)
                nc.tensor.matmul(k.ps[:, OB, 0:inner], b.ptt[:], b.vt[:, ds(n, 1), :].rearrange("g a c -> g (a c)"),
                                 start=True, stop=False)
                for g in range(ng):
                    for half in range(2):
                        last = nc.tensor.matmul(k.ps[:, OB, g * gw:(g + 1) * gw], b.pt[:, half, g * P:(g + 1) * P],
                                                b.val[:, par, half, g * gw:(g + 1) * gw], start=False,
                                                stop=(g == ng - 1 and half == 1))
                last.then_inc(s.pv_done, 1)

            def turn_outputs(n):
                pe.wait_ge(s.o_ready, n + 2)
                nc.tensor.transpose(k.ps[:, OTB, 0:P], b.o[:], k.ident).then_inc(s.ot_done, 1)

            def output_product(it):
                pe.wait_ge(s.ot_ready, it * BT + BT)
                for h in range(4):
                    mm = nc.tensor.matmul(k.ps[:, OTB, YT], b.ot[:, h, :], w.wo[0:ng * hd, h, :],
                                          start=h == 0, stop=h == 3)
                mm.then_inc(s.y_done, 1)

            def body(it, first, last):
                for j in range(BT):
                    n = it * BT + j
                    final = last and j == BT - 1
                    start = first and j == 0
                    if not final:
                        keys_values(n + 1, (j + 1) % 2)
                    if not final and OTB in KB:
                        pe.wait_ge(s.keys_ready, n + 2)
                    if not start:
                        turn_outputs(n - 1)
                    turn_last_column(n, j % 2)
                    turn_probs(n, j % 2, final)
                    if j == 0 and not first:
                        pe.wait_ge(s.turned_act, 2 * n + 1)
                        output_product(it - 1)
                    if not final:
                        scores(n + 1, (j + 1) % 2)
                    if not start:
                        pe.wait_ge(s.ot_ready, n)
                    if j == 0 and not first:
                        pe.wait_ge(s.y_added, it)
                    probs_values(n, j % 2)

            keys_values(0, 0, first=True)
            pe.wait_ge(s.tail_ready, 1)
            scores(0, 0)
            pe.wait_ge(s.values_ready, 1)
            pe.wait_ge(s.tail_placed, 16 * ng)
            body(0, True, False)
            with pe.Fori(1, NT - 1) as it:
                body(it, False, False)
            body(NT - 1, False, True)
            turn_outputs(B - 1)
            output_product(NT - 1)

        @block.scalar
        def _(act):
            act.wait_ge(*w.at)

            def take_keys(n, par):
                act.wait_ge(s.keys_done, n + 1)
                for j in range(kc):
                    if w.bk is None:
                        last = nc.scalar.copy(b.key[:, par, j, :], k.ps[:, KB[j], 0:LK])
                    else:
                        last = nc.scalar.activation(b.key[:, par, j, :], k.ps[:, KB[j], 0:LK], ACT.Identity,
                                                    bias=w.bk[:, j:j + 1])
                last.then_inc(s.keys_ready, 1)

            def exponentials(n, par):
                act.wait_ge(s.max_ready, n + 1)
                for g in range(ng):
                    score = b.sc[:, g, :] if clamp else k.ps[:, SB + g, 0:LK]
                    last = nc.scalar.activation(b.p[:, par, g, :], score, ACT.Exp, bias=b.nmax[:, par, g:g + 1],
                                                accum_out=b.sums[:, par, g:g + 1])
                last.then_inc(s.probs_ready, 1)

            def take_turned_outputs(n, j):
                act.wait_ge(s.ot_done, n + 1)
                nc.scalar.copy(b.ot[:, :, j * S:(j + 1) * S],
                               k.ps[0:ng * hd, OTB, 0:P].rearrange("p (h q) -> p h q", q=S)).then_inc(s.ot_ready, 1)

            def body(it, first, last):
                for j in range(BT):
                    n = it * BT + j
                    final = last and j == BT - 1
                    if not final:
                        take_keys(n + 1, (j + 1) % 2)
                    act.wait_ge(s.tail_turned, n + 1)
                    if not (first and j == 0):
                        take_turned_outputs(n - 1, (j - 1) % BT)
                    nc.scalar.copy(b.ptt[:], k.ps[0:ng, OTB, TT]).then_inc(s.turned_act, 1)
                    act.wait_ge(s.turned_done, 2 * n + 1)
                    nc.scalar.copy(b.pt[:, 0, :], k.ps[:, TB[0], 0:ng * P]).then_inc(s.turned_act, 1)
                    if not final:
                        exponentials(n + 1, (j + 1) % 2)

            for u, part in ((0, w.wk), (1, w.wv)):
                nc.scalar.copy(r.w[:, 0, :, u * inner:(u + 1) * inner], part).then_inc(s.w_hi, 1)
            take_keys(0, 0)
            exponentials(0, 0)
            body(0, True, False)
            with act.Fori(1, NT - 1) as it:
                body(it, False, False)
            body(NT - 1, False, True)
            take_turned_outputs(B - 1, BT - 1)

        @block.gpsimd
        def _(pool):
            nc.gpsimd.memset(b.vt[:], 0.0).then_inc(s.cleared, 1)
            nc.gpsimd.memset(b.o[:], 0.0).then_inc(s.cleared, 1)

            def spread_queries(n, par):
                for c in range(kc):
                    m = k.head8 if hd == 16 else k.half4[:, c % 2, :]
                    q = spread(qt[:, c, ds(n * S, S)], nh, 1)
                    last = nc.gpsimd.tensor_tensor(b.qx[:, par, c, :, :], q, spread(m, S, 2), ALU.mult)
                last.then_inc(s.spread_ready, 1)

            def split_context(n, par):
                pool.wait_ge(s.ctx_hi, n + 1)
                nc.gpsimd.tensor_tensor(r.clo[:, par, :], b.c[:, par, 0, :], r.c[:, par, 0, :],
                                        ALU.subtract).then_inc(s.ctx_split, 1)

            split_context(0, 0)
            spread_queries(0, 0)
            split_context(1, 1)
            spread_queries(1, 1)

            def body(it, last):
                for j in range(BT):
                    if last and j >= 2:
                        break
                    n = it * BT + j
                    split_context(n + 2, j % 2)
                    pool.wait_ge(s.scores_done, n + 1)
                    spread_queries(n + 2, j % 2)

            with pool.Fori(0, NT - 1) as it:
                body(it, False)
            body(NT - 1, True)

        @block.vector
        def _(dve):
            def round_context(n, par, turn):
                dve.wait_ge(ctx_loaded[par], 16 * turn)
                nc.vector.tensor_copy(r.c[:, par], b.c[:, par]).then_inc(s.ctx_hi, 1)
                dve.wait_ge(s.ctx_hi, n + 1)
                low = slice(DK - P, P)
                nc.vector.tensor_tensor(r.c[low, par, 1, :], b.c[low, par, 1, :], r.c[low, par, 1, :],
                                        ALU.subtract).then_inc(s.ctx_low, 1)

            round_context(0, 0, 1)
            round_context(1, 1, 1)
            dve.wait_ge(*w.at)
            for u, part in ((0, w.wk), (1, w.wv)):
                at = slice(u * inner, (u + 1) * inner)
                dve.wait_ge(s.w_hi, u + 1)
                nc.vector.tensor_tensor(r.w[:, 1, :, at], part, r.w[:, 0, :, at], ALU.subtract).then_inc(s.w_split, 1)
            dve.wait_ge(s.cleared, 2)
            dve.sem_inc(s.o_ready, 1)
            dve.wait_ge(s.tail_done, 1)
            if w.bv is None:
                nc.vector.tensor_copy(b.vtail[:], k.ps[0:B, 7, 0:inner]).then_inc(s.tail_ready, 1)
            else:
                nc.vector.tensor_tensor(b.vtail[:], k.ps[0:B, 7, 0:inner], w.bv[0:B, :], ALU.add).then_inc(s.tail_ready, 1)

            outputs = b.o[:, 0:ng * hd].rearrange("p (g d) -> p g d", d=hd)

            def take_values(n, par):
                dve.wait_ge(s.values_done, n + 1)
                if VB[0][0] == VB[1][0]:
                    src, dst = k.ps[:, VB[0][0], :].rearrange("p (r c) -> p r c", r=2), b.val[:, par, :, :]
                else:
                    src, dst = k.ps[:, VB[0][0]:VB[0][0] + 2, 0:inner], b.val[:, par, :, :]
                if w.bv is None:
                    nc.vector.tensor_copy(dst, src).then_inc(s.values_ready, 1)
                else:
                    nc.vector.tensor_tensor(dst, src, spread(w.bv, 2, 1), ALU.add).then_inc(s.values_ready, 1)

            def maxima(n, par):
                dve.wait_ge(s.scores_done, n + 1)
                score = k.ps[:, SB:SB + ng, 0:LK]
                if clamp:
                    nc.vector.tensor_scalar(b.sc[:], score, clamp, -clamp, ALU.min, ALU.max).then_inc(s.clamped, 1)
                    dve.wait_ge(s.clamped, n + 1)
                    score = b.sc[:]
                nc.vector.tensor_reduce(b.nmax[:, par, :], score, AX.X, ALU.max, negate=True).then_inc(s.max_ready, 1)

            def add(it):
                dve.wait_ge(s.y_done, it + 1)
                tile = k.x[:, ds(it, 1), :].rearrange("p a d -> p (a d)")
                nc.vector.tensor_tensor(tile, tile, k.ps[:, OTB, YT], ALU.add).then_inc(s.y_added, 1)

            def body(it, first, last):
                for j in range(BT):
                    n = it * BT + j
                    par = j % 2
                    final = last and j == BT - 1
                    if not final:
                        take_values(n + 1, 1 - par)
                    if not (last and j >= 2):
                        round_context(n + 2, par, 2 * it + j // 2 + 2)
                    dve.wait_ge(s.turned_done, 2 * n + 2)
                    nc.vector.tensor_copy(b.pt[:, 1, :], k.ps[:, TB[1], 0:ng * P]).then_inc(s.turned_dve, 1)
                    dve.wait_ge(s.probs_ready, n + 1)
                    nc.vector.reciprocal(b.rsum[:, par, :], b.sums[:, par, :]).then_inc(s.rsum_ready, 1)
                    if j == 0 and not first:
                        add(it - 1)
                    if not final:
                        maxima(n + 1, 1 - par)
                    dve.wait_ge(s.rsum_ready, n + 1)
                    dve.wait_ge(s.pv_done, n + 1)
                    for h in range(4):
                        rows = slice(h * S, (h + 1) * S)
                        own = k.ps[rows, OB, 0:inner].rearrange("p (g h d) -> p g h d", h=4, d=hd)[:, :, h, :]
                        o = nc.vector.tensor_tensor(outputs[rows, :, :], own, spread(b.rsum[rows, par, :], hd, 2), ALU.mult)
                    o.then_inc(s.o_ready, 1)

            dve.wait_ge(*w.at)
            nc.vector.tensor_tensor(k.x[:], k.x[:], spread(w.bo, NT, 1), ALU.add).then_inc(s.x_ready, 1)
            take_values(0, 0)
            maxima(0, 0)
            dve.wait_ge(s.x_ready, 1)
            body(0, True, False)
            with dve.Fori(1, NT - 1) as it:
                body(it, False, False)
            body(NT - 1, False, True)
            add(NT - 1)


def self_attention(k, w, qt, kt, v, into, causal=False, relu=False, scale=0.25, more=()):
    nc = k.nc
    sets = [(qt, kt), *more]
    HD, NG, GW = 16, 4, 64
    SB, PB, OB, TB, YB = 0, 1, 2, 4, 5
    names = ("cleared spread_dve spread_pool spread_act vspread_ready scores_done masked max_ready shifted probs_ready "
             "sums_raw sums_ready rsum_ready turned_done turned_ready pv_done o_ready ot_done ot_ready y_done y_added "
             "y_biased")
    with stage(k, names) as (block, s), \
            buffers(k, qx=[P, len(sets), DC, BT, 8, S], vx=[P, NG, BT, GW], sc=[P, NG, BT, S], p=[P, NG, BT, S],
                    m=[P, NG, BT], sums=[P, NG, BT], rsum=[P, NG, BT], pt=[P, NG, P], o=[P, BT, P],
                    ot=[NG * HD, 4, P]) as b:
        spread_by = [s.spread_dve, s.spread_pool, s.spread_act][:len(sets)]

        def score_bank():
            return k.ps[:, SB, :].rearrange("p (u l) -> p u l", l=S)

        def head_rows(m, i, h):
            return (b.qx[:, m, :, :, h, :], sets[m][0][:, :, ds(i * P, P)].rearrange("p c (b q) -> p c b q", b=BT))

        @block.tensor
        def _(pe):
            def scores(i, last_tile=False):
                for done in spread_by:
                    pe.wait_ge(done, i + 1)
                for g in range(NG):
                    c, h0 = g // 2, 4 * (g % 2)
                    for b_ in range(BT):
                        own = (g * BT + b_) * S
                        rest = min(P, BANK - own, (BT - b_) * S if last_tile else P)
                        for m, (_, keys) in enumerate(sets):
                            last = nc.tensor.matmul(k.ps[:, SB, own:own + rest], b.qx[:, m, c, b_, h0:h0 + 4, :],
                                                    keys[:, c, ds(i * P + b_ * S, rest)], start=m == 0,
                                                    stop=m == len(sets) - 1)
                last.then_inc(s.scores_done, 1)

            def output_product(i):
                pe.wait_ge(s.ot_ready, i + 1)
                pe.wait_ge(s.y_added, i + 1)
                for h in range(4):
                    mm = nc.tensor.matmul(k.ps[:, YB, 0:D], b.ot[:, h, :], w.wo[0:NG * HD, h, :],
                                          start=h == 0, stop=h == 3)
                mm.then_inc(s.y_done, 1)

            def body(i, first, last, last_scores=False):
                pe.wait_ge(s.probs_ready, i + 1)
                for g in range(NG):
                    mm = nc.tensor.transpose(k.ps[:, PB, g * P:(g + 1) * P],
                                             b.p[:, g, :, :].rearrange("p b l -> p (b l)"), k.ident)
                mm.then_inc(s.turned_done, 1)
                if not last:
                    scores(i + 1, last_scores)
                pe.wait_ge(s.turned_ready, i + 1)
                pe.wait_ge(s.vspread_ready, i + 1)
                for g in range(NG):
                    mm = nc.tensor.matmul(k.ps[:, OB + g // 2, (g % 2) * 256:(g % 2) * 256 + 256], b.pt[:, g, :],
                                          b.vx[:, g, :, :].rearrange("p b c -> p (b c)"), start=True, stop=True)
                mm.then_inc(s.pv_done, 1)
                if not first:
                    output_product(i - 1)
                pe.wait_ge(s.o_ready, i + 1)
                for b_ in range(BT):
                    mm = nc.tensor.transpose(k.ps[:, TB, b_ * P:(b_ + 1) * P], b.o[:, b_, :], k.ident)
                mm.then_inc(s.ot_done, 1)

            pe.wait_ge(*w.at)
            scores(0)
            body(0, True, False)
            with pe.Fori(1, NT - 2) as i:
                body(i, False, False)
            body(NT - 2, False, False, last_scores=True)
            body(NT - 1, False, True)
            output_product(NT - 1)

        @block.scalar
        def _(act):
            def spread_third(i):
                for h in range(8):
                    out, q = head_rows(2, i, h)
                    last = nc.scalar.mul(out, q, k.head8[:, h:h + 1])
                last.then_inc(s.spread_act, 1)

            def probs(i):
                if relu:
                    act.wait_ge(s.scores_done, i + 1)
                    nc.scalar.activation(b.p[:].rearrange("p g b l -> p (g b) l"), score_bank(), ACT.Relu, scale=scale).then_inc(s.probs_ready, 1)
                else:
                    act.wait_ge(s.shifted, i + 1)
                    nc.scalar.activation(b.p[:], b.sc[:], ACT.Exp, scale=scale).then_inc(s.probs_ready, 1)

            def body(i, last):
                act.wait_ge(s.turned_done, i + 1)
                nc.scalar.copy(b.pt[:], k.ps[:, PB, :].rearrange("p (g c) -> p g c", g=NG)).then_inc(s.turned_ready, 1)
                if not last:
                    act.wait_ge(s.sums_ready, i + 1)
                    probs(i + 1)
                act.wait_ge(s.ot_done, i + 1)
                nc.scalar.copy(b.ot[:].rearrange("p h (b q) -> p h b q", b=BT),
                               k.ps[0:NG * HD, TB, :].rearrange("p (b h q) -> p h b q", b=BT, h=4)).then_inc(s.ot_ready, 1)

            if more:
                act.wait_ge(*w.at)
                spread_third(0)
            probs(0)
            if more:
                spread_third(1)
            with act.Fori(0, NT - 2) as i:
                body(i, False)
                if more:
                    spread_third(i + 2)
            body(NT - 2, False)
            body(NT - 1, True)

        @block.gpsimd
        def _(pool):
            nc.gpsimd.memset(b.o[:], 0.0).then_inc(s.cleared, 1)

            def spread_second(i):
                for c in range(DC):
                    for b_ in range(BT):
                        queries = spread(sets[1][0][:, c, ds(i * P + b_ * S, S)], 8, 1)
                        last = nc.gpsimd.tensor_tensor(b.qx[:, 1, c, b_, :, :], queries, spread(k.head8, S, 2), ALU.mult)
                last.then_inc(s.spread_pool, 1)

            def spread_values(i):
                for g in range(NG):
                    vg = v[:, ds(i, 1), g * GW:(g + 1) * GW].rearrange("p a c -> p (a c)")
                    last = nc.gpsimd.tensor_tensor(b.vx[:, g, :, :], spread(vg, BT, 1), spread(k.seq4, GW, 2), ALU.mult)
                last.then_inc(s.vspread_ready, 1)

            if more:
                spread_second(0)
            spread_values(0)
            if more:
                pool.wait_ge(s.scores_done, 1)
                spread_second(1)
            with pool.Fori(0, NT - 2) as i:
                if more:
                    pool.wait_ge(s.scores_done, i + 2)
                    spread_second(i + 2)
                pool.wait_ge(s.pv_done, i + 1)
                spread_values(i + 1)
            pool.wait_ge(s.pv_done, NT - 1)
            spread_values(NT - 1)

        @block.vector
        def _(dve):
            def spread_first(i):
                for h in range(8):
                    out, q = head_rows(0, i, h)
                    last = nc.vector.tensor_scalar(out, q, k.head8[:, h:h + 1], None, ALU.mult)
                last.then_inc(s.spread_dve, 1)

            def shift(i):
                dve.wait_ge(s.scores_done, i + 1)
                if relu:
                    return
                src = score_bank()
                flat = b.sc[:].rearrange("p g b l -> p (g b) l")
                if causal:
                    nc.vector.tensor_tensor(flat, src, spread(k.causal, NG * BT, 1), ALU.add).then_inc(s.masked, 1)
                    dve.wait_ge(s.masked, i + 1)
                    src = flat
                top = b.m[:].rearrange("p g b -> p (g b)")
                nc.vector.tensor_reduce(top, src, AX.X, ALU.max).then_inc(s.max_ready, 1)
                dve.wait_ge(s.max_ready, i + 1)
                nc.vector.tensor_tensor(flat, src, spread(top, S, 2), ALU.subtract).then_inc(s.shifted, 1)

            def sums(i):
                dve.wait_ge(s.probs_ready, i + 1)
                if relu:
                    nc.vector.tensor_reduce(b.sums[:], b.p[:], AX.X, ALU.add).then_inc(s.sums_raw, 1)
                    dve.wait_ge(s.sums_raw, i + 1)
                    nc.vector.tensor_scalar(b.sums[:], b.sums[:], 1e-6, None, ALU.add).then_inc(s.sums_ready, 1)
                else:
                    nc.vector.tensor_reduce(b.sums[:], b.p[:], AX.X, ALU.add).then_inc(s.sums_ready, 1)
                dve.wait_ge(s.sums_ready, i + 1)
                nc.vector.reciprocal(b.rsum[:], b.sums[:]).then_inc(s.rsum_ready, 1)

            def add(i):
                dve.wait_ge(s.y_done, i + 1)
                tile = into[:, ds(i, 1), :].rearrange("p a d -> p (a d)")
                nc.vector.tensor_tensor(tile, tile, k.ps[:, YB, 0:D], ALU.add).then_inc(s.y_added, 1)

            def body(i, first, last, ahead):
                sums(i)
                if not last:
                    shift(i + 1)
                dve.wait_ge(s.rsum_ready, i + 1)
                dve.wait_ge(s.pv_done, i + 1)
                for h in range(4):
                    rows = slice(h * S, (h + 1) * S)
                    own = k.ps[rows, OB:OB + 2, :].rearrange("p a (g b h d) -> p (a g) b h d", g=2, b=BT, h=4)[:, :, :, h, :]
                    out = b.o[rows, :, 0:NG * HD].rearrange("p b (g d) -> p g b d", g=NG)
                    o = nc.vector.tensor_tensor(out, own, spread(b.rsum[rows, :, :], HD, 3), ALU.mult)
                o.then_inc(s.o_ready, 1)
                if ahead:
                    spread_first(i + 2)
                if not first:
                    add(i - 1)

            spread_first(0)
            dve.wait_ge(*w.at)
            dve.wait_ge(s.cleared, 1)
            dve.sem_inc(s.y_added, 1)
            if w.bo is not None:
                nc.vector.tensor_tensor(into[:], into[:], spread(w.bo, NT, 1), ALU.add).then_inc(s.y_biased, 1)
            shift(0)
            if relu:
                dve.wait_ge(s.scores_done, 1)
            spread_first(1)
            if w.bo is not None:
                dve.wait_ge(s.y_biased, 1)
            body(0, True, False, True)
            with dve.Fori(1, NT - 2) as i:
                body(i, False, False, True)
            body(NT - 2, False, False, False)
            body(NT - 1, False, True, False)
            add(NT - 1)


def phase_features(k, w, qk, ph, amp, sn, cs):
    nc = k.nc
    PI = float(np.float32(np.pi))
    names = ("abs_done exp_done plus_done rest_done ln_done sum_done amp_done square_done mean_done root_done "
             "recip_done norm_done tanh_done fold_done sin_done cos_done lam_tanh lam_done const_done sq_ready q_sin")
    with stage(k, names) as (block, s), \
            buffers(k, f=[P, 2, DC, T], eps=[P, 1], half=[P, 1], lam=[P, 2, DC]) as b:
        @block.vector
        def _(dve):
            nc.vector.memset(b.eps[:], 1e-6).then_inc(s.const_done, 1)
            nc.vector.memset(b.half[:], PI / 2).then_inc(s.const_done, 1)
            for u in range(2):
                nc.vector.scalar_tensor_tensor(amp[:, u], qk[:, u], -1.0, qk[:, u], ALU.mult, ALU.max).then_inc(s.abs_done, 1)
            for u in range(2):
                dve.wait_ge(s.exp_done, u + 1)
                nc.vector.tensor_scalar(b.f[:, u], amp[:, u], 1.0, None, ALU.add).then_inc(s.plus_done, 1)
                dve.wait_ge(s.plus_done, u + 1)
                nc.vector.scalar_tensor_tensor(amp[:, u], b.f[:, u], -1.0, amp[:, u], ALU.add,
                                               ALU.subtract).then_inc(s.rest_done, 1)
            for u in range(2):
                dve.wait_ge(s.ln_done, u + 1)
                nc.vector.scalar_tensor_tensor(b.f[:, u], qk[:, u], 0.0, b.f[:, u], ALU.max, ALU.add).then_inc(s.sum_done, 1)
                dve.wait_ge(s.sum_done, u + 1)
                dve.wait_ge(s.rest_done, u + 1)
                nc.vector.tensor_tensor(amp[:, u], b.f[:, u], amp[:, u], ALU.subtract).then_inc(s.amp_done, 1)
                dve.wait_ge(s.amp_done, u + 1)
                nc.vector.tensor_tensor(b.f[:, u], amp[:, u], amp[:, u], ALU.mult).then_inc(s.square_done, 1)
            dve.wait_ge(s.lam_tanh, 1)
            nc.vector.tensor_scalar(b.lam[:, 1], b.lam[:, 0], 0.5, None, ALU.mult).then_inc(s.lam_done, 1)
            for u in range(2):
                dve.wait_ge(s.root_done, 4 * (u + 1))
                nc.vector.reciprocal(b.f[:, u], b.f[:, u]).then_inc(s.recip_done, 1)
                dve.wait_ge(s.recip_done, u + 1)
                nc.vector.tensor_tensor(amp[:, u], amp[:, u], b.f[:, u], ALU.mult).then_inc(s.norm_done, 1)
            for u in range(2):
                dve.wait_ge(s.tanh_done, u + 1)
                dve.wait_ge(s.norm_done, u + 1)
                nc.vector.scalar_tensor_tensor(b.f[:, u], ph[:, u], -1.0, ph[:, u], ALU.mult, ALU.max).then_inc(s.fold_done, 1)
            dve.wait_ge(s.lam_done, 1)
            for u in range(2):
                for done, t in ((s.sin_done, sn), (s.cos_done, cs)):
                    dve.wait_ge(done, u + 1)
                    if u == 0:
                        for c in range(DC):
                            nc.vector.scalar_tensor_tensor(t[:, u, c], t[:, u, c], b.lam[:, 1, c:c + 1], amp[:, u, c],
                                                           ALU.mult, ALU.mult)
                    else:
                        nc.vector.tensor_tensor(t[:, u], t[:, u], amp[:, u], ALU.mult)

        @block.scalar
        def _(act):
            for u in range(2):
                act.wait_ge(s.abs_done, u + 1)
                nc.scalar.activation(amp[:, u], amp[:, u], ACT.Exp, scale=-1.0).then_inc(s.exp_done, 1)
            for u in range(2):
                act.wait_ge(s.plus_done, u + 1)
                act.wait_ge(s.rest_done, u + 1)
                nc.scalar.activation(b.f[:, u], b.f[:, u], ACT.Ln).then_inc(s.ln_done, 1)
            act.wait_ge(*w.at)
            nc.scalar.activation(b.lam[:, 0], w.lam, ACT.Tanh).then_inc(s.lam_tanh, 1)
            for u in range(2):
                nc.scalar.activation(ph[:, u], ph[:, u], ACT.Tanh).then_inc(s.tanh_done, 1)
            act.wait_ge(s.const_done, 2)
            for u in range(2):
                for q in range(4):
                    act.wait_ge(s.mean_done, 4 * u + q + 1)
                    nc.scalar.activation(b.f[:, u, q // 2, (q % 2) * 512:(q % 2) * 512 + 512], k.ps[:, 4 * u + q, :],
                                         ACT.Sqrt, bias=b.eps[:, 0:1]).then_inc(s.root_done, 1)
            act.wait_ge(s.tanh_done, 2)
            for u in range(2):
                nc.scalar.activation(sn[:, u], ph[:, u], ACT.Sin, scale=PI).then_inc(s.sin_done, 1)
            for u in range(2):
                act.wait_ge(s.fold_done, u + 1)
                nc.scalar.activation(cs[:, u], b.f[:, u], ACT.Sin, bias=b.half[:, 0:1], scale=-PI).then_inc(s.cos_done, 1)

        @block.tensor
        def _(pe):
            for u in range(2):
                pe.wait_ge(s.square_done, u + 1)
                for q in range(4):
                    nc.tensor.matmul(k.ps[:, 4 * u + q, :], k.headmean, b.f[:, u, q // 2, (q % 2) * 512:(q % 2) * 512 + 512],
                                     start=True, stop=True).then_inc(s.mean_done, 1)


def gate(k, w, n_exp, top, kind, comb, comb_t):
    nc = k.nc
    E = n_exp
    CAP = int(1.25 * T * top / E)
    W = NT * E
    down = k.down8 if E == 8 else k.down16
    mm_name = "logits_done step exp_done mask_ready spread_done comb_ready turned"
    with stage(k, mm_name) as (block, s), \
            buffers(k, l=[P, NT, E], r=[P, NT, E], eq=[P, NT, E], pick=[P, NT, E], mask=[P, NT, E], pr=[P, NT, E],
                    m=[P, NT], m1=[P, NT], sm=[P, NT], rs=[P, NT]) as b:

        @block.tensor
        def _(pe):
            pe.wait_ge(*w.at)
            for t in range(NT):
                for c in range(DC):
                    mm = nc.tensor.matmul(k.ps[:, 0, t * E:(t + 1) * E], k.ht[:, c, t * P:(t + 1) * P], w.gate[:, c, :],
                                          start=c == 0, stop=c == DC - 1)
            mm.then_inc(s.logits_done, 1)
            if kind in ("sequence", "capacity"):
                pe.wait_ge(s.mask_ready, 1)
                flat = b.mask[:].rearrange("p t e -> p (t e)")
                if kind == "sequence":
                    mm = nc.tensor.matmul(k.ps[:, 1, 0:W], k.first, flat, start=True, stop=True)
                else:
                    mm = nc.tensor.matmul(k.ps[:, 1, 0:W], k.before, flat, start=True, stop=False)
                    for t in range(NT - 1):
                        mm = nc.tensor.matmul(k.ps[:, 1, (t + 1) * E:W], k.ones, spread(b.mask[:, t, :], NT - 1 - t, 1),
                                              start=False, stop=t == NT - 2)
                mm.then_inc(s.spread_done, 1)
            if comb_t is not None:
                pe.wait_ge(s.comb_ready, 1)
                for t in range(NT):
                    mm = nc.tensor.transpose(k.ps[0:E, 2 + t // 4, (t % 4) * P:(t % 4 + 1) * P], comb[:, t, :], k.ident)
                mm.then_inc(s.turned, 1)

        @block.scalar
        def _(act):
            if kind != "sequence":
                act.wait_ge(s.step, EXP_AT[kind])
                nc.scalar.activation(b.pr[:], b.pr[:], ACT.Exp,
                                     scale=-1.0 if kind == "capacity" else 1.0).then_inc(s.exp_done, 1)
            if comb_t is not None:
                act.wait_ge(s.turned, 1)
                nc.scalar.copy(comb_t[:].rearrange("e (a n) -> e a n", a=2), k.ps[0:E, 2:4, :])

        @block.vector
        def _(dve):
            steps = [0]

            def step(ins):
                steps[0] += 1
                ins.then_inc(s.step, 1)
                dve.wait_ge(s.step, steps[0])

            def over_experts(a):
                return spread(a[:], E, 2)

            dve.wait_ge(*w.at)
            dve.wait_ge(s.logits_done, 1)
            logits = k.ps[:, 0, 0:W].rearrange("p (t e) -> p t e", e=E)
            if w.gb is None:
                step(nc.vector.tensor_copy(b.l[:], logits))
            else:
                step(nc.vector.tensor_tensor(b.l[:], logits, spread(w.gb, NT, 1), ALU.add))
            if kind == "capacity":
                step(nc.vector.tensor_copy(b.pr[:], b.l[:]))
            elif kind != "sequence":
                step(nc.vector.tensor_reduce(b.m1[:], b.l[:], AX.X, ALU.max))
                step(nc.vector.tensor_tensor(b.pr[:], b.l[:], over_experts(b.m1), ALU.subtract))
            step(nc.vector.tensor_copy(b.r[:], b.l[:]))
            for n in range(top):
                step(nc.vector.tensor_reduce(b.m[:], b.r[:], AX.X, ALU.max))
                step(nc.vector.tensor_tensor(b.eq[:], b.r[:], over_experts(b.m), ALU.is_equal))
                step(nc.vector.tensor_tensor(b.eq[:], b.eq[:], spread(down, NT, 1), ALU.mult))
                step(nc.vector.tensor_reduce(b.m[:], b.eq[:], AX.X, ALU.max))
                step(nc.vector.tensor_tensor(b.pick[:], b.eq[:], over_experts(b.m), ALU.is_equal))
                if n == 0:
                    step(nc.vector.tensor_copy(b.mask[:], b.pick[:]))
                else:
                    step(nc.vector.tensor_tensor(b.mask[:], b.mask[:], b.pick[:], ALU.add))
                if n < top - 1:
                    step(nc.vector.scalar_tensor_tensor(b.r[:], b.pick[:], NEG, b.r[:], ALU.mult, ALU.add))
            if kind == "sequence":
                dve.sem_inc(s.mask_ready, 1)
                dve.wait_ge(s.spread_done, 1)
                chosen = k.ps[:, 1, 0:W].rearrange("p (t e) -> p t e", e=E)
                nc.vector.tensor_scalar(comb[:], chosen, 1.0 / top, None, ALU.mult).then_inc(s.comb_ready, 1)
                return
            dve.wait_ge(s.exp_done, 1)
            if kind == "capacity":
                dve.sem_inc(s.mask_ready, 1)
                step(nc.vector.tensor_scalar(b.pr[:], b.pr[:], 1.0, None, ALU.add))
                step(nc.vector.reciprocal(b.pr[:], b.pr[:]))
            if kind == "masked":
                step(nc.vector.tensor_reduce(b.sm[:], b.pr[:], AX.X, ALU.add))
                step(nc.vector.reciprocal(b.rs[:], b.sm[:]))
                step(nc.vector.tensor_tensor(b.pr[:], b.pr[:], over_experts(b.rs), ALU.mult))
            step(nc.vector.tensor_tensor(b.pr[:], b.pr[:], b.mask[:], ALU.mult))
            step(nc.vector.tensor_reduce(b.sm[:], b.pr[:], AX.X, ALU.add))
            if kind == "masked":
                step(nc.vector.tensor_scalar(b.sm[:], b.sm[:], 1e-12, None, ALU.max))
            if kind == "capacity":
                step(nc.vector.tensor_scalar(b.sm[:], b.sm[:], 1e-6, None, ALU.add))
            step(nc.vector.reciprocal(b.rs[:], b.sm[:]))
            if kind == "capacity":
                step(nc.vector.tensor_tensor(b.pr[:], b.pr[:], over_experts(b.rs), ALU.mult))
                dve.wait_ge(s.spread_done, 1)
                ranks = k.ps[:, 1, 0:W].rearrange("p (t e) -> p t e", e=E)
                step(nc.vector.tensor_scalar(b.eq[:], ranks, float(CAP), None, ALU.is_lt))
                nc.vector.tensor_tensor(comb[:], b.pr[:], b.eq[:], ALU.mult).then_inc(s.comb_ready, 1)
            else:
                nc.vector.tensor_tensor(comb[:], b.pr[:], over_experts(b.rs), ALU.mult).then_inc(s.comb_ready, 1)


EXP_AT = {"softmax": 3, "masked": 3, "capacity": 2}


def ffn(k, w, n_exp, hid, w1, w2, func, comb, comb_t, into, b1=None, row_bias=None, also=None):
    nc = k.nc
    HC = hid // P
    RING = 4
    UNITS = min(4, 2 * n_exp)
    TURNS = max(1, n_exp // 2)
    names = ("raw1_loaded raw2_loaded w1_hi w1_split w2_hi w2_split x_hi x_split h_done g_ready g_hi g_split y_done "
             "y_free bias_done bias_added bias_placed also_added")
    with stage(k, names) as (block, s), \
            buffers(k, raw1=[P, DC, hid], raw2=[P, HC, D], g=[P, RING, 512], bias=[P, 2, HC]) as b, \
            buffers(k, F32R, x=[P, 2, DC, T], w1=[P, 2, 2, DC, hid], w2=[P, 2, 2, HC, D], g=[P, 2, RING, 512]) as r:
        HI, LO = 0, 1
        TERMS = ((HI, HI), (HI, LO), (LO, HI))

        def chunk(it, j, h):
            return (4 * it + j) * HC + h

        def slot(j, h):
            return (j * HC + h) % RING

        def ahead(it, j, h, n):
            at = j * HC + h + n
            return it + at // (4 * HC), at // HC % 4, at % HC

        @block.sync
        def _(sp):
            def load(e):
                sp.dma_start(b.raw1[:], w1[ds(e, 1)].rearrange("a p c n -> (a p) c n")).then_inc(s.raw1_loaded, 16)
                sp.dma_start(b.raw2[:], w2[ds(e, 1)].rearrange("a p c n -> (a p) c n")).then_inc(s.raw2_loaded, 16)

            load(0)
            fetch_weights(k, sp)
            if n_exp > 1:
                with sp.Fori(0, n_exp - 1) as e:
                    sp.wait_ge(s.w1_split, e + 1)
                    sp.wait_ge(s.w2_split, e + 1)
                    load(e + 1)

        @block.tensor
        def _(pe):
            def hidden(it, j, h):
                if h == 0 and j % 2 == 0:
                    pe.wait_ge(s.w1_split, 2 * it + j // 2 + 1)
                pe.wait_ge(s.g_ready, chunk(it, j, h) + 1)
                for t, (p1, p2) in enumerate(TERMS):
                    for c in range(DC):
                        mm = nc.tensor.matmul(k.ps[:, slot(j, h), :], r.w1[:, j // 2, p1, c, h * P:(h + 1) * P],
                                              r.x[:, p2, c, (j % 2) * 512:(j % 2 + 1) * 512],
                                              start=t == 0 and c == 0, stop=t == 2 and c == DC - 1)
                mm.then_inc(s.h_done, 1)

            def outputs(it, j, h):
                if h == 0 and j % 2 == 0:
                    pe.wait_ge(s.w2_split, 2 * it + j // 2 + 1)
                pe.wait_ge(s.g_split, chunk(it, j, h) + 1 + RING)
                for t in range(4):
                    if h == 0:
                        pe.wait_ge(s.y_free, 4 * (4 * it + j) + t + 1)
                    for i, (p1, p2) in enumerate(TERMS):
                        mm = nc.tensor.matmul(k.ps[:, 4 + t, 0:D], r.g[:, p1, slot(j, h), t * P:(t + 1) * P],
                                              r.w2[:, j // 2, p2, h, :], start=h == 0 and i == 0,
                                              stop=h == HC - 1 and i == 2)
                    if h == HC - 1:
                        mm.then_inc(s.y_done, 1)

            def body(it, last):
                for j in range(UNITS):
                    for h in range(HC):
                        if not (last and j * HC + h + 2 >= UNITS * HC):
                            hidden(*ahead(it, j, h, 2))
                        outputs(it, j, h)

            if comb_t is not None:
                for t in range(NT):
                    mm = nc.tensor.matmul(k.ps[:, 4 + t // 2, (t % 2) * D:(t % 2 + 1) * D], comb_t[:, t * P:(t + 1) * P],
                                          w.b2[0:n_exp, :], start=True, stop=True)
                mm.then_inc(s.bias_done, 1)
            pe.wait_ge(s.x_split, 1)
            hidden(0, 0, 0)
            hidden(0, 0, 1)
            if TURNS > 1:
                with pe.Fori(0, TURNS - 1) as it:
                    body(it, False)
            body(TURNS - 1, True)

        @block.scalar
        def _(act):
            def round_w1(e, par):
                act.wait_ge(s.raw1_loaded, 16 * (e + 1))
                nc.scalar.copy(r.w1[:, par, HI], b.raw1[:]).then_inc(s.w1_hi, 1)

            def round_w2(e, par):
                act.wait_ge(s.raw2_loaded, 16 * (e + 1))
                nc.scalar.copy(r.w2[:, par, HI], b.raw2[:]).then_inc(s.w2_hi, 1)

            def values(it, j, h):
                if b1 is not None and h == 0 and j % 2 == 0:
                    e = 2 * it + j // 2
                    nc.scalar.copy(b.bias[:, j // 2, :], b1[:, ds(e * HC, HC)]).then_inc(s.bias_placed, 1)
                    act.wait_ge(s.bias_placed, e + 1)
                act.wait_ge(s.g_split, chunk(it, j, h) + 1)
                act.wait_ge(s.h_done, chunk(it, j, h) + 1)
                out, inp = b.g[:, slot(j, h), :], k.ps[:, slot(j, h), :]
                if b1 is None:
                    nc.scalar.activation(out, inp, func).then_inc(s.g_ready, 1)
                else:
                    nc.scalar.activation(out, inp, func, bias=b.bias[:, j // 2, h:h + 1]).then_inc(s.g_ready, 1)

            def body(it, last):
                for j in range(UNITS):
                    for h in range(HC):
                        values(it, j, h)
                        more = not (last and j // 2 == (UNITS - 1) // 2)
                        if more and (j % 2) * HC + h == 1:
                            round_w1(2 * it + j // 2 + 1, 1 - j // 2)
                        if more and (j % 2) * HC + h == 2:
                            round_w2(2 * it + j // 2 + 1, 1 - j // 2)

            act.sem_inc(s.g_ready, RING)
            nc.scalar.copy(r.x[:, HI], k.ht[:]).then_inc(s.x_hi, 1)
            round_w1(0, 0)
            round_w2(0, 0)
            if b1 is not None:
                act.wait_ge(*w.at)
            if TURNS > 1:
                with act.Fori(0, TURNS - 1) as it:
                    body(it, False)
            body(TURNS - 1, True)

        @block.gpsimd
        def _(pool):
            def rest_w1(e, par):
                pool.wait_ge(s.w1_hi, e + 1)
                nc.gpsimd.tensor_tensor(r.w1[:, par, LO], b.raw1[:], r.w1[:, par, HI], ALU.subtract).then_inc(s.w1_split, 1)

            def rest_w2(e, par):
                pool.wait_ge(s.w2_hi, e + 1)
                nc.gpsimd.tensor_tensor(r.w2[:, par, LO], b.raw2[:], r.w2[:, par, HI], ALU.subtract).then_inc(s.w2_split, 1)

            rest_w2(0, 0)
            if n_exp > 1:
                if TURNS > 1:
                    with pool.Fori(0, TURNS - 1) as it:
                        for e, par in ((2 * it + 1, 1), (2 * it + 2, 0)):
                            rest_w1(e, par)
                            rest_w2(e, par)
                rest_w1(n_exp - 1, 1)
                rest_w2(n_exp - 1, 1)

        @block.vector
        def _(dve):
            def split(it, j, h):
                g, hi, lo = b.g[:, slot(j, h), :], r.g[:, HI, slot(j, h), :], r.g[:, LO, slot(j, h), :]
                dve.wait_ge(s.g_ready, chunk(it, j, h) + 1 + RING)
                nc.vector.tensor_copy(hi, g).then_inc(s.g_hi, 1)
                dve.wait_ge(s.g_hi, chunk(it, j, h) + 1)
                nc.vector.tensor_tensor(lo, g, hi, ALU.subtract).then_inc(s.g_split, 1)

            def add(it, j):
                half = j % 2
                for t in range(4):
                    dve.wait_ge(s.y_done, 4 * (4 * it + j) + t + 1)
                    tile = into[:, half * 4 + t, :]
                    if comb is None:
                        nc.vector.tensor_tensor(tile, tile, k.ps[:, 4 + t, 0:D], ALU.add).then_inc(s.y_free, 1)
                    else:
                        share = comb[:, half * 4 + t, ds(2 * it + j // 2, 1)]
                        nc.vector.scalar_tensor_tensor(tile, k.ps[:, 4 + t, 0:D], share, tile, ALU.mult,
                                                       ALU.add).then_inc(s.y_free, 1)

            def body(it, last):
                for j in range(UNITS):
                    for h in range(1, HC):
                        split(it, j, h)
                    if not (last and j == UNITS - 1):
                        split(*ahead(it, j, 0, HC))
                    add(it, j)

            dve.sem_inc(s.g_split, RING)
            dve.wait_ge(s.x_hi, 1)
            nc.vector.tensor_tensor(r.x[:, LO], k.ht[:], r.x[:, HI], ALU.subtract).then_inc(s.x_split, 1)
            dve.wait_ge(s.w1_hi, 1)
            nc.vector.tensor_tensor(r.w1[:, 0, LO], b.raw1[:], r.w1[:, 0, HI], ALU.subtract).then_inc(s.w1_split, 1)
            if comb_t is not None:
                dve.wait_ge(s.bias_done, 1)
                nc.vector.tensor_tensor(into[:], into[:], k.ps[:, 4:8, :].rearrange("p a (t d) -> p (a t) d", d=D),
                                        ALU.add).then_inc(s.bias_added, 1)
                dve.wait_ge(s.bias_added, 1)
            if also is not None:
                nc.vector.tensor_tensor(into[:], into[:], also[:], ALU.add).then_inc(s.also_added, 1)
                dve.wait_ge(s.also_added, 1)
            if row_bias is not None:
                dve.wait_ge(*w.at)
                nc.vector.tensor_tensor(into[:], into[:], spread(row_bias, NT, 1), ALU.add).then_inc(s.bias_added, 1)
                dve.wait_ge(s.bias_added, 1)
            dve.sem_inc(s.y_free, 4)
            split(0, 0, 0)
            if TURNS > 1:
                with dve.Fori(0, TURNS - 1) as it:
                    body(it, False)
            body(TURNS - 1, True)


def clear(k, view):
    nc = k.nc
    with stage(k, "cleared") as (block, s):
        @block.gpsimd
        def _(pool):
            for c in range(view.shape[1]):
                nc.gpsimd.memset(view[:, c], 0.0).then_inc(s.cleared, 1)


def convolve(k, w, hp, ct):
    nc = k.nc
    taps = w.conv.shape[2]
    with stage(k, "conv_done") as (block, s):
        @block.tensor
        def _(pe):
            pe.wait_ge(*w.at)
            for m in range(DC):
                for half in range(2):
                    for j in range(taps):
                        mm = nc.tensor.matmul(k.ps[:, 2 * m + half, :], w.conv[:, m, j, :],
                                              hp[:, m, half * 16:(half + 1) * 16, j:j + S], start=j == 0, stop=j == taps - 1)
                    mm.then_inc(s.conv_done, 1)

        @block.scalar
        def _(act):
            for q in (0, 2):
                act.wait_ge(s.conv_done, q + 1)
                nc.scalar.activation(ct[:, q // 2, 0:512], k.ps[:, q, :], ACT.Identity, bias=w.cb[:, q // 2:q // 2 + 1])

        @block.vector
        def _(dve):
            for q in (1, 3):
                dve.wait_ge(s.conv_done, q + 1)
                nc.vector.tensor_scalar(ct[:, q // 2, 512:1024], k.ps[:, q, :], w.cb[:, q // 2:q // 2 + 1], None, ALU.add)


def pool_keys(k, q, key, v):
    nc = k.nc
    names = "q_sums q_means q_keys k_sums k_means"
    with stage(k, names) as (block, s), buffers(k, acc=[P, DC, T]) as b:
        @block.vector
        def _(dve):
            for c in range(DC):
                nc.vector.tensor_tensor_scan(b.acc[:, c, :], k.keep, q[:, c, :], 0.0, ALU.mult, ALU.add).then_inc(s.q_sums, 1)
            for c in range(DC):
                dve.wait_ge(s.q_sums, c + 1)
                nc.vector.tensor_tensor(q[:, c, :], b.acc[:, c, :], k.rcount, ALU.mult).then_inc(s.q_means, 1)
            for c in range(DC):
                dve.wait_ge(s.q_means, c + 1)
                nc.vector.tensor_tensor(key[:, c, :], q[:, c, :], key[:, c, :], ALU.mult).then_inc(s.q_keys, 1)
            for c in range(DC):
                dve.wait_ge(s.q_keys, c + 1)
                nc.vector.tensor_tensor_scan(b.acc[:, c, :], k.keep, key[:, c, :], 0.0, ALU.mult, ALU.add).then_inc(s.k_sums, 1)
            for c in range(DC):
                dve.wait_ge(s.k_sums, c + 1)
                nc.vector.tensor_tensor(key[:, c, :], b.acc[:, c, :], k.rcount, ALU.mult).then_inc(s.k_means, 1)
            for c in range(DC):
                dve.wait_ge(s.k_means, c + 1)
                nc.vector.tensor_tensor(v[:, c, :], key[:, c, :], v[:, c, :], ALU.mult)


def wide_cross_attention(k, w, qt):
    nc = k.nc
    SB, PB, OB = 6, 7, 4
    names = ("w_hi w_split ctx_hi ctx_low ctx_split tail_loaded tail_done tail_ready tail_placed ctx_loaded0 ctx_loaded1 ctx_loaded2 ctx_loaded3 keys_done "
             "keys_ready values_done values_ready q_placed scores_done max_ready probs_ready tail_spread turned_done "
             "turned_ready rsum_ready o_done x_ready")
    with stage(k, names) as (block, s), \
            buffers(k, c=[P, BT, 2, LP], t0=[P, B], t1=[DK - P, B], vtail=[B, D], vt=[BT, NT, D],
                    key=[P, BT, DC, LK], val=[P, BT, 2, D], q=[P, DC, P], p=[P, LK], pb=[P, BT], nmax=[P, 1],
                    sums=[P, 1], rsum=[P, 1], pt=[P, 2, P], ptt=[BT, P]) as b, \
            buffers(k, F32R, w=[P, 2, 2, 2 * D], c=[P, BT, 2, LP], clo=[P, BT, LP]) as r:
        ctx_loaded = [s.ctx_loaded0, s.ctx_loaded1, s.ctx_loaded2, s.ctx_loaded3]

        def factors(j, at, rows):
            whi, wlo = r.w[:, 0, :, at], r.w[:, 1, :, at]
            return ((whi[:, 0], r.c[:, j, 0, rows]), (whi[:, 0], r.clo[:, j, rows]), (wlo[:, 0], r.c[:, j, 0, rows]),
                    (whi[:, 1], r.c[:, j, 1, rows]), (wlo[0:DK - P, 1], r.c[0:DK - P, j, 1, rows]))

        @block.sync
        def _(sp):
            sp.dma_start(b.t0[:], k.ctx_t0).then_inc(s.tail_loaded, 16)
            sp.dma_start(b.t1[:], k.ctx_t1).then_inc(s.tail_loaded, 16)

            def load(i, j):
                n = i * BT + j
                sp.dma_start(b.c[:, j], k.ctx[ds(n, 1)].rearrange("a p c l -> (a p) c l")).then_inc(ctx_loaded[j], 16)

            for j in range(BT):
                load(0, j)
            sp.wait_ge(s.tail_ready, 1)
            for j in range(BT):
                sp.dma_start(b.vt[j:j + 1, :, :], b.vtail[j:B:BT, :]).then_inc(s.tail_placed, 16)
            with sp.Fori(0, NT - 1) as i:
                for j in range(BT):
                    sp.wait_ge(s.ctx_low, i * BT + j + 1)
                    sp.wait_ge(s.ctx_split, i * BT + j + 1)
                    load(i + 1, j)

        @block.gpsimd
        def _(pool):
            def place(i):
                nc.gpsimd.tensor_copy(b.q[:], qt[:, :, ds(i * P, P)]).then_inc(s.q_placed, 1)

            def split_context(i):
                for j in range(BT):
                    pool.wait_ge(s.ctx_hi, i * BT + j + 1)
                    nc.gpsimd.tensor_tensor(r.clo[:, j, :], b.c[:, j, 0, :], r.c[:, j, 0, :],
                                            ALU.subtract).then_inc(s.ctx_split, 1)

            split_context(0)
            place(0)
            with pool.Fori(0, NT - 1) as i:
                split_context(i + 1)
                pool.wait_ge(s.scores_done, i + 1)
                place(i + 1)

        @block.tensor
        def _(pe):
            pe.wait_ge(*w.at)
            pe.wait_ge(s.tail_loaded, 32)
            for c, t, kr in ((0, b.t0, P), (1, b.t1, DK - P)):
                mm = nc.tensor.matmul(k.ps[0:B, 7, 0:D], t[:], w.wv[0:kr, c, :], start=c == 0, stop=c == 1)
            mm.then_inc(s.tail_done, 1)
            pe.wait_ge(s.w_split, 2)

            def keys(i, first=False):
                for j in range(BT):
                    pe.wait_ge(s.ctx_low, i * BT + j + 1)
                    pe.wait_ge(s.ctx_split, i * BT + j + 1)
                    if not (first and j < 2):
                        pe.wait_ge(s.keys_ready, i * BT + j - 1)
                    for m in range(DC):
                        for t, (wp, cp) in enumerate(factors(j, slice(m * P, (m + 1) * P), slice(0, LP))):
                            mm = nc.tensor.matmul(k.ps[:, 2 * (j % 2) + m, 0:LP], wp, cp, start=t == 0, stop=t == 4)
                    mm.then_inc(s.keys_done, 1)

            def values(i, first=False):
                for j in range(BT):
                    if not (first and j < 2):
                        pe.wait_ge(s.values_ready, i * BT + j - 1)
                    if j == 1 and not first:
                        pe.wait_ge(s.x_ready, i)
                    bank = 5 - j % 2
                    for half in range(2):
                        for t, (wp, cp) in enumerate(factors(j, slice(D, 2 * D), slice(half * P, (half + 1) * P))):
                            mm = nc.tensor.matmul(k.ps[:, bank, half * D:(half + 1) * D], cp, wp, start=t == 0, stop=t == 4)
                    mm.then_inc(s.values_done, 1)

            def body(i, last):
                pe.wait_ge(s.keys_ready, (i + 1) * BT)
                pe.wait_ge(s.q_placed, i + 1)
                for j in range(BT):
                    for c in range(DC):
                        mm = nc.tensor.matmul(k.ps[j * S:(j + 1) * S, SB, 0:LK], b.q[:, c, j * S:(j + 1) * S],
                                              b.key[:, j, c, :], start=c == 0, stop=c == DC - 1)
                mm.then_inc(s.scores_done, 1)
                if not last:
                    keys(i + 1)
                pe.wait_ge(s.tail_spread, i + 1)
                for half in range(2):
                    nc.tensor.transpose(k.ps[:, PB, half * P:(half + 1) * P], b.p[:, half * P:(half + 1) * P], k.ident)
                nc.tensor.transpose(k.ps[0:BT, PB, 2 * P:3 * P], b.pb[:], k.ident).then_inc(s.turned_done, 1)
                pe.wait_ge(s.turned_ready, i + 1)
                pe.wait_ge(s.values_ready, (i + 1) * BT)
                nc.tensor.matmul(k.ps[:, OB, 0:D], b.ptt[:], b.vt[:, ds(i, 1), :].rearrange("g a c -> g (a c)"),
                                 start=True, stop=False, skip_group_check=True)
                for j in range(BT):
                    for half in range(2):
                        mm = nc.tensor.matmul(k.ps[j * S:(j + 1) * S, OB, 0:D], b.pt[:, half, j * S:(j + 1) * S],
                                              b.val[:, j, half, :], start=False, stop=half == 1, skip_group_check=True)
                mm.then_inc(s.o_done, 1)
                if not last:
                    values(i + 1)

            pe.wait_ge(s.tail_ready, 1)
            keys(0, first=True)
            values(0, first=True)
            pe.wait_ge(s.tail_placed, 16 * BT)
            with pe.Fori(0, NT - 1) as i:
                body(i, False)
            body(NT - 1, True)

        @block.scalar
        def _(act):
            act.wait_ge(*w.at)

            def take_keys(i):
                for j in range(BT):
                    act.wait_ge(s.keys_done, i * BT + j + 1)
                    for m in range(DC):
                        last = nc.scalar.activation(b.key[:, j, m, :], k.ps[:, 2 * (j % 2) + m, 0:LK], ACT.Identity,
                                                    bias=w.bk[:, m:m + 1])
                    last.then_inc(s.keys_ready, 1)

            def body(i, last):
                act.wait_ge(s.max_ready, i + 1)
                nc.scalar.activation(b.p[:], k.ps[:, SB, 0:LK], ACT.Exp, bias=b.nmax[:, 0:1],
                                     accum_out=b.sums[:, 0:1]).then_inc(s.probs_ready, 1)
                if not last:
                    take_keys(i + 1)

            for u, part in ((0, w.wk), (1, w.wv)):
                nc.scalar.copy(r.w[:, 0, :, u * D:(u + 1) * D], part).then_inc(s.w_hi, 1)
            take_keys(0)
            with act.Fori(0, NT - 1) as i:
                body(i, False)
            body(NT - 1, True)

        @block.vector
        def _(dve):
            def round_context(i):
                for j in range(BT):
                    dve.wait_ge(ctx_loaded[j], 16 * (i + 1))
                    nc.vector.tensor_copy(r.c[:, j], b.c[:, j]).then_inc(s.ctx_hi, 1)
                    dve.wait_ge(s.ctx_hi, i * BT + j + 1)
                    low = slice(DK - P, P)
                    nc.vector.tensor_tensor(r.c[low, j, 1, :], b.c[low, j, 1, :], r.c[low, j, 1, :],
                                            ALU.subtract).then_inc(s.ctx_low, 1)

            round_context(0)
            dve.wait_ge(*w.at)
            for u, part in ((0, w.wk), (1, w.wv)):
                at = slice(u * D, (u + 1) * D)
                dve.wait_ge(s.w_hi, u + 1)
                nc.vector.tensor_tensor(r.w[:, 1, :, at], part, r.w[:, 0, :, at], ALU.subtract).then_inc(s.w_split, 1)
            dve.wait_ge(s.tail_done, 1)
            nc.vector.tensor_tensor(b.vtail[:], k.ps[0:B, 7, 0:D], w.bv[0:B, :], ALU.add).then_inc(s.tail_ready, 1)

            def take_values(i):
                for j in range(BT):
                    dve.wait_ge(s.values_done, i * BT + j + 1)
                    nc.vector.tensor_tensor(b.val[:, j, :, :], k.ps[:, 5 - j % 2, :].rearrange("p (r c) -> p r c", r=2),
                                            spread(w.bv, 2, 1), ALU.add).then_inc(s.values_ready, 1)

            def body(i, last):
                if not last:
                    round_context(i + 1)
                dve.wait_ge(s.scores_done, i + 1)
                nc.vector.tensor_reduce(b.nmax[:], k.ps[:, SB, 0:LK], AX.X, ALU.max, negate=True).then_inc(s.max_ready, 1)
                dve.wait_ge(s.probs_ready, i + 1)
                nc.vector.tensor_scalar(b.pb[:], k.seq4, b.p[:, 2 * P:LK], None, ALU.mult).then_inc(s.tail_spread, 1)
                nc.vector.reciprocal(b.rsum[:], b.sums[:]).then_inc(s.rsum_ready, 1)
                dve.wait_ge(s.turned_done, i + 1)
                nc.vector.tensor_copy(b.pt[:], k.ps[:, PB, 0:2 * P].rearrange("p (r c) -> p r c", r=2))
                nc.vector.tensor_copy(b.ptt[:], k.ps[0:BT, PB, 2 * P:3 * P]).then_inc(s.turned_ready, 1)
                dve.wait_ge(s.rsum_ready, i + 1)
                dve.wait_ge(s.o_done, i + 1)
                tile = k.x[:, ds(i, 1), :].rearrange("p a d -> p (a d)")
                nc.vector.scalar_tensor_tensor(tile, k.ps[:, OB, 0:D], b.rsum[:, 0:1], tile, ALU.mult,
                                               ALU.add).then_inc(s.x_ready, 1)
                if not last:
                    take_values(i + 1)

            take_values(0)
            with dve.Fori(0, NT - 1) as i:
                body(i, False)
            body(NT - 1, True)


def build(nc, args, packed, fields, order):
    k = Core()
    k.nc, k.stages, k.buffers = nc, 0, 0
    k.packed, k.fields, k.order = packed, fields, order
    k.in_x, k.out = args["x"], args["out_0"]
    k.in_const = args["const"]
    k.ctx, k.ctx_t0, k.ctx_t1 = (args[n] for n in ("ctx", "ctx_t0", "ctx_t1"))
    k.args = args
    with ExitStack() as ctx:
        def sb(name, *shape):
            return ctx.enter_context(nc.sbuf_tensor(f"{name}_sb", list(shape), F32))

        k.x = sb("x", P, NT, D)
        k.z = sb("z", P, NT, D)
        k.ht = sb("ht", P, DC, T)
        k.store = sb("store", P, 2, max(int(a.shape[1]) for a in packed.values()))
        k.consts = sb("consts", P, int(k.in_const.shape[1]))
        made, at = constants(), 0
        for name, a in made.items():
            made[name] = k.consts[:, at:at + a.shape[1]]
            at += a.shape[1]
        k.ident, k.head8, k.seq4, k.causal, k.headmean, k.first = (
            made[n] for n in ("ident", "head8", "seq4", "causal", "headmean", "first"))
        k.before, k.ones, k.down8, k.down16, k.keep, k.rcount = (
            made[n] for n in ("before", "ones", "down8", "down16", "keep", "rcount"))
        k.half4 = made["half4"].rearrange("p (c h) -> p c h", c=2)
        k.ps = ctx.enter_context(nc.psum_tensor("ps", [P, 8, BANK], F32))
        k.weights_loaded = [ctx.enter_context(nc.semaphore(f"weights_loaded{h}")) for h in range(2)]
        k.stored = ctx.enter_context(nc.semaphore("stored"))
        k.fetched, k.fetch_to = 0, 2
        load_inputs(k)

        def begin(name):
            k.fetch_to = order.index(name) + 2
            return weights(k, name)

        for name in order:
            w = begin(name)
            if name in ("L0_xattn", "L1_xattn", "L2_xattn"):
                heads, hd = (8, 64) if name == "L2_xattn" else (16, 16)
                with buffers(k, qt=[P, heads * hd // P, T]) as b:
                    normalize(k, k.x, k.z)
                    transpose_tokens(k, k.z, k.ht)
                    project(k, k.ht, [(b.qt, w.wq, w.bq, 0.25 if hd == 16 else 0.125)], w.at)
                    cross_attention(k, w, b.qt, heads, hd, clamp=1.0e4 if name == "L1_xattn" else None)
            if name in ("L1_attn", "L3_attn", "L3_gqa"):
                with buffers(k, qt=[P, DC, T], kt=[P, DC, T], v=[P, NT, D]) as b:
                    normalize(k, k.x, k.z)
                    transpose_tokens(k, k.z, k.ht)
                    project(k, k.ht, [(b.qt, w.wq, w.bq, 1.0), (b.kt, w.wk, w.bk, 1.0)], w.at, [(b.v, w.wv, w.bv)])
                    self_attention(k, w, b.qt, b.kt, b.v, k.x if name == "L3_attn" else k.z,
                                   causal=name == "L3_attn", relu=name == "L1_attn")
                if name == "L1_attn":
                    normalize(k, k.z, k.z, gain=w.gamma, shift=w.beta, w_at=w.at, add=k.x)
            if name == "L0_attn":
                with buffers(k, qk=[P, 2, DC, T], v=[P, NT, D], sn=[P, 2, DC, T], cs=[P, 2, DC, T]) as b:
                    normalize(k, k.x, k.z)
                    transpose_tokens(k, k.z, k.ht)
                    with buffers(k, ph=[P, 2, DC, T], amp=[P, 2, DC, T]) as f:
                        project(k, k.ht, [(b.qk[:, 0], w.wq, None, 1.0), (b.qk[:, 1], w.wk, None, 1.0),
                                          (f.ph[:, 0], w.wqp, None, 1.0), (f.ph[:, 1], w.wkp, None, 1.0)], w.at,
                                [(b.v, w.wv, None)])
                        phase_features(k, w, b.qk, f.ph, f.amp, b.sn, b.cs)
                    self_attention(k, w, b.qk[:, 0], b.qk[:, 1], b.v, k.x, causal=True,
                                   more=[(b.sn[:, 0], b.sn[:, 1]), (b.cs[:, 0], b.cs[:, 1])])
            if name in ("L0_ffn", "L1_ffn", "L2_ffn", "L3_ffn"):
                n_exp, hid, top, kind, func = {
                    "L0_ffn": (8, 1024, 2, "softmax", ACT.Gelu), "L1_ffn": (16, 512, 3, "masked", ACT.Relu),
                    "L2_ffn": (8, 256, 2, "sequence", ACT.Gelu), "L3_ffn": (8, 512, 2, "capacity", ACT.Gelu)}[name]
                biased = name != "L3_ffn"
                if biased:
                    normalize(k, k.x, k.z)
                else:
                    normalize(k, k.z, k.z, rms=True, gain=gains[0], eps=1e-6, w_at=gains[2])
                transpose_tokens(k, k.z, k.ht)
                with ExitStack() as c2:
                    b = c2.enter_context(buffers(k, comb=[P, NT, n_exp]))
                    comb_t = c2.enter_context(buffers(k, t=[n_exp, T])).t if biased else None
                    gate(k, w, n_exp, top, kind, b.comb, comb_t)
                    ffn(k, w, n_exp, hid, args[f"{name}_w1"], args[f"{name}_w2"], func, b.comb, comb_t,
                        k.x if biased else k.z, b1=w.b1.rearrange("p e h -> p (e h)") if biased else None)
                if not biased:
                    normalize(k, k.z, k.z, rms=True, gain=gains[1], eps=1e-6, add=k.x)
            if name == "L3_gqa":
                gains = (w.gamma, w.gamma2, w.at)
            if name == "L3_xattn":
                with buffers(k, qt=[P, DC, T]) as b:
                    normalize(k, k.x, k.z)
                    transpose_tokens(k, k.z, k.ht)
                    project(k, k.ht, [(b.qt, w.wq, w.bq, 1.0 / 16)], w.at)
                    wide_cross_attention(k, w, b.qt)
            if name == "L2_attn":
                pad = w.conv.shape[2] - 1
                with buffers(k, hn=[P, NT, D]) as b:
                    normalize(k, k.x, k.z)
                    normalize(k, k.z, b.hn)
                    with buffers(k, hp=[P, DC, B, S + pad], ct=[P, DC, T]) as f:
                        clear(k, f.hp[:, :, :, 0:pad])
                        transpose_tokens(k, b.hn, None, w.g1, w.b1, padded=f.hp[:, :, :, pad:], w_at=w.at)
                        convolve(k, w, f.hp, f.ct)
                        transpose_channels(k, f.ct, k.z, k.z)
                    normalize(k, k.z, b.hn)
                    transpose_tokens(k, b.hn, k.ht, w.g2, w.b2, w_at=w.at)
                    with buffers(k, q=[P, DC, T], key=[P, DC, T], v=[P, DC, T]) as f:
                        project(k, k.ht, [(f.q, w.wq, w.bq, 1.0), (f.key, w.wk, w.bk, 1.0), (f.v, w.wv, w.bv, 1.0)], w.at)
                        pool_keys(k, f.q, f.key, f.v)
                        transpose_channels(k, f.v, k.z, k.z)
                    normalize(k, k.z, b.hn)
                    transpose_tokens(k, b.hn, k.ht, w.g3, w.b3, w_at=w.at)
            if name == "L2_boom":
                ffn(k, w, 1, 1024, args["L2_boom_w1"], args["L2_boom_w2"], ACT.Gelu, None, None, k.x,
                    b1=w.b1, row_bias=w.bo, also=k.z)
        store_output(k)


def unlay(y):
    return np.ascontiguousarray(y.transpose(1, 0, 2)).reshape(B, S, D)


def kernel(**inputs):
    import concourse.bacc as _bacc
    from concourse.bass_utils import run_bass_kernel_spmd as _run

    nc = _bacc.Bacc("TRN2", target_bir_lowering=False, num_devices=1)
    i = {n: np.asarray(a) for n, a in inputs.items()}
    arrays = {"x": i["x"].reshape(NT, P, D).transpose(1, 0, 2)}
    ctx = np.zeros((B, DK, LP), np.float32)
    ctx[:, :, 0:LK] = i["ctx_768"].transpose(0, 2, 1)
    arrays["ctx"] = np.stack([ctx[:, 0:P, :], np.concatenate([ctx[:, P:DK, :]] * 2, axis=1)], axis=2)
    arrays["ctx_t0"], arrays["ctx_t1"] = ctx[:, 0:P, LK - 1].T, ctx[:, P:DK, LK - 1].T
    arrays["const"] = np.concatenate(list(constants().values()), axis=1)
    order = ORDER
    fields = {}
    for name, parts in packs(i).items():
        if name in order:
            fields[name] = [(f, a.shape) for f, a in parts]
            arrays[f"w_{name}"] = np.concatenate([a.reshape(P, -1) for _, a in parts], axis=1)
    for name, a, c in (("L0_ffn", "w1", "w2"), ("L1_ffn", "W1", "W2"), ("L2_ffn", "W1", "W2"), ("L3_ffn", "w1", "w2")):
        if name in order:
            arrays[f"{name}_w1"], arrays[f"{name}_w2"] = experts(i[f"{name}_{a}"], i[f"{name}_{c}"])
    if "L2_boom" in order:
        arrays["L2_boom_w1"], arrays["L2_boom_w2"] = experts(i["L2_attn_Wb"].T[None], i["L2_attn_Wu"].T[None])
    arrays = {n: np.ascontiguousarray(a) for n, a in arrays.items()}
    args = {n: nc.dram_tensor(f"in_{n}", a.shape, mybir.dt.from_np(a.dtype), kind="ExternalInput").ap()
            for n, a in arrays.items()}
    args["out_0"] = nc.dram_tensor("out_0", (P, NT, D), F32, kind="ExternalOutput").ap()
    build(nc, args, {n: args[f"w_{n}"] for n in order}, fields, order)
    r = _run(nc, [{f"in_{n}": a for n, a in arrays.items()}], core_ids=[0])
    return unlay(r.results[0]["out_0"])
```

```python
from collections import namedtuple
from contextlib import ExitStack, contextmanager, nullcontext

import numpy as np

import concourse.bass as bass
from concourse import mybir

F32, F32R = mybir.dt.float32, mybir.dt.float32r
ALU = mybir.AluOpType
ACT = mybir.ActivationFunctionType
AX = mybir.AxisListType
ds = bass.ds

P = 128
B, S, D = 32, 32, 256
T = B * S
NT = T // P
BT = P // S
DC = D // P
LK, DK = 257, 192
LP = LK + LK % 2
BANK = 512
LN_EPS = 1e-5
NEG = -1.0e30



def constants():
    p = np.arange(P)
    f = np.float32
    out = {}
    out["ident"] = np.eye(P, dtype=f)
    out["head8"] = (p[:, None] // 16 == np.arange(8)[None, :]).astype(f)
    out["half4"] = (2 * np.arange(2)[None, :, None] + p[:, None, None] // 64 == np.arange(4)).astype(f).reshape(P, 8)
    out["seq4"] = (p[:, None] // S == np.arange(BT)[None, :]).astype(f)
    out["causal"] = np.where(np.arange(S)[None, :] <= (p % S)[:, None], 0.0, NEG).astype(f)
    out["first"] = (p[:, None] == (p[None, :] // S) * S).astype(f)
    out["before"] = (p[:, None] < p[None, :]).astype(f)
    out["ones"] = np.ones((P, P), f)
    out["down8"] = np.tile(8 - np.arange(8), (P, 1)).astype(f)
    out["down16"] = np.tile(16 - np.arange(16), (P, 1)).astype(f)
    keep = (np.arange(T) % S != 0).astype(f)
    out["keep"] = np.tile(keep, (P, 1))
    out["rcount"] = np.tile((1.0 / (np.arange(T) % S + 1)).astype(f), (P, 1))
    return out


def stacked(w):
    return np.stack([w[0:P], np.concatenate([w[P:], w[P:]])], axis=1)


def chunks(w):
    k = -(-w.shape[0] // P) * P
    w = np.concatenate([w, np.zeros((k - w.shape[0],) + w.shape[1:], w.dtype)]) if k != w.shape[0] else w
    return w.reshape(k // P, P, -1).transpose(1, 0, 2)


def column(v):
    return v.reshape(-1, P).T


def row(v):
    return np.broadcast_to(v.reshape(1, -1), (P, v.size))


def wo_rows(w, ng, hd):
    w = w.reshape(ng, 4, hd, -1).transpose(0, 2, 1, 3).reshape(ng * hd, 4, -1)
    return np.concatenate([w, np.zeros((P - ng * hd,) + w.shape[1:], w.dtype)]) if ng * hd < P else w


def conv_blocks(w):
    g = w.shape[1]
    out = np.zeros((P, DC, w.shape[2], P), w.dtype)
    for c in range(DC):
        for j in range(P // g):
            o = c * P + j * g
            out[j * g:(j + 1) * g, c, :, j * g:(j + 1) * g] = w[o:o + g].transpose(1, 2, 0)
    return out


def packs(i):
    out = {}
    for n in ("L0", "L1", "L2", "L3"):
        g = lambda k: i[f"{n}_xattn_{k}"]
        f = [("wq", chunks(g("Wq"))), ("wk", stacked(g("Wk"))), ("wv", stacked(g("Wv")))]
        if n in ("L0", "L1"):
            f += [("wo", wo_rows(g("Wo"), 4, 16)), ("bq", column(g("bq"))), ("bk", column(g("bk"))),
                  ("bv", row(g("bv"))), ("bo", row(g("bo")))]
        elif n == "L2":
            f += [("wo", wo_rows(g("Wo"), 2, 64)), ("bo", row(g("bo")))]
        else:
            f += [("bq", column(g("bq"))), ("bk", column(g("bk"))), ("bv", row(g("bv")))]
        out[f"{n}_xattn"] = f
    g = lambda k: i[f"L0_attn_{k}"]
    lam = np.repeat(g("lambda_raw"), 16)
    out["L0_attn"] = [("wq", chunks(g("Wq"))), ("wk", chunks(g("Wk"))), ("wv", chunks(g("Wv"))),
                      ("wqp", chunks(g("Wqp"))), ("wkp", chunks(g("Wkp"))), ("wo", wo_rows(g("Wo"), 4, 16)),
                      ("lam", column(lam))]
    w = i["L1_attn_w_qkv"].reshape(D, 16, 3, 16)
    q, k, v = (w[:, :, j].reshape(D, D) for j in range(3))
    out["L1_attn"] = [("wq", chunks(q)), ("wk", chunks(k)), ("wv", chunks(v)), ("wo", wo_rows(i["L1_attn_w_out"], 4, 16)),
                      ("bo", row(i["L1_attn_b_out"])), ("gamma", row(i["L1_attn_gamma"])), ("beta", row(i["L1_attn_beta"]))]
    g = lambda k: i[f"L2_attn_{k}"]
    out["L2_attn"] = [("wq", chunks(g("Wq").T)), ("wk", chunks(g("Wk").T)), ("wv", chunks(g("Wv").T)),
                      ("conv", conv_blocks(g("conv_w")))] + \
                     [(a, column(g(b))) for a, b in (("bq", "bq"), ("bk", "bk"), ("bv", "bv"), ("cb", "conv_b"),
                                                     ("g1", "ln_conv_g"), ("b1", "ln_conv_b"), ("g2", "ln_attn_g"),
                                                     ("b2", "ln_attn_b"), ("g3", "ln_boom_g"), ("b3", "ln_boom_b"))]
    out["L2_boom"] = [("b1", column(g("bb"))), ("bo", row(g("bu")))]
    g = lambda k: i[f"L3_attn_{k}"]
    out["L3_attn"] = [("wq", chunks(g("Wq").reshape(D, D))), ("wk", chunks(g("Wk").reshape(D, D))),
                      ("wv", chunks(g("Wv").reshape(D, D))), ("wo", wo_rows(g("Wout").reshape(D, D), 4, 16))]
    g = lambda k: i[f"L3_ffn_{k}"]

    def heads(w):
        return np.repeat(w.reshape(-1, 4, 16), 4, axis=1).reshape(-1, D)

    out["L3_gqa"] = [("wq", chunks(g("qw"))), ("wk", chunks(heads(g("kw")))), ("wv", chunks(heads(g("vw")))),
                     ("wo", wo_rows(g("ow"), 4, 16)), ("bq", column(g("qb"))), ("bk", column(heads(g("kb")).reshape(-1))),
                     ("bv", row(heads(g("vb")).reshape(-1))), ("bo", row(g("ob"))),
                     ("gamma", row(g("norm1_w"))), ("gamma2", row(g("norm2_w")))]

    def moe(gate, bias, b1, b2):
        f = [("gate", chunks(gate))]
        if bias is not None:
            f.append(("gb", row(bias)))
        if b1 is not None:
            f.append(("b1", b1.reshape(b1.shape[0], -1, P).transpose(2, 0, 1)))
            f.append(("b2", np.concatenate([b2, np.zeros((P - b2.shape[0], D), b2.dtype)])))
        return f

    out["L0_ffn"] = moe(i["L0_ffn_gate_w"], i["L0_ffn_gate_b"], i["L0_ffn_b1"], i["L0_ffn_b2"])
    out["L1_ffn"] = moe(i["L1_ffn_gate"], None, i["L1_ffn_b1"], i["L1_ffn_b2"])
    out["L2_ffn"] = moe(i["L2_ffn_Wr"], i["L2_ffn_br"], i["L2_ffn_b1"], i["L2_ffn_b2"])
    out["L3_ffn"] = moe(i["L3_ffn_gate_w"], None, None, None)
    return out


def experts(w1, w2):
    return (np.stack([chunks(a) for a in w1]), np.stack([chunks(a) for a in w2]))


ORDER = ["L0_xattn", "L0_attn", "L0_ffn", "L1_xattn", "L1_attn", "L1_ffn",
         "L2_xattn", "L2_attn", "L2_boom", "L2_ffn", "L3_xattn", "L3_attn", "L3_gqa", "L3_ffn"]



class Core:
    pass


@contextmanager
def stage(k, names):
    k.stages += 1
    sems = {n: k.nc.alloc_semaphore(name=f"{n}_{k.stages}") for n in names.split()}
    with k.nc.Block() as block:
        yield block, namedtuple("Semaphores", sems)(**sems)
    k.nc.clear_and_free_semaphores(list(sems.values()))
    k.nc.all_engine_barrier(sem_only=True)


@contextmanager
def buffers(k, dtype=F32, **shapes):
    with ExitStack() as ctx:
        k.buffers += 1
        made = {n: ctx.enter_context(k.nc.sbuf_tensor(f"{n}_{k.buffers}", list(s), dtype)) for n, s in shapes.items()}
        yield namedtuple("Buffers", made)(**made)


def fetch_weights(k, sp):
    i = k.fetched
    if i < min(k.fetch_to, len(k.order)):
        k.fetched += 1
        name = k.order[i]
        width = k.packed[name].shape[1]
        sp.dma_start(k.store[:, i % 2, 0:width], k.packed[name]).then_inc(k.weights_loaded[i % 2], 16)


FIELDS = "wq wk wv wo bq bk bv bo wqp wkp lam gamma gamma2 beta conv cb g1 b1 g2 b2 g3 b3 gate gb"
Weights = namedtuple("Weights", "at " + FIELDS, defaults=[None] * len(FIELDS.split()))


def weights(k, name):
    i = k.order.index(name)
    views, at = {}, 0
    for field, shape in k.fields[name]:
        n = int(np.prod(shape[1:]))
        v = k.store[:, i % 2, at:at + n]
        if len(shape) == 3:
            v = v.rearrange("p (a b) -> p a b", a=shape[1])
        if len(shape) == 4:
            v = v.rearrange("p (a b c) -> p a b c", a=shape[1], b=shape[2])
        views[field] = v
        at += n
    return Weights(at=(k.weights_loaded[i % 2], 16 * (i // 2 + 1)), **views)


def spread(ap, n, axis):
    shape = list(ap.shape)
    return ap.unsqueeze(axis).broadcast_to(shape[:axis] + [n] + shape[axis:])


def load_inputs(k):
    nc = k.nc
    with stage(k, "loaded") as (block, s):
        @block.sync
        def _(sp):
            sp.dma_start(k.x[:], k.in_x).then_inc(s.loaded, 16)
            sp.dma_start(k.consts[:, 0:k.late], k.in_const[:, 0:k.late]).then_inc(s.loaded, 16)
            fetch_weights(k, sp)
            sp.wait_ge(s.loaded, 32)


def store_output(k):
    with k.nc.Block() as block:
        @block.sync
        def _(sp):
            sp.dma_start(k.out, k.x[:]).then_inc(k.stored, 16)
            sp.wait_ge(k.stored, 16)


def normalize(k, src, dst, rms=False, gain=None, shift=None, eps=LN_EPS, w_at=None, add=None,
              early=()):
    nc = k.nc
    with stage(k, "stats_done aggr_done std_done rstd_done norm_done gained shifted early_loaded") as (block, s), \
            buffers(k, stats=[P, NT, 6], mv=[P, NT, 2], std=[P, NT], rstd=[P, NT], sq=[P, 2, D], eps=[P, 1]) as b:
        @block.vector
        def _(dve):
            if w_at:
                dve.wait_ge(*w_at)
            nc.vector.memset(b.eps[:], eps).then_inc(s.stats_done, 1)
            for t in range(NT):
                if rms:
                    if t >= 2:
                        dve.wait_ge(s.stats_done, t)
                    nc.vector.tensor_tensor_reduce(b.sq[:, t % 2, :], src[:, t, :], src[:, t, :], 1.0 / D, 0.0,
                                                   ALU.mult, ALU.add, b.mv[:, t, 1:2]).then_inc(s.stats_done, 1)
                else:
                    nc.vector.bn_stats(b.stats[:, t, :], src[:, t, :]).then_inc(s.stats_done, 1)
            for t in range(NT):
                if not rms:
                    dve.wait_ge(s.stats_done, t + 2)
                    nc.vector.bn_aggr(b.mv[:, t, :], b.stats[:, t, :]).then_inc(s.aggr_done, 1)
            dve.wait_ge(s.std_done, 1)
            nc.vector.reciprocal(b.rstd[:], b.std[:]).then_inc(s.rstd_done, 1)
            dve.wait_ge(s.rstd_done, 1)
            for t in range(NT):
                if rms:
                    nc.vector.tensor_scalar(dst[:, t, :], src[:, t, :], b.rstd[:, t:t + 1], None,
                                            ALU.mult).then_inc(s.norm_done, 1)
                else:
                    nc.vector.tensor_scalar(dst[:, t, :], src[:, t, :], b.mv[:, t, 0:1], b.rstd[:, t:t + 1],
                                            ALU.subtract, ALU.mult).then_inc(s.norm_done, 1)
            if gain is not None:
                dve.wait_ge(s.norm_done, NT)
                nc.vector.tensor_tensor(dst[:], dst[:], spread(gain, NT, 1), ALU.mult).then_inc(s.gained, 1)
            if shift is not None:
                dve.wait_ge(s.gained, 1)
                nc.vector.tensor_tensor(dst[:], dst[:], spread(shift, NT, 1), ALU.add).then_inc(s.shifted, 1)
            if add is not None:
                if shift is not None:
                    dve.wait_ge(s.shifted, 1)
                elif gain is not None:
                    dve.wait_ge(s.gained, 1)
                nc.vector.tensor_tensor(add[:], add[:], dst[:], ALU.add)

        @block.sync
        def _(sp):
            load_early(k, sp, s, early)

        @block.scalar
        def _(act):
            act.wait_ge(s.stats_done, NT + 1)
            if not rms:
                act.wait_ge(s.aggr_done, NT)
            nc.scalar.activation(b.std[:], b.mv[:, :, 1], ACT.Sqrt, bias=b.eps[:, 0:1]).then_inc(s.std_done, 1)


def load_early(k, sp, s, early):
    for dst, src in early:
        sp.dma_start(dst, src).then_inc(s.early_loaded, 16)
    fetch_weights(k, sp)
    if not k.late_started:
        k.late_started = True
        sp.dma_start(k.consts[:, k.late:], k.in_const[:, k.late:]).then_inc(k.late_loaded, 16)
    if early:
        sp.wait_ge(s.early_loaded, 16 * len(early))


def prepare(k, src, z, ht=None, padded=None, jobs=(), token_major=(), gain=None, shift=None, w_at=None,
            early=(), clear_early=None):
    nc = k.nc
    HT = NT // 2
    HI, LO = 0, 1
    TERMS = ((HI, HI), (HI, LO), (LO, HI))
    ws = [w for _, w, _, _ in jobs] + [w for _, w, _ in token_major]
    starts = [sum(w.shape[2] for w in ws[:n]) for n in range(len(ws) + 1)]
    units = [("channel", n, dst, bias, scale, m) for n, (dst, w, bias, scale) in enumerate(jobs)
             for m in range(w.shape[2] // P)]
    units += [("token", len(jobs) + n, dst, r_, None, q) for n, (dst, w, r_) in enumerate(token_major) for q in range(2)]
    owner = ["act" if n % 2 == 0 and (u[3] is None or (u[0] == "channel" and u[4] == 1.0)) else "dve"
             for n, u in enumerate(units)]
    total = {e: owner.count(e) for e in ("act", "dve")}
    rank = [owner[:n].count(owner[n]) for n in range(len(units))]
    BANKS = 4
    names = ("stats_done aggr_done std_done rstd_done norm_done turned x_gained x_hi x_lo w_hi w_split eps_set product_done "
             "taken_act taken_dve early_loaded early_cleared")
    with stage(k, names) as (block, s), ExitStack() as ctx:
        b = ctx.enter_context(buffers(k, stats=[P, NT, 6], mv=[P, NT, 2], std=[P, NT], rstd=[P, NT], eps=[P, 1]))
        if jobs:
            r = ctx.enter_context(buffers(k, F32R, x=[P, 2, DC, T], w=[P, 2, DC, starts[-1]]))
        if jobs and gain is not None:
            f = ctx.enter_context(buffers(k, x=[P, DC, T]))

        def turned_tiles(half, c):
            bank = k.ps[:, 2 * half + c, :]
            if padded is None:
                return ht[:, c, half * 512:(half + 1) * 512], bank
            return padded[:, c, half * 16:(half + 1) * 16, :], bank.rearrange("p (b s) -> p b s", s=S)

        def taken(n, half):
            return (s.taken_act if owner[n] == "act" else s.taken_dve, half * total[owner[n]] + rank[n] + 1)

        def view(unit, half):
            kind, _, dst, _, _, at = units[unit]
            bank = k.ps[:, 4 + (half * len(units) + unit) % BANKS, :]
            if kind == "channel":
                return dst[:, at, half * 512:(half + 1) * 512], bank
            tile = half * HT + 2 * at
            return dst[:, tile:tile + 2, :], bank.rearrange("p (t d) -> p t d", d=D)

        @block.sync
        def _(sp):
            load_early(k, sp, s, early)

        @block.tensor
        def _(pe):
            for half in range(2):
                for t in range(HT):
                    pe.wait_ge(s.norm_done, half * HT + t + 1)
                    for c in range(DC):
                        mm = nc.tensor.transpose(k.ps[:, 2 * half + c, t * P:(t + 1) * P],
                                                 z[:, half * HT + t, c * P:(c + 1) * P], k.ident)
                mm.then_inc(s.turned, 1)
                for n, (kind, wi, _, _, _, at) in enumerate(units):
                    if n == 0:
                        pe.wait_ge(s.x_lo, DC * (half + 1))
                    if half == 0:
                        pe.wait_ge(s.w_split, wi + 1)
                    turn = half * len(units) + n
                    if turn >= BANKS:
                        pe.wait_ge(*taken((turn - BANKS) % len(units), (turn - BANKS) // len(units)))
                    bank = k.ps[:, 4 + turn % BANKS, :]
                    for i, (p1, p2) in enumerate(TERMS):
                        for c in range(DC):
                            if kind == "channel":
                                col = starts[wi] + at * P
                                mm = nc.tensor.matmul(bank, r.w[:, p1, c, col:col + P],
                                                      r.x[:, p2, c, half * 512:(half + 1) * 512],
                                                      start=i == 0 and c == 0, stop=i == 2 and c == DC - 1)
                    if kind == "token":
                        for t in range(2):
                            for i, (p1, p2) in enumerate(TERMS):
                                for c in range(DC):
                                    tok = (half * HT + 2 * at + t) * P
                                    mm = nc.tensor.matmul(bank[:, t * D:(t + 1) * D], r.x[:, p1, c, tok:tok + P],
                                                          r.w[:, p2, c, starts[wi]:starts[wi] + D],
                                                          start=i == 0 and c == 0, stop=i == 2 and c == DC - 1)
                    mm.then_inc(s.product_done, 1)

        @block.scalar
        def _(act):
            if w_at:
                act.wait_ge(*w_at)
            for n, w in enumerate(ws):
                nc.scalar.copy(r.w[:, HI, :, starts[n]:starts[n + 1]], w).then_inc(s.w_hi, 1)
            act.wait_ge(s.eps_set, 1)
            for half in range(2):
                tiles = slice(half * HT, (half + 1) * HT)
                act.wait_ge(s.aggr_done, (half + 1) * HT)
                nc.scalar.activation(b.std[:, tiles], b.mv[:, tiles, 1], ACT.Sqrt, bias=b.eps[:, 0:1]).then_inc(s.std_done, 1)
            for half in range(2):
                tokens = slice(half * 512, (half + 1) * 512)
                act.wait_ge(s.turned, half + 1)
                for c in range(DC):
                    if jobs and gain is None:
                        nc.scalar.copy(r.x[:, HI, c, tokens], k.ps[:, 2 * half + c, :]).then_inc(s.x_hi, 1)
                    elif jobs:
                        nc.scalar.activation(f.x[:, c, tokens], k.ps[:, 2 * half + c, :], ACT.Identity,
                                             bias=shift[:, c:c + 1], scale=gain[:, c:c + 1]).then_inc(s.x_gained, 1)
                    elif c == 0:
                        out, inp = turned_tiles(half, c)
                        if gain is None:
                            nc.scalar.copy(out, inp)
                        else:
                            nc.scalar.activation(out, inp, ACT.Identity, bias=shift[:, c:c + 1], scale=gain[:, c:c + 1])
                for n, (kind, _, _, bias, scale, m) in enumerate(units):
                    if owner[n] == "dve":
                        continue
                    act.wait_ge(s.product_done, half * len(units) + n + 1)
                    out, inp = view(n, half)
                    if kind == "token":
                        nc.scalar.copy(out, inp).then_inc(s.taken_act, 1)
                    elif bias is None:
                        nc.scalar.mul(out, inp, scale).then_inc(s.taken_act, 1)
                    else:
                        nc.scalar.activation(out, inp, ACT.Identity, bias=bias[:, m:m + 1]).then_inc(s.taken_act, 1)

        @block.gpsimd
        def _(pool):
            for n, w in enumerate(ws):
                at = slice(starts[n], starts[n + 1])
                pool.wait_ge(s.w_hi, n + 1)
                nc.gpsimd.tensor_tensor(r.w[:, LO, :, at], w, r.w[:, HI, :, at], ALU.subtract).then_inc(s.w_split, 1)
            if clear_early is not None:
                nc.gpsimd.memset(clear_early, 0.0).then_inc(s.early_cleared, 1)

        @block.vector
        def _(dve):
            nc.vector.memset(b.eps[:], LN_EPS).then_inc(s.eps_set, 1)
            for half in range(2):
                for t in range(half * HT, (half + 1) * HT):
                    nc.vector.bn_stats(b.stats[:, t, :], src[:, t, :]).then_inc(s.stats_done, 1)
                for t in range(half * HT, (half + 1) * HT):
                    dve.wait_ge(s.stats_done, t + 1)
                    nc.vector.bn_aggr(b.mv[:, t, :], b.stats[:, t, :]).then_inc(s.aggr_done, 1)
            for half in range(2):
                tiles = slice(half * HT, (half + 1) * HT)
                dve.wait_ge(s.std_done, half + 1)
                nc.vector.reciprocal(b.rstd[:, tiles], b.std[:, tiles]).then_inc(s.rstd_done, 1)
                dve.wait_ge(s.rstd_done, half + 1)
                for t in range(half * HT, (half + 1) * HT):
                    nc.vector.tensor_scalar(z[:, t, :], src[:, t, :], b.mv[:, t, 0:1], b.rstd[:, t:t + 1],
                                            ALU.subtract, ALU.mult).then_inc(s.norm_done, 1)
            if w_at:
                dve.wait_ge(*w_at)
            for half in range(2):
                tokens = slice(half * 512, (half + 1) * 512)
                for c in range(DC):
                    if jobs:
                        whole = k.ps[:, 2 * half + c, :]
                        if gain is not None:
                            whole = f.x[:, c, tokens]
                            dve.wait_ge(s.x_gained, DC * half + c + 1)
                            nc.vector.tensor_copy(r.x[:, HI, c, tokens], whole).then_inc(s.x_hi, 1)
                        dve.wait_ge(s.x_hi, DC * half + c + 1)
                        nc.vector.tensor_tensor(r.x[:, LO, c, tokens], whole, r.x[:, HI, c, tokens],
                                                ALU.subtract).then_inc(s.x_lo, 1)
                    elif c == 1:
                        dve.wait_ge(s.turned, half + 1)
                        out, inp = turned_tiles(half, c)
                        if gain is None:
                            nc.vector.tensor_copy(out, inp)
                        else:
                            nc.vector.tensor_scalar(out, inp, gain[:, c:c + 1], shift[:, c:c + 1], ALU.mult, ALU.add)
                for n, (kind, _, _, bias, scale, m) in enumerate(units):
                    if owner[n] == "act":
                        continue
                    dve.wait_ge(s.product_done, half * len(units) + n + 1)
                    out, inp = view(n, half)
                    if kind == "token" and bias is None or kind == "channel" and bias is None and scale == 1.0:
                        nc.vector.tensor_copy(out, inp).then_inc(s.taken_dve, 1)
                    elif kind == "token":
                        nc.vector.tensor_tensor(out, inp, spread(bias, 2, 1), ALU.add).then_inc(s.taken_dve, 1)
                    elif bias is None:
                        nc.vector.tensor_scalar(out, inp, scale, None, ALU.mult).then_inc(s.taken_dve, 1)
                    else:
                        nc.vector.tensor_scalar(out, inp, bias[:, m:m + 1], scale, ALU.add, ALU.mult).then_inc(s.taken_dve, 1)


def transpose_tokens(k, src, dst, gain=None, shift=None, padded=None, w_at=None):
    nc = k.nc
    with stage(k, "turned copied") as (block, s):
        @block.tensor
        def _(pe):
            for q in range(2 * DC):
                c, half = q % DC, q // DC
                for t in range(4):
                    last = nc.tensor.transpose(k.ps[:, q, t * P:(t + 1) * P],
                                               src[:, half * 4 + t, c * P:(c + 1) * P], k.ident)
                last.then_inc(s.turned, 1)

        def copy(eng, which, q):
            c, half = q % DC, q // DC
            eng.wait_ge(s.turned, q + 1)
            if padded is not None:
                out = padded[:, c, half * 16:(half + 1) * 16, :]
                inp = k.ps[:, q, :].rearrange("p (b s) -> p b s", s=S)
            else:
                out, inp = dst[:, c, half * 512:(half + 1) * 512], k.ps[:, q, :]
            if which == "act":
                if gain is None:
                    nc.scalar.copy(out, inp)
                else:
                    nc.scalar.activation(out, inp, ACT.Identity, bias=shift[:, c:c + 1], scale=gain[:, c:c + 1])
            elif gain is None:
                nc.vector.tensor_copy(out, inp)
            else:
                nc.vector.tensor_scalar(out, inp, gain[:, c:c + 1], shift[:, c:c + 1], ALU.mult, ALU.add)

        @block.scalar
        def _(act):
            if w_at:
                act.wait_ge(*w_at)
            for q in (0, 2):
                copy(act, "act", q)

        @block.vector
        def _(dve):
            if w_at:
                dve.wait_ge(*w_at)
            for q in (1, 3):
                copy(dve, "dve", q)


def transpose_channels(k, src, dst, adds):
    nc = k.nc
    with stage(k, "turned") as (block, s):
        @block.tensor
        def _(pe):
            for t in range(NT):
                for c in range(DC):
                    last = nc.tensor.transpose(k.ps[:, t // 2, (t % 2) * D + c * P:(t % 2) * D + (c + 1) * P],
                                               src[:, c, t * P:(t + 1) * P], k.ident)
                if t % 2:
                    last.then_inc(s.turned, 1)

        @block.vector
        def _(dve):
            for q in range(NT // 2):
                dve.wait_ge(s.turned, q + 1)
                nc.vector.tensor_tensor(dst[:, 2 * q:2 * q + 2, :], adds[:, 2 * q:2 * q + 2, :],
                                        k.ps[:, q, :].rearrange("p (t d) -> p t d", d=D), ALU.add)


def cross_attention(k, w, qt, given, heads, hd, clamp=None):
    nc = k.nc
    inner = heads * hd
    ng, kc = heads // 4, inner // P
    gc = max(1, 4 * hd // P)
    gw = 4 * hd
    nh = 8 if hd == 16 else 4
    TAIL = 2 * P
    if hd == 16:
        KB, VB, SB, TB, OB, OTB = [0, 1], [(2, 0), (2, 256)], 4, [0, 1], 3, 3
    else:
        KB, VB, SB, TB, OB, OTB = [0, 1, 2, 3], [(4, 0), (5, 0)], 6, [0, 1], 2, 3
    TT, YT = slice(3 * P, 4 * P), slice(P, P + D)
    names = ("ctx_loaded0 ctx_loaded1 w_hi w_split ctx_hi ctx_low ctx_split tail_done tail_ready tail_placed cleared keys_done values_done "
             "keys_ready values_ready spread_ready scores_done clamped max_ready probs_ready turned_done "
             "tail_turned turned_act turned_dve rsum_ready pv_done o_ready ot_done ot_ready y_done y_added x_ready")
    with stage(k, names) as (block, s), \
            buffers(k, vtail=[B, inner], key=[P, 2, kc, LK], val=[P, 2, 2, inner], qx=[P, 2, kc, nh, S],
                    p=[P, 2, ng, LK], nmax=[P, 2, ng], sums=[P, 2, ng], rsum=[P, 2, ng],
                    pt=[P, 2, ng * P], ptt=[ng, P], o=[P, P], ot=[ng * hd, 4, P],
                    sc=[P, ng if clamp else 1, LK if clamp else 1]) as b, \
            buffers(k, F32R, w=[P, 2, 2, 2 * inner], c=[P, 2, 2, LP], clo=[P, 2, LP]) as r:
        ctx_loaded = [s.ctx_loaded0, s.ctx_loaded1]

        def factors(par, at, rows):
            whi, wlo = r.w[:, 0, :, at], r.w[:, 1, :, at]
            return ((whi[:, 0], r.c[:, par, 0, rows]), (whi[:, 0], r.clo[:, par, rows]), (wlo[:, 0], r.c[:, par, 0, rows]),
                    (whi[:, 1], r.c[:, par, 1, rows]), (wlo[0:DK - P, 1], r.c[0:DK - P, par, 1, rows]))

        @block.sync
        def _(sp):
            def load(n, par):
                sp.dma_start(given.c[:, par], k.ctx[ds(n, 1)].rearrange("a p c l -> (a p) c l")).then_inc(ctx_loaded[par], 16)

            sp.wait_ge(s.tail_ready, 1)
            for g in range(ng):
                sp.dma_start(given.vt[g:g + 1, :, g * gw:(g + 1) * gw],
                             b.vtail[:, g * gw:(g + 1) * gw]).then_inc(s.tail_placed, 16)

            def body(it, last):
                for j in range(BT):
                    if last and j >= 2:
                        break
                    n = it * BT + j
                    sp.wait_ge(s.ctx_low, n + 1)
                    sp.wait_ge(s.ctx_split, n + 1)
                    load(n + 2, j % 2)

            with sp.Fori(0, NT - 1) as it:
                body(it, False)
            body(NT - 1, True)

        @block.tensor
        def _(pe):
            pe.wait_ge(*w.at)
            for c, t in ((0, given.t0), (1, given.t1)):
                kr = P if c == 0 else DK - P
                last = nc.tensor.matmul(k.ps[0:B, 7, 0:inner], t[:], w.wv[0:kr, c, :], start=c == 0, stop=c == 1)
            last.then_inc(s.tail_done, 1)
            pe.wait_ge(s.w_split, 2)

            def keys_values(m, par, first=False):
                pe.wait_ge(s.ctx_low, m + 1)
                pe.wait_ge(s.ctx_split, m + 1)
                for j in range(kc):
                    if KB[j] == OB and not first:
                        pe.wait_ge(s.o_ready, m)
                    for t, (wp, cp) in enumerate(factors(par, slice(j * P, (j + 1) * P), slice(0, LP))):
                        last = nc.tensor.matmul(k.ps[:, KB[j], 0:LP], wp, cp, start=t == 0, stop=t == 4)
                last.then_inc(s.keys_done, 1)
                for half in range(2):
                    bank, at = VB[half]
                    for t, (wp, cp) in enumerate(factors(par, slice(inner, 2 * inner), slice(half * P, (half + 1) * P))):
                        last = nc.tensor.matmul(k.ps[:, bank, at:at + inner], cp, wp, start=t == 0, stop=t == 4)
                last.then_inc(s.values_done, 1)

            def scores(n, par):
                pe.wait_ge(s.keys_ready, n + 1)
                pe.wait_ge(s.spread_ready, n + 1)
                for g in range(ng):
                    for c in range(gc):
                        chunk = (g * gw) // P + c
                        h0 = ((g * gw) % P) // hd
                        last = nc.tensor.matmul(k.ps[:, SB + g, 0:LK], b.qx[:, par, chunk, h0:h0 + 4, :],
                                                b.key[:, par, chunk, :], start=c == 0, stop=c == gc - 1)
                    if g % (ng // 2) == ng // 2 - 1:
                        last.then_inc(s.scores_done, 1)

            def turn_last_column(n, par):
                pe.wait_ge(s.probs_ready, n + 1)
                nc.tensor.transpose(k.ps[0:ng, OTB, TT], b.p[:, par, :, TAIL], k.ident).then_inc(s.tail_turned, 1)

            def turn_probs(n, par, final):
                if not final:
                    pe.wait_ge(s.keys_ready, n + 2)
                for half in range(2):
                    for g in range(ng):
                        last = nc.tensor.transpose(k.ps[:, TB[half], g * P:(g + 1) * P],
                                                   b.p[:, par, g, half * P:(half + 1) * P], k.ident)
                    last.then_inc(s.turned_done, 1)

            def probs_values(n, par):
                pe.wait_ge(s.turned_act, 2 * n + 2)
                pe.wait_ge(s.turned_dve, n + 1)
                nc.tensor.matmul(k.ps[:, OB, 0:inner], b.ptt[:], given.vt[:, ds(n, 1), :].rearrange("g a c -> g (a c)"),
                                 start=True, stop=False)
                for g in range(ng):
                    for half in range(2):
                        last = nc.tensor.matmul(k.ps[:, OB, g * gw:(g + 1) * gw], b.pt[:, half, g * P:(g + 1) * P],
                                                b.val[:, par, half, g * gw:(g + 1) * gw], start=False,
                                                stop=(g == ng - 1 and half == 1))
                last.then_inc(s.pv_done, 1)

            def turn_outputs(n):
                pe.wait_ge(s.o_ready, n + 2)
                nc.tensor.transpose(k.ps[:, OTB, 0:P], b.o[:], k.ident).then_inc(s.ot_done, 1)

            def output_product(it):
                pe.wait_ge(s.ot_ready, it * BT + BT)
                for h in range(4):
                    mm = nc.tensor.matmul(k.ps[:, OTB, YT], b.ot[:, h, :], w.wo[0:ng * hd, h, :],
                                          start=h == 0, stop=h == 3)
                mm.then_inc(s.y_done, 1)

            def body(it, first, last):
                for j in range(BT):
                    n = it * BT + j
                    final = last and j == BT - 1
                    start = first and j == 0
                    if not final:
                        keys_values(n + 1, (j + 1) % 2)
                    if not final and OTB in KB:
                        pe.wait_ge(s.keys_ready, n + 2)
                    if not start:
                        turn_outputs(n - 1)
                    turn_last_column(n, j % 2)
                    turn_probs(n, j % 2, final)
                    if j == 0 and not first:
                        pe.wait_ge(s.turned_act, 2 * n + 1)
                        output_product(it - 1)
                    if not final:
                        scores(n + 1, (j + 1) % 2)
                    if not start:
                        pe.wait_ge(s.ot_ready, n)
                    if j == 0 and not first:
                        pe.wait_ge(s.y_added, it)
                    probs_values(n, j % 2)

            keys_values(0, 0, first=True)
            pe.wait_ge(s.tail_ready, 1)
            scores(0, 0)
            pe.wait_ge(s.values_ready, 1)
            pe.wait_ge(s.tail_placed, 16 * ng)
            body(0, True, False)
            with pe.Fori(1, NT - 1) as it:
                body(it, False, False)
            body(NT - 1, False, True)
            turn_outputs(B - 1)
            output_product(NT - 1)

        @block.scalar
        def _(act):
            act.wait_ge(*w.at)

            def take_keys(n, par):
                act.wait_ge(s.keys_done, n + 1)
                for j in range(kc):
                    if w.bk is None:
                        last = nc.scalar.copy(b.key[:, par, j, :], k.ps[:, KB[j], 0:LK])
                    else:
                        last = nc.scalar.activation(b.key[:, par, j, :], k.ps[:, KB[j], 0:LK], ACT.Identity,
                                                    bias=w.bk[:, j:j + 1])
                last.then_inc(s.keys_ready, 1)

            def exponentials(n, par):
                for g in range(ng):
                    if g % (ng // 2) == 0:
                        act.wait_ge(s.max_ready, 2 * n + 1 + g // (ng // 2))
                    score = b.sc[:, g, :] if clamp else k.ps[:, SB + g, 0:LK]
                    last = nc.scalar.activation(b.p[:, par, g, :], score, ACT.Exp, bias=b.nmax[:, par, g:g + 1],
                                                accum_out=b.sums[:, par, g:g + 1])
                last.then_inc(s.probs_ready, 1)

            def take_turned_outputs(n, j):
                act.wait_ge(s.ot_done, n + 1)
                nc.scalar.copy(b.ot[:, :, j * S:(j + 1) * S],
                               k.ps[0:ng * hd, OTB, 0:P].rearrange("p (h q) -> p h q", q=S)).then_inc(s.ot_ready, 1)

            def body(it, first, last):
                for j in range(BT):
                    n = it * BT + j
                    final = last and j == BT - 1
                    if not final:
                        take_keys(n + 1, (j + 1) % 2)
                    act.wait_ge(s.tail_turned, n + 1)
                    if not (first and j == 0):
                        take_turned_outputs(n - 1, (j - 1) % BT)
                    nc.scalar.copy(b.ptt[:], k.ps[0:ng, OTB, TT]).then_inc(s.turned_act, 1)
                    act.wait_ge(s.turned_done, 2 * n + 1)
                    nc.scalar.copy(b.pt[:, 0, :], k.ps[:, TB[0], 0:ng * P]).then_inc(s.turned_act, 1)
                    if not final:
                        exponentials(n + 1, (j + 1) % 2)

            for u, part in ((0, w.wk), (1, w.wv)):
                nc.scalar.copy(r.w[:, 0, :, u * inner:(u + 1) * inner], part).then_inc(s.w_hi, 1)
            take_keys(0, 0)
            exponentials(0, 0)
            body(0, True, False)
            with act.Fori(1, NT - 1) as it:
                body(it, False, False)
            body(NT - 1, False, True)
            take_turned_outputs(B - 1, BT - 1)

        @block.gpsimd
        def _(pool):
            nc.gpsimd.memset(b.o[:], 0.0).then_inc(s.cleared, 1)

            def spread_queries(n, par):
                for c in range(kc):
                    m = k.head8 if hd == 16 else k.half4[:, c % 2, :]
                    q = spread(qt[:, c, ds(n * S, S)], nh, 1)
                    last = nc.gpsimd.tensor_tensor(b.qx[:, par, c, :, :], q, spread(m, S, 2), ALU.mult)
                last.then_inc(s.spread_ready, 1)

            def split_context(n, par):
                pool.wait_ge(s.ctx_hi, n + 1)
                nc.gpsimd.tensor_tensor(r.clo[:, par, :], given.c[:, par, 0, :], r.c[:, par, 0, :],
                                        ALU.subtract).then_inc(s.ctx_split, 1)

            split_context(0, 0)
            spread_queries(0, 0)
            split_context(1, 1)
            spread_queries(1, 1)

            def body(it, last):
                for j in range(BT):
                    if last and j >= 2:
                        break
                    n = it * BT + j
                    split_context(n + 2, j % 2)
                    pool.wait_ge(s.scores_done, 2 * n + 2)
                    spread_queries(n + 2, j % 2)

            with pool.Fori(0, NT - 1) as it:
                body(it, False)
            body(NT - 1, True)

        @block.vector
        def _(dve):
            def round_context(n, par, turn):
                if turn is not None:
                    dve.wait_ge(ctx_loaded[par], 16 * turn)
                nc.vector.tensor_copy(r.c[:, par], given.c[:, par]).then_inc(s.ctx_hi, 1)
                dve.wait_ge(s.ctx_hi, n + 1)
                low = slice(DK - P, P)
                nc.vector.tensor_tensor(r.c[low, par, 1, :], given.c[low, par, 1, :], r.c[low, par, 1, :],
                                        ALU.subtract).then_inc(s.ctx_low, 1)

            round_context(0, 0, None)
            round_context(1, 1, None)
            dve.wait_ge(*w.at)
            for u, part in ((0, w.wk), (1, w.wv)):
                at = slice(u * inner, (u + 1) * inner)
                dve.wait_ge(s.w_hi, u + 1)
                nc.vector.tensor_tensor(r.w[:, 1, :, at], part, r.w[:, 0, :, at], ALU.subtract).then_inc(s.w_split, 1)
            dve.wait_ge(s.cleared, 1)
            dve.sem_inc(s.o_ready, 1)
            dve.wait_ge(s.tail_done, 1)
            if w.bv is None:
                nc.vector.tensor_copy(b.vtail[:], k.ps[0:B, 7, 0:inner]).then_inc(s.tail_ready, 1)
            else:
                nc.vector.tensor_tensor(b.vtail[:], k.ps[0:B, 7, 0:inner], w.bv[0:B, :], ALU.add).then_inc(s.tail_ready, 1)

            outputs = b.o[:, 0:ng * hd].rearrange("p (g d) -> p g d", d=hd)

            def take_values(n, par):
                dve.wait_ge(s.values_done, n + 1)
                if VB[0][0] == VB[1][0]:
                    src, dst = k.ps[:, VB[0][0], :].rearrange("p (r c) -> p r c", r=2), b.val[:, par, :, :]
                else:
                    src, dst = k.ps[:, VB[0][0]:VB[0][0] + 2, 0:inner], b.val[:, par, :, :]
                if w.bv is None:
                    nc.vector.tensor_copy(dst, src).then_inc(s.values_ready, 1)
                else:
                    nc.vector.tensor_tensor(dst, src, spread(w.bv, 2, 1), ALU.add).then_inc(s.values_ready, 1)

            def maxima(n, par):
                for half in range(2):
                    gs = slice(half * ng // 2, (half + 1) * ng // 2)
                    dve.wait_ge(s.scores_done, 2 * n + 1 + half)
                    score = k.ps[:, SB + gs.start:SB + gs.stop, 0:LK]
                    if clamp:
                        nc.vector.tensor_scalar(b.sc[:, gs, :], score, clamp, -clamp, ALU.min,
                                                ALU.max).then_inc(s.clamped, 1)
                        dve.wait_ge(s.clamped, 2 * n + 1 + half)
                        score = b.sc[:, gs, :]
                    nc.vector.tensor_reduce(b.nmax[:, par, gs], score, AX.X, ALU.max, negate=True).then_inc(s.max_ready, 1)

            def add(it):
                dve.wait_ge(s.y_done, it + 1)
                tile = k.x[:, ds(it, 1), :].rearrange("p a d -> p (a d)")
                nc.vector.tensor_tensor(tile, tile, k.ps[:, OTB, YT], ALU.add).then_inc(s.y_added, 1)

            def body(it, first, last):
                for j in range(BT):
                    n = it * BT + j
                    par = j % 2
                    final = last and j == BT - 1
                    if not final:
                        take_values(n + 1, 1 - par)
                    if not (last and j >= 2):
                        round_context(n + 2, par, 2 * it + j // 2 + 1)
                    dve.wait_ge(s.turned_done, 2 * n + 2)
                    nc.vector.tensor_copy(b.pt[:, 1, :], k.ps[:, TB[1], 0:ng * P]).then_inc(s.turned_dve, 1)
                    dve.wait_ge(s.probs_ready, n + 1)
                    nc.vector.reciprocal(b.rsum[:, par, :], b.sums[:, par, :]).then_inc(s.rsum_ready, 1)
                    if j == 0 and not first:
                        add(it - 1)
                    if not final:
                        maxima(n + 1, 1 - par)
                    dve.wait_ge(s.rsum_ready, n + 1)
                    dve.wait_ge(s.pv_done, n + 1)
                    for h in range(4):
                        rows = slice(h * S, (h + 1) * S)
                        own = k.ps[rows, OB, 0:inner].rearrange("p (g h d) -> p g h d", h=4, d=hd)[:, :, h, :]
                        o = nc.vector.tensor_tensor(outputs[rows, :, :], own, spread(b.rsum[rows, par, :], hd, 2), ALU.mult)
                    o.then_inc(s.o_ready, 1)

            dve.wait_ge(*w.at)
            nc.vector.tensor_tensor(k.x[:], k.x[:], spread(w.bo, NT, 1), ALU.add).then_inc(s.x_ready, 1)
            take_values(0, 0)
            maxima(0, 0)
            dve.wait_ge(s.x_ready, 1)
            body(0, True, False)
            with dve.Fori(1, NT - 1) as it:
                body(it, False, False)
            body(NT - 1, False, True)
            add(NT - 1)


def self_attention(k, w, qt, kt, v, into, causal=False, relu=False, scale=0.25, more=()):
    nc = k.nc
    sets = [(qt, kt), *more]
    HD, NG, GW = 16, 4, 64
    SB, PB, OB, TB, YB = 0, 1, 2, 4, 5
    names = ("cleared spread_dve spread_pool spread_act vspread_ready scores_done masked max_ready shifted probs_ready "
             "sums_raw sums_ready rsum_ready turned_done turned_ready pv_done o_ready ot_done ot_ready y_done y_added "
             "y_biased")
    with stage(k, names) as (block, s), \
            buffers(k, qx=[P, len(sets), DC, BT, 8, S], vx=[P, NG, BT, GW], sc=[P, NG, BT, S], p=[P, NG, BT, S],
                    m=[P, NG, BT], sums=[P, NG, BT], rsum=[P, NG, BT], pt=[P, NG, P], o=[P, BT, P],
                    ot=[NG * HD, 4, P]) as b:
        spread_by = [s.spread_dve, s.spread_act] + ([s.spread_pool] if more else [])
        dve_slots = range(8) if more else range(4)
        act_set, act_slots = (2, range(8)) if more else (0, range(4, 8))

        def score_bank():
            return k.ps[:, SB, :].rearrange("p (u l) -> p u l", l=S)

        def head_rows(m, i, h):
            return (b.qx[:, m, :, :, h, :], sets[m][0][:, :, ds(i * P, P)].rearrange("p c (b q) -> p c b q", b=BT))

        @block.tensor
        def _(pe):
            def scores(i, last_tile=False):
                for done in spread_by:
                    pe.wait_ge(done, i + 1)
                for g in range(NG):
                    c, h0 = g // 2, 4 * (g % 2)
                    for b_ in range(BT):
                        own = (g * BT + b_) * S
                        rest = min(P, BANK - own, (BT - b_) * S if last_tile else P)
                        for m, (_, keys) in enumerate(sets):
                            last = nc.tensor.matmul(k.ps[:, SB, own:own + rest], b.qx[:, m, c, b_, h0:h0 + 4, :],
                                                    keys[:, c, ds(i * P + b_ * S, rest)], start=m == 0,
                                                    stop=m == len(sets) - 1)
                last.then_inc(s.scores_done, 1)

            def output_product(i):
                pe.wait_ge(s.ot_ready, i + 1)
                pe.wait_ge(s.y_added, i + 1)
                for h in range(4):
                    mm = nc.tensor.matmul(k.ps[:, YB, 0:D], b.ot[:, h, :], w.wo[0:NG * HD, h, :],
                                          start=h == 0, stop=h == 3)
                mm.then_inc(s.y_done, 1)

            def body(i, first, last, last_scores=False):
                pe.wait_ge(s.probs_ready, i + 1)
                for g in range(NG):
                    mm = nc.tensor.transpose(k.ps[:, PB, g * P:(g + 1) * P],
                                             b.p[:, g, :, :].rearrange("p b l -> p (b l)"), k.ident)
                mm.then_inc(s.turned_done, 1)
                if not last:
                    scores(i + 1, last_scores)
                pe.wait_ge(s.turned_ready, i + 1)
                pe.wait_ge(s.vspread_ready, i + 1)
                for g in range(NG):
                    mm = nc.tensor.matmul(k.ps[:, OB + g // 2, (g % 2) * 256:(g % 2) * 256 + 256], b.pt[:, g, :],
                                          b.vx[:, g, :, :].rearrange("p b c -> p (b c)"), start=True, stop=True)
                mm.then_inc(s.pv_done, 1)
                if not first:
                    output_product(i - 1)
                pe.wait_ge(s.o_ready, i + 1)
                for b_ in range(BT):
                    mm = nc.tensor.transpose(k.ps[:, TB, b_ * P:(b_ + 1) * P], b.o[:, b_, :], k.ident)
                mm.then_inc(s.ot_done, 1)

            pe.wait_ge(*w.at)
            scores(0)
            body(0, True, False)
            with pe.Fori(1, NT - 2) as i:
                body(i, False, False)
            body(NT - 2, False, False, last_scores=True)
            body(NT - 1, False, True)
            output_product(NT - 1)

        @block.scalar
        def _(act):
            def spread_queries(i):
                for h in act_slots:
                    out, q = head_rows(act_set, i, h)
                    last = nc.scalar.mul(out, q, k.head8[:, h:h + 1])
                last.then_inc(s.spread_act, 1)

            def probs(i):
                if relu:
                    act.wait_ge(s.scores_done, i + 1)
                    nc.scalar.activation(b.p[:].rearrange("p g b l -> p (g b) l"), score_bank(), ACT.Relu, scale=scale).then_inc(s.probs_ready, 1)
                else:
                    act.wait_ge(s.shifted, i + 1)
                    nc.scalar.activation(b.p[:], b.sc[:], ACT.Exp, scale=scale).then_inc(s.probs_ready, 1)

            def body(i, last, ahead):
                act.wait_ge(s.turned_done, i + 1)
                nc.scalar.copy(b.pt[:], k.ps[:, PB, :].rearrange("p (g c) -> p g c", g=NG)).then_inc(s.turned_ready, 1)
                if not last:
                    act.wait_ge(s.sums_ready, i + 1)
                    probs(i + 1)
                if ahead:
                    spread_queries(i + 2)
                act.wait_ge(s.ot_done, i + 1)
                nc.scalar.copy(b.ot[:].rearrange("p h (b q) -> p h b q", b=BT),
                               k.ps[0:NG * HD, TB, :].rearrange("p (b h q) -> p h b q", b=BT, h=4)).then_inc(s.ot_ready, 1)

            spread_queries(0)
            probs(0)
            spread_queries(1)
            with act.Fori(0, NT - 2) as i:
                body(i, False, True)
            body(NT - 2, False, False)
            body(NT - 1, True, False)

        @block.gpsimd
        def _(pool):
            nc.gpsimd.memset(b.o[:], 0.0).then_inc(s.cleared, 1)

            def spread_second(i):
                for c in range(DC):
                    for b_ in range(BT):
                        queries = spread(sets[1][0][:, c, ds(i * P + b_ * S, S)], 8, 1)
                        last = nc.gpsimd.tensor_tensor(b.qx[:, 1, c, b_, :, :], queries, spread(k.head8, S, 2), ALU.mult)
                last.then_inc(s.spread_pool, 1)

            def spread_values(i):
                for g in range(NG):
                    vg = v[:, ds(i, 1), g * GW:(g + 1) * GW].rearrange("p a c -> p (a c)")
                    last = nc.gpsimd.tensor_tensor(b.vx[:, g, :, :], spread(vg, BT, 1), spread(k.seq4, GW, 2), ALU.mult)
                last.then_inc(s.vspread_ready, 1)

            if more:
                spread_second(0)
            spread_values(0)
            if more:
                pool.wait_ge(s.scores_done, 1)
                spread_second(1)
            with pool.Fori(0, NT - 2) as i:
                if more:
                    pool.wait_ge(s.scores_done, i + 2)
                    spread_second(i + 2)
                pool.wait_ge(s.pv_done, i + 1)
                spread_values(i + 1)
            pool.wait_ge(s.pv_done, NT - 1)
            spread_values(NT - 1)

        @block.vector
        def _(dve):
            def spread_first(i):
                for h in dve_slots:
                    out, q = head_rows(0, i, h)
                    last = nc.vector.tensor_scalar(out, q, k.head8[:, h:h + 1], None, ALU.mult)
                last.then_inc(s.spread_dve, 1)

            def shift(i):
                dve.wait_ge(s.scores_done, i + 1)
                if relu:
                    return
                src = score_bank()
                flat = b.sc[:].rearrange("p g b l -> p (g b) l")
                if causal:
                    nc.vector.tensor_tensor(flat, src, spread(k.causal, NG * BT, 1), ALU.add).then_inc(s.masked, 1)
                    dve.wait_ge(s.masked, i + 1)
                    src = flat
                top = b.m[:].rearrange("p g b -> p (g b)")
                nc.vector.tensor_reduce(top, src, AX.X, ALU.max).then_inc(s.max_ready, 1)
                dve.wait_ge(s.max_ready, i + 1)
                nc.vector.tensor_tensor(flat, src, spread(top, S, 2), ALU.subtract).then_inc(s.shifted, 1)

            def sums(i):
                dve.wait_ge(s.probs_ready, i + 1)
                if relu:
                    nc.vector.tensor_reduce(b.sums[:], b.p[:], AX.X, ALU.add).then_inc(s.sums_raw, 1)
                    dve.wait_ge(s.sums_raw, i + 1)
                    nc.vector.tensor_scalar(b.sums[:], b.sums[:], 1e-6, None, ALU.add).then_inc(s.sums_ready, 1)
                else:
                    nc.vector.tensor_reduce(b.sums[:], b.p[:], AX.X, ALU.add).then_inc(s.sums_ready, 1)
                dve.wait_ge(s.sums_ready, i + 1)
                nc.vector.reciprocal(b.rsum[:], b.sums[:]).then_inc(s.rsum_ready, 1)

            def add(i):
                dve.wait_ge(s.y_done, i + 1)
                tile = into[:, ds(i, 1), :].rearrange("p a d -> p (a d)")
                nc.vector.tensor_tensor(tile, tile, k.ps[:, YB, 0:D], ALU.add).then_inc(s.y_added, 1)

            def body(i, first, last, ahead):
                sums(i)
                if not last:
                    shift(i + 1)
                dve.wait_ge(s.rsum_ready, i + 1)
                dve.wait_ge(s.pv_done, i + 1)
                for h in range(4):
                    rows = slice(h * S, (h + 1) * S)
                    own = k.ps[rows, OB:OB + 2, :].rearrange("p a (g b h d) -> p (a g) b h d", g=2, b=BT, h=4)[:, :, :, h, :]
                    out = b.o[rows, :, 0:NG * HD].rearrange("p b (g d) -> p g b d", g=NG)
                    o = nc.vector.tensor_tensor(out, own, spread(b.rsum[rows, :, :], HD, 3), ALU.mult)
                o.then_inc(s.o_ready, 1)
                if ahead:
                    spread_first(i + 2)
                if not first:
                    add(i - 1)

            spread_first(0)
            dve.wait_ge(*w.at)
            dve.wait_ge(s.cleared, 1)
            dve.sem_inc(s.y_added, 1)
            if w.bo is not None:
                nc.vector.tensor_tensor(into[:], into[:], spread(w.bo, NT, 1), ALU.add).then_inc(s.y_biased, 1)
            shift(0)
            if relu:
                dve.wait_ge(s.scores_done, 1)
            spread_first(1)
            if w.bo is not None:
                dve.wait_ge(s.y_biased, 1)
            body(0, True, False, True)
            with dve.Fori(1, NT - 2) as i:
                body(i, False, False, True)
            body(NT - 2, False, False, False)
            body(NT - 1, False, True, False)
            add(NT - 1)


def phase_features(k, w, qk, ph, amp, sn, cs):
    nc = k.nc
    PI = float(np.float32(np.pi))
    names = ("abs_done exp_done plus_done rest_done ln_done sum_done amp_done square_done sums_done root_done recip_done spread_done wide_done "
             "norm_done tanh_done rise_done fold_done sin_done cos_done lam_tanh lam_done const_done")
    with stage(k, names) as (block, s), \
            buffers(k, f=[P, 2, DC, T], rms=[P, 2, 2, NT, DC, 8], eps=[P, 1], half=[P, 1], lam=[P, 2, DC]) as b:
        def roots(u):
            return b.f[:, u].rearrange("p c t -> p (c t)").rearrange("p (a ch) -> p a ch", ch=P)

        @block.vector
        def _(dve):
            for u in range(2):
                nc.vector.scalar_tensor_tensor(amp[:, u], qk[:, u], -1.0, qk[:, u], ALU.mult, ALU.max).then_inc(s.abs_done, 1)
            for u in range(2):
                dve.wait_ge(s.exp_done, u + 1)
                nc.vector.tensor_scalar(b.f[:, u], amp[:, u], 1.0, None, ALU.add).then_inc(s.plus_done, 1)
                dve.wait_ge(s.plus_done, u + 1)
                nc.vector.scalar_tensor_tensor(amp[:, u], b.f[:, u], -1.0, amp[:, u], ALU.add,
                                               ALU.subtract).then_inc(s.rest_done, 1)
            for u in range(2):
                dve.wait_ge(s.ln_done, u + 1)
                nc.vector.scalar_tensor_tensor(b.f[:, u], qk[:, u], 0.0, b.f[:, u], ALU.max, ALU.add).then_inc(s.sum_done, 1)
                dve.wait_ge(s.sum_done, u + 1)
                dve.wait_ge(s.rest_done, u + 1)
                nc.vector.tensor_tensor(amp[:, u], b.f[:, u], amp[:, u], ALU.subtract).then_inc(s.amp_done, 1)
                dve.wait_ge(s.amp_done, u + 1)
                nc.vector.tensor_tensor(b.f[:, u], amp[:, u], amp[:, u], ALU.mult).then_inc(s.square_done, 1)
            dve.wait_ge(s.lam_tanh, 1)
            nc.vector.tensor_scalar(b.lam[:, 1], b.lam[:, 0], 0.5, None, ALU.mult).then_inc(s.lam_done, 1)
            for u in range(2):
                dve.wait_ge(s.root_done, u + 1)
                nc.vector.reciprocal(b.rms[:, 1, u], b.rms[:, 0, u]).then_inc(s.recip_done, 1)
            for u in range(2):
                for q in range(4):
                    dve.wait_ge(s.wide_done, 4 * u + q + 1)
                    part = amp[:, u, q // 2, (q % 2) * 512:(q % 2) * 512 + 512]
                    nc.vector.tensor_tensor(part, part, k.ps[:, 4 * u + q, :], ALU.mult).then_inc(s.norm_done, 1)
            dve.wait_ge(s.norm_done, 8)
            dve.wait_ge(s.lam_done, 1)
            for done, t in ((s.sin_done, sn), (s.cos_done, cs)):
                dve.wait_ge(done, 2)
                for c in range(DC):
                    nc.vector.scalar_tensor_tensor(t[:, 0, c], t[:, 0, c], b.lam[:, 1, c:c + 1], amp[:, 0, c],
                                                   ALU.mult, ALU.mult)
            nc.vector.tensor_tensor(cs[:, 1], cs[:, 1], amp[:, 1], ALU.mult)

        @block.scalar
        def _(act):
            act.wait_ge(*w.at)
            nc.scalar.activation(b.lam[:, 0], w.lam, ACT.Tanh).then_inc(s.lam_tanh, 1)
            for u in range(2):
                nc.scalar.activation(ph[:, u], ph[:, u], ACT.Tanh).then_inc(s.tanh_done, 1)
            for u in range(2):
                act.wait_ge(s.abs_done, u + 1)
                nc.scalar.activation(amp[:, u], amp[:, u], ACT.Exp, scale=-1.0).then_inc(s.exp_done, 1)
            for u in range(2):
                act.wait_ge(s.plus_done, u + 1)
                act.wait_ge(s.rest_done, u + 1)
                nc.scalar.activation(b.f[:, u], b.f[:, u], ACT.Ln).then_inc(s.ln_done, 1)
            act.wait_ge(s.tanh_done, 2)
            act.wait_ge(s.const_done, 2)
            for u in range(2):
                nc.scalar.activation(sn[:, u], ph[:, u], ACT.Sin, scale=PI).then_inc(s.sin_done, 1)
            for u in range(2):
                act.wait_ge(s.fold_done, u + 1)
                nc.scalar.activation(cs[:, u], cs[:, u], ACT.Sin, bias=b.half[:, 0:1], scale=-PI).then_inc(s.cos_done, 1)
            for u in range(2):
                act.wait_ge(s.sums_done, u + 1)
                nc.scalar.activation(b.rms[:, 0, u].rearrange("p t c h -> p (t c h)"), k.ps[:, 4 + u, 0:P], ACT.Sqrt,
                                     bias=b.eps[:, 0:1], scale=1.0 / 16).then_inc(s.root_done, 1)
            for u in range(2):
                act.wait_ge(s.recip_done, u + 1)
                inverse = b.rms[:, 1, u].rearrange("p t c h -> p (t c h)")
                nc.scalar.copy(roots(u).rearrange("p a (h d) -> p (a h) d", d=16), spread(inverse, 16, 2)).then_inc(s.spread_done, 1)

        @block.gpsimd
        def _(pool):
            nc.gpsimd.memset(b.eps[:], 1e-6).then_inc(s.const_done, 1)
            nc.gpsimd.memset(b.half[:], PI / 2).then_inc(s.const_done, 1)
            for u in range(2):
                pool.wait_ge(s.tanh_done, u + 1)
                nc.gpsimd.tensor_scalar(cs[:, u], ph[:, u], 0.0, 2.0, ALU.max, ALU.mult).then_inc(s.rise_done, 1)
                pool.wait_ge(s.rise_done, u + 1)
                nc.gpsimd.tensor_tensor(cs[:, u], cs[:, u], ph[:, u], ALU.subtract).then_inc(s.fold_done, 1)
            pool.wait_ge(s.norm_done, 8)
            pool.wait_ge(s.sin_done, 2)
            nc.gpsimd.tensor_tensor(sn[:, 1], sn[:, 1], amp[:, 1], ALU.mult)

        @block.tensor
        def _(pe):
            for u in range(2):
                pe.wait_ge(s.square_done, u + 1)
                for t in range(NT):
                    for c in range(DC):
                        at = (t * DC + c) * 8
                        mm = nc.tensor.matmul(k.ps[:, 4 + u, at:at + 8], b.f[:, u, c, t * P:(t + 1) * P], k.head8,
                                              start=True, stop=True)
                mm.then_inc(s.sums_done, 1)
            for u in range(2):
                pe.wait_ge(s.spread_done, u + 1)
                for c in range(DC):
                    for half in range(2):
                        for t in range(4):
                            mm = nc.tensor.transpose(k.ps[:, 4 * u + 2 * c + half, t * P:(t + 1) * P],
                                                     roots(u)[:, (half * 4 + t) * DC + c, :], k.ident)
                        mm.then_inc(s.wide_done, 1)


def gate(k, w, n_exp, top, kind, comb, comb_t):
    nc = k.nc
    E = n_exp
    CAP = int(1.25 * T * top / E)
    W = NT * E
    down = k.down8 if E == 8 else k.down16
    mm_name = "logits_done step exp_done mask_ready spread_done comb_ready turned"
    with stage(k, mm_name) as (block, s), \
            buffers(k, l=[P, NT, E], r=[P, NT, E], eq=[P, NT, E], pick=[P, NT, E], mask=[P, NT, E], pr=[P, NT, E],
                    m=[P, NT], m1=[P, NT], sm=[P, NT], rs=[P, NT]) as b:

        @block.tensor
        def _(pe):
            pe.wait_ge(*w.at)
            for t in range(NT):
                for c in range(DC):
                    mm = nc.tensor.matmul(k.ps[:, 0, t * E:(t + 1) * E], k.ht[:, c, t * P:(t + 1) * P], w.gate[:, c, :],
                                          start=c == 0, stop=c == DC - 1)
            mm.then_inc(s.logits_done, 1)
            if kind in ("sequence", "capacity"):
                pe.wait_ge(s.mask_ready, 1)
                flat = b.mask[:].rearrange("p t e -> p (t e)")
                if kind == "sequence":
                    mm = nc.tensor.matmul(k.ps[:, 1, 0:W], k.first, flat, start=True, stop=True)
                else:
                    mm = nc.tensor.matmul(k.ps[:, 1, 0:W], k.before, flat, start=True, stop=False)
                    for t in range(NT - 1):
                        mm = nc.tensor.matmul(k.ps[:, 1, (t + 1) * E:W], k.ones, spread(b.mask[:, t, :], NT - 1 - t, 1),
                                              start=False, stop=t == NT - 2)
                mm.then_inc(s.spread_done, 1)
            if comb_t is not None:
                pe.wait_ge(s.comb_ready, 1)
                for t in range(NT):
                    mm = nc.tensor.transpose(k.ps[0:E, 2 + t // 4, (t % 4) * P:(t % 4 + 1) * P], comb[:, t, :], k.ident)
                mm.then_inc(s.turned, 1)

        @block.scalar
        def _(act):
            if kind != "sequence":
                act.wait_ge(s.step, EXP_AT[kind])
                nc.scalar.activation(b.pr[:], b.pr[:], ACT.Exp,
                                     scale=-1.0 if kind == "capacity" else 1.0).then_inc(s.exp_done, 1)
            if comb_t is not None:
                act.wait_ge(s.turned, 1)
                nc.scalar.copy(comb_t[:].rearrange("e (a n) -> e a n", a=2), k.ps[0:E, 2:4, :])

        @block.vector
        def _(dve):
            steps = [0]

            def step(ins):
                steps[0] += 1
                ins.then_inc(s.step, 1)
                dve.wait_ge(s.step, steps[0])

            def over_experts(a):
                return spread(a[:], E, 2)

            dve.wait_ge(*w.at)
            dve.wait_ge(s.logits_done, 1)
            logits = k.ps[:, 0, 0:W].rearrange("p (t e) -> p t e", e=E)
            if w.gb is None:
                step(nc.vector.tensor_copy(b.l[:], logits))
            else:
                step(nc.vector.tensor_tensor(b.l[:], logits, spread(w.gb, NT, 1), ALU.add))
            if kind == "capacity":
                step(nc.vector.tensor_copy(b.pr[:], b.l[:]))
            elif kind != "sequence":
                step(nc.vector.tensor_reduce(b.m1[:], b.l[:], AX.X, ALU.max))
                step(nc.vector.tensor_tensor(b.pr[:], b.l[:], over_experts(b.m1), ALU.subtract))
            step(nc.vector.tensor_copy(b.r[:], b.l[:]))
            for n in range(top):
                step(nc.vector.tensor_reduce(b.m[:], b.r[:], AX.X, ALU.max))
                step(nc.vector.tensor_tensor(b.eq[:], b.r[:], over_experts(b.m), ALU.is_equal))
                step(nc.vector.tensor_tensor(b.eq[:], b.eq[:], spread(down, NT, 1), ALU.mult))
                step(nc.vector.tensor_reduce(b.m[:], b.eq[:], AX.X, ALU.max))
                step(nc.vector.tensor_tensor(b.pick[:], b.eq[:], over_experts(b.m), ALU.is_equal))
                if n == 0:
                    step(nc.vector.tensor_copy(b.mask[:], b.pick[:]))
                else:
                    step(nc.vector.tensor_tensor(b.mask[:], b.mask[:], b.pick[:], ALU.add))
                if n < top - 1:
                    step(nc.vector.scalar_tensor_tensor(b.r[:], b.pick[:], NEG, b.r[:], ALU.mult, ALU.add))
            if kind == "sequence":
                dve.sem_inc(s.mask_ready, 1)
                dve.wait_ge(s.spread_done, 1)
                chosen = k.ps[:, 1, 0:W].rearrange("p (t e) -> p t e", e=E)
                nc.vector.tensor_scalar(comb[:], chosen, 1.0 / top, None, ALU.mult).then_inc(s.comb_ready, 1)
                return
            dve.wait_ge(s.exp_done, 1)
            if kind == "capacity":
                dve.sem_inc(s.mask_ready, 1)
                step(nc.vector.tensor_scalar(b.pr[:], b.pr[:], 1.0, None, ALU.add))
                step(nc.vector.reciprocal(b.pr[:], b.pr[:]))
            if kind == "masked":
                step(nc.vector.tensor_reduce(b.sm[:], b.pr[:], AX.X, ALU.add))
                step(nc.vector.reciprocal(b.rs[:], b.sm[:]))
                step(nc.vector.tensor_tensor(b.pr[:], b.pr[:], over_experts(b.rs), ALU.mult))
            step(nc.vector.tensor_tensor(b.pr[:], b.pr[:], b.mask[:], ALU.mult))
            step(nc.vector.tensor_reduce(b.sm[:], b.pr[:], AX.X, ALU.add))
            if kind == "masked":
                step(nc.vector.tensor_scalar(b.sm[:], b.sm[:], 1e-12, None, ALU.max))
            if kind == "capacity":
                step(nc.vector.tensor_scalar(b.sm[:], b.sm[:], 1e-6, None, ALU.add))
            step(nc.vector.reciprocal(b.rs[:], b.sm[:]))
            if kind == "capacity":
                step(nc.vector.tensor_tensor(b.pr[:], b.pr[:], over_experts(b.rs), ALU.mult))
                dve.wait_ge(s.spread_done, 1)
                ranks = k.ps[:, 1, 0:W].rearrange("p (t e) -> p t e", e=E)
                step(nc.vector.tensor_scalar(b.eq[:], ranks, float(CAP), None, ALU.is_lt))
                nc.vector.tensor_tensor(comb[:], b.pr[:], b.eq[:], ALU.mult).then_inc(s.comb_ready, 1)
            else:
                nc.vector.tensor_tensor(comb[:], b.pr[:], over_experts(b.rs), ALU.mult).then_inc(s.comb_ready, 1)


EXP_AT = {"softmax": 3, "masked": 3, "capacity": 2}


def ffn(k, w, n_exp, hid, w1, w2, func, comb, comb_t, into, b1=None, row_bias=None, also=None, raw=None):
    nc = k.nc
    HC = hid // P
    RING = 4
    UNITS = min(4, 2 * n_exp)
    TURNS = max(1, n_exp // 2)
    loads_here = 1 if raw is None else 0
    names = ("raw1_loaded raw2_loaded w1_hi w1_split w2_hi w2_split x_hi x_split h_done g_ready g_hi g_split y_done "
             "y_free bias_done bias_added bias_placed also_added")
    with stage(k, names) as (block, s), \
            (buffers(k, raw1=[P, DC, hid], raw2=[P, HC, D]) if raw is None else nullcontext(raw)) as given, \
            buffers(k, g=[P, RING, 512], bias=[P, 2, HC]) as b, \
            buffers(k, F32R, x=[P, 2, DC, T], w1=[P, 2, 2, DC, hid], w2=[P, 2, 2, HC, D], g=[P, 2, RING, 512]) as r:
        HI, LO = 0, 1
        TERMS = ((HI, HI), (HI, LO), (LO, HI))

        def chunk(it, j, h):
            return (4 * it + j) * HC + h

        def slot(j, h):
            return (j * HC + h) % RING

        def ahead(it, j, h, n):
            at = j * HC + h + n
            return it + at // (4 * HC), at // HC % 4, at % HC

        @block.sync
        def _(sp):
            def load(e):
                sp.dma_start(given.raw1[:], w1[ds(e, 1)].rearrange("a p c n -> (a p) c n")).then_inc(s.raw1_loaded, 16)
                sp.dma_start(given.raw2[:], w2[ds(e, 1)].rearrange("a p c n -> (a p) c n")).then_inc(s.raw2_loaded, 16)

            if raw is None:
                load(0)
            fetch_weights(k, sp)
            if n_exp > 1:
                with sp.Fori(0, n_exp - 1) as e:
                    sp.wait_ge(s.w1_split, e + 1)
                    sp.wait_ge(s.w2_split, e + 1)
                    load(e + 1)

        @block.tensor
        def _(pe):
            def hidden(it, j, h):
                if h == 0 and j % 2 == 0:
                    pe.wait_ge(s.w1_split, 2 * it + j // 2 + 1)
                pe.wait_ge(s.g_ready, chunk(it, j, h) + 1)
                for t, (p1, p2) in enumerate(TERMS):
                    for c in range(DC):
                        mm = nc.tensor.matmul(k.ps[:, slot(j, h), :], r.w1[:, j // 2, p1, c, h * P:(h + 1) * P],
                                              r.x[:, p2, c, (j % 2) * 512:(j % 2 + 1) * 512],
                                              start=t == 0 and c == 0, stop=t == 2 and c == DC - 1)
                mm.then_inc(s.h_done, 1)

            def outputs(it, j, h):
                if h == 0 and j % 2 == 0:
                    pe.wait_ge(s.w2_split, 2 * it + j // 2 + 1)
                pe.wait_ge(s.g_split, chunk(it, j, h) + 1 + RING)
                for t in range(4):
                    if h == 0:
                        pe.wait_ge(s.y_free, 4 * (4 * it + j) + t + 1)
                    for i, (p1, p2) in enumerate(TERMS):
                        mm = nc.tensor.matmul(k.ps[:, 4 + t, 0:D], r.g[:, p1, slot(j, h), t * P:(t + 1) * P],
                                              r.w2[:, j // 2, p2, h, :], start=h == 0 and i == 0,
                                              stop=h == HC - 1 and i == 2)
                    if h == HC - 1:
                        mm.then_inc(s.y_done, 1)

            def body(it, last):
                for j in range(UNITS):
                    for h in range(HC):
                        if not (last and j * HC + h + 2 >= UNITS * HC):
                            hidden(*ahead(it, j, h, 2))
                        outputs(it, j, h)

            if comb_t is not None:
                for t in range(NT):
                    mm = nc.tensor.matmul(k.ps[:, 4 + t // 2, (t % 2) * D:(t % 2 + 1) * D], comb_t[:, t * P:(t + 1) * P],
                                          w.b2[0:n_exp, :], start=True, stop=True)
                mm.then_inc(s.bias_done, 1)
            pe.wait_ge(s.x_split, 1)
            hidden(0, 0, 0)
            hidden(0, 0, 1)
            if TURNS > 1:
                with pe.Fori(0, TURNS - 1) as it:
                    body(it, False)
            body(TURNS - 1, True)

        @block.scalar
        def _(act):
            def round_w1(e, par):
                if raw is None or par != 0 or not isinstance(e, int):
                    act.wait_ge(s.raw1_loaded, 16 * (e + loads_here))
                nc.scalar.copy(r.w1[:, par, HI], given.raw1[:]).then_inc(s.w1_hi, 1)

            def round_w2(e, par):
                if raw is None or par != 0 or not isinstance(e, int):
                    act.wait_ge(s.raw2_loaded, 16 * (e + loads_here))
                nc.scalar.copy(r.w2[:, par, HI], given.raw2[:]).then_inc(s.w2_hi, 1)

            def values(it, j, h):
                if b1 is not None and h == 0 and j % 2 == 0:
                    e = 2 * it + j // 2
                    nc.scalar.copy(b.bias[:, j // 2, :], b1[:, ds(e * HC, HC)]).then_inc(s.bias_placed, 1)
                    act.wait_ge(s.bias_placed, e + 1)
                act.wait_ge(s.g_split, chunk(it, j, h) + 1)
                act.wait_ge(s.h_done, chunk(it, j, h) + 1)
                out, inp = b.g[:, slot(j, h), :], k.ps[:, slot(j, h), :]
                if b1 is None:
                    nc.scalar.activation(out, inp, func).then_inc(s.g_ready, 1)
                else:
                    nc.scalar.activation(out, inp, func, bias=b.bias[:, j // 2, h:h + 1]).then_inc(s.g_ready, 1)

            def body(it, last):
                for j in range(UNITS):
                    for h in range(HC):
                        values(it, j, h)
                        more = not (last and j // 2 == (UNITS - 1) // 2)
                        if more and (j % 2) * HC + h == 1:
                            round_w1(2 * it + j // 2 + 1, 1 - j // 2)
                        if more and (j % 2) * HC + h == 2:
                            round_w2(2 * it + j // 2 + 1, 1 - j // 2)

            act.sem_inc(s.g_ready, RING)
            nc.scalar.copy(r.x[:, HI], k.ht[:]).then_inc(s.x_hi, 1)
            round_w1(0, 0)
            round_w2(0, 0)
            if b1 is not None:
                act.wait_ge(*w.at)
            if TURNS > 1:
                with act.Fori(0, TURNS - 1) as it:
                    body(it, False)
            body(TURNS - 1, True)

        @block.gpsimd
        def _(pool):
            def rest_w1(e, par):
                pool.wait_ge(s.w1_hi, e + 1)
                nc.gpsimd.tensor_tensor(r.w1[:, par, LO], given.raw1[:], r.w1[:, par, HI], ALU.subtract).then_inc(s.w1_split, 1)

            def rest_w2(e, par):
                pool.wait_ge(s.w2_hi, e + 1)
                nc.gpsimd.tensor_tensor(r.w2[:, par, LO], given.raw2[:], r.w2[:, par, HI], ALU.subtract).then_inc(s.w2_split, 1)

            rest_w2(0, 0)
            if n_exp > 1:
                if TURNS > 1:
                    with pool.Fori(0, TURNS - 1) as it:
                        for e, par in ((2 * it + 1, 1), (2 * it + 2, 0)):
                            rest_w1(e, par)
                            rest_w2(e, par)
                rest_w1(n_exp - 1, 1)
                rest_w2(n_exp - 1, 1)

        @block.vector
        def _(dve):
            def split(it, j, h):
                g, hi, lo = b.g[:, slot(j, h), :], r.g[:, HI, slot(j, h), :], r.g[:, LO, slot(j, h), :]
                dve.wait_ge(s.g_ready, chunk(it, j, h) + 1 + RING)
                nc.vector.tensor_copy(hi, g).then_inc(s.g_hi, 1)
                dve.wait_ge(s.g_hi, chunk(it, j, h) + 1)
                nc.vector.tensor_tensor(lo, g, hi, ALU.subtract).then_inc(s.g_split, 1)

            def add(it, j):
                half = j % 2
                for t in range(4):
                    dve.wait_ge(s.y_done, 4 * (4 * it + j) + t + 1)
                    tile = into[:, half * 4 + t, :]
                    if comb is None:
                        nc.vector.tensor_tensor(tile, tile, k.ps[:, 4 + t, 0:D], ALU.add).then_inc(s.y_free, 1)
                    else:
                        share = comb[:, half * 4 + t, ds(2 * it + j // 2, 1)]
                        nc.vector.scalar_tensor_tensor(tile, k.ps[:, 4 + t, 0:D], share, tile, ALU.mult,
                                                       ALU.add).then_inc(s.y_free, 1)

            def body(it, last):
                for j in range(UNITS):
                    for h in range(1, HC):
                        split(it, j, h)
                    if not (last and j == UNITS - 1):
                        split(*ahead(it, j, 0, HC))
                    add(it, j)

            dve.sem_inc(s.g_split, RING)
            dve.wait_ge(s.x_hi, 1)
            nc.vector.tensor_tensor(r.x[:, LO], k.ht[:], r.x[:, HI], ALU.subtract).then_inc(s.x_split, 1)
            dve.wait_ge(s.w1_hi, 1)
            nc.vector.tensor_tensor(r.w1[:, 0, LO], given.raw1[:], r.w1[:, 0, HI], ALU.subtract).then_inc(s.w1_split, 1)
            if comb_t is not None:
                dve.wait_ge(s.bias_done, 1)
                nc.vector.tensor_tensor(into[:], into[:], k.ps[:, 4:8, :].rearrange("p a (t d) -> p (a t) d", d=D),
                                        ALU.add).then_inc(s.bias_added, 1)
                dve.wait_ge(s.bias_added, 1)
            if also is not None:
                nc.vector.tensor_tensor(into[:], into[:], also[:], ALU.add).then_inc(s.also_added, 1)
                dve.wait_ge(s.also_added, 1)
            if row_bias is not None:
                dve.wait_ge(*w.at)
                nc.vector.tensor_tensor(into[:], into[:], spread(row_bias, NT, 1), ALU.add).then_inc(s.bias_added, 1)
                dve.wait_ge(s.bias_added, 1)
            dve.sem_inc(s.y_free, 4)
            split(0, 0, 0)
            if TURNS > 1:
                with dve.Fori(0, TURNS - 1) as it:
                    body(it, False)
            body(TURNS - 1, True)


def clear(k, view):
    nc = k.nc
    with stage(k, "cleared") as (block, s):
        @block.gpsimd
        def _(pool):
            for c in range(view.shape[1]):
                nc.gpsimd.memset(view[:, c], 0.0).then_inc(s.cleared, 1)


def convolve(k, w, hp, ct):
    nc = k.nc
    taps = w.conv.shape[2]
    with stage(k, "conv_done") as (block, s):
        @block.tensor
        def _(pe):
            pe.wait_ge(*w.at)
            for m in range(DC):
                for half in range(2):
                    for j in range(taps):
                        mm = nc.tensor.matmul(k.ps[:, 2 * m + half, :], w.conv[:, m, j, :],
                                              hp[:, m, half * 16:(half + 1) * 16, j:j + S], start=j == 0, stop=j == taps - 1)
                    mm.then_inc(s.conv_done, 1)

        @block.scalar
        def _(act):
            for q in (0, 2):
                act.wait_ge(s.conv_done, q + 1)
                nc.scalar.activation(ct[:, q // 2, 0:512], k.ps[:, q, :], ACT.Identity, bias=w.cb[:, q // 2:q // 2 + 1])

        @block.vector
        def _(dve):
            for q in (1, 3):
                dve.wait_ge(s.conv_done, q + 1)
                nc.vector.tensor_scalar(ct[:, q // 2, 512:1024], k.ps[:, q, :], w.cb[:, q // 2:q // 2 + 1], None, ALU.add)


def pool_keys(k, q, key, v):
    nc = k.nc
    names = "q_sums q_means q_keys k_sums k_means"
    with stage(k, names) as (block, s), buffers(k, acc=[P, DC, T]) as b:
        @block.vector
        def _(dve):
            dve.wait_ge(k.late_loaded, 16)
            for c in range(DC):
                nc.vector.tensor_tensor_scan(b.acc[:, c, :], k.keep, q[:, c, :], 0.0, ALU.mult, ALU.add).then_inc(s.q_sums, 1)
            for c in range(DC):
                dve.wait_ge(s.q_sums, c + 1)
                nc.vector.tensor_tensor(q[:, c, :], b.acc[:, c, :], k.rcount, ALU.mult).then_inc(s.q_means, 1)
            for c in range(DC):
                dve.wait_ge(s.q_means, c + 1)
                nc.vector.tensor_tensor(key[:, c, :], q[:, c, :], key[:, c, :], ALU.mult).then_inc(s.q_keys, 1)
            for c in range(DC):
                dve.wait_ge(s.q_keys, c + 1)
                nc.vector.tensor_tensor_scan(b.acc[:, c, :], k.keep, key[:, c, :], 0.0, ALU.mult, ALU.add).then_inc(s.k_sums, 1)
            for c in range(DC):
                dve.wait_ge(s.k_sums, c + 1)
                nc.vector.tensor_tensor(key[:, c, :], b.acc[:, c, :], k.rcount, ALU.mult).then_inc(s.k_means, 1)
            for c in range(DC):
                dve.wait_ge(s.k_means, c + 1)
                nc.vector.tensor_tensor(v[:, c, :], key[:, c, :], v[:, c, :], ALU.mult)


def wide_cross_attention(k, w, qt, given):
    nc = k.nc
    SB, PB, OB = 6, 7, 4
    names = ("w_hi w_split ctx_hi ctx_low ctx_split tail_done tail_ready tail_placed ctx_loaded0 ctx_loaded1 ctx_loaded2 ctx_loaded3 keys_done "
             "keys_ready values_done values_ready q_placed scores_done max_ready probs_ready tail_spread turned_done "
             "turned_ready rsum_ready o_done x_ready")
    with stage(k, names) as (block, s), \
            buffers(k, vtail=[B, D], vt=[BT, NT, D],
                    key=[P, BT, DC, LK], val=[P, BT, 2, D], q=[P, DC, P], p=[P, LK], pb=[P, BT], nmax=[P, 1],
                    sums=[P, 1], rsum=[P, 1], pt=[P, 2, P], ptt=[BT, P]) as b, \
            buffers(k, F32R, w=[P, 2, 2, 2 * D], c=[P, BT, 2, LP], clo=[P, BT, LP]) as r:
        ctx_loaded = [s.ctx_loaded0, s.ctx_loaded1, s.ctx_loaded2, s.ctx_loaded3]

        def factors(j, at, rows):
            whi, wlo = r.w[:, 0, :, at], r.w[:, 1, :, at]
            return ((whi[:, 0], r.c[:, j, 0, rows]), (whi[:, 0], r.clo[:, j, rows]), (wlo[:, 0], r.c[:, j, 0, rows]),
                    (whi[:, 1], r.c[:, j, 1, rows]), (wlo[0:DK - P, 1], r.c[0:DK - P, j, 1, rows]))

        @block.sync
        def _(sp):
            def load(i, j):
                n = i * BT + j
                sp.dma_start(given.c[:, j], k.ctx[ds(n, 1)].rearrange("a p c l -> (a p) c l")).then_inc(ctx_loaded[j], 16)

            sp.wait_ge(s.tail_ready, 1)
            for j in range(BT):
                sp.dma_start(b.vt[j:j + 1, :, :], b.vtail[j:B:BT, :]).then_inc(s.tail_placed, 16)
            with sp.Fori(0, NT - 1) as i:
                for j in range(BT):
                    sp.wait_ge(s.ctx_low, i * BT + j + 1)
                    sp.wait_ge(s.ctx_split, i * BT + j + 1)
                    load(i + 1, j)

        @block.gpsimd
        def _(pool):
            def place(i):
                nc.gpsimd.tensor_copy(b.q[:], qt[:, :, ds(i * P, P)]).then_inc(s.q_placed, 1)

            def split_context(i):
                for j in range(BT):
                    pool.wait_ge(s.ctx_hi, i * BT + j + 1)
                    nc.gpsimd.tensor_tensor(r.clo[:, j, :], given.c[:, j, 0, :], r.c[:, j, 0, :],
                                            ALU.subtract).then_inc(s.ctx_split, 1)

            split_context(0)
            place(0)
            with pool.Fori(0, NT - 1) as i:
                split_context(i + 1)
                pool.wait_ge(s.scores_done, i + 1)
                place(i + 1)

        @block.tensor
        def _(pe):
            pe.wait_ge(*w.at)
            for c, t, kr in ((0, given.t0, P), (1, given.t1, DK - P)):
                mm = nc.tensor.matmul(k.ps[0:B, 7, 0:D], t[:], w.wv[0:kr, c, :], start=c == 0, stop=c == 1)
            mm.then_inc(s.tail_done, 1)
            pe.wait_ge(s.w_split, 2)

            def keys(i, first=False):
                for j in range(BT):
                    pe.wait_ge(s.ctx_low, i * BT + j + 1)
                    pe.wait_ge(s.ctx_split, i * BT + j + 1)
                    if not (first and j < 2):
                        pe.wait_ge(s.keys_ready, i * BT + j - 1)
                    for m in range(DC):
                        for t, (wp, cp) in enumerate(factors(j, slice(m * P, (m + 1) * P), slice(0, LP))):
                            mm = nc.tensor.matmul(k.ps[:, 2 * (j % 2) + m, 0:LP], wp, cp, start=t == 0, stop=t == 4)
                    mm.then_inc(s.keys_done, 1)

            def values(i, first=False):
                for j in range(BT):
                    if not (first and j < 2):
                        pe.wait_ge(s.values_ready, i * BT + j - 1)
                    if j == 1 and not first:
                        pe.wait_ge(s.x_ready, i)
                    bank = 5 - j % 2
                    for half in range(2):
                        for t, (wp, cp) in enumerate(factors(j, slice(D, 2 * D), slice(half * P, (half + 1) * P))):
                            mm = nc.tensor.matmul(k.ps[:, bank, half * D:(half + 1) * D], cp, wp, start=t == 0, stop=t == 4)
                    mm.then_inc(s.values_done, 1)

            def body(i, last):
                pe.wait_ge(s.keys_ready, (i + 1) * BT)
                pe.wait_ge(s.q_placed, i + 1)
                for j in range(BT):
                    for c in range(DC):
                        mm = nc.tensor.matmul(k.ps[j * S:(j + 1) * S, SB, 0:LK], b.q[:, c, j * S:(j + 1) * S],
                                              b.key[:, j, c, :], start=c == 0, stop=c == DC - 1)
                mm.then_inc(s.scores_done, 1)
                if not last:
                    keys(i + 1)
                pe.wait_ge(s.tail_spread, i + 1)
                for half in range(2):
                    nc.tensor.transpose(k.ps[:, PB, half * P:(half + 1) * P], b.p[:, half * P:(half + 1) * P], k.ident)
                nc.tensor.transpose(k.ps[0:BT, PB, 2 * P:3 * P], b.pb[:], k.ident).then_inc(s.turned_done, 1)
                pe.wait_ge(s.turned_ready, i + 1)
                pe.wait_ge(s.values_ready, (i + 1) * BT)
                nc.tensor.matmul(k.ps[:, OB, 0:D], b.ptt[:], b.vt[:, ds(i, 1), :].rearrange("g a c -> g (a c)"),
                                 start=True, stop=False, skip_group_check=True)
                for j in range(BT):
                    for half in range(2):
                        mm = nc.tensor.matmul(k.ps[j * S:(j + 1) * S, OB, 0:D], b.pt[:, half, j * S:(j + 1) * S],
                                              b.val[:, j, half, :], start=False, stop=half == 1, skip_group_check=True)
                mm.then_inc(s.o_done, 1)
                if not last:
                    values(i + 1)

            pe.wait_ge(s.tail_ready, 1)
            keys(0, first=True)
            values(0, first=True)
            pe.wait_ge(s.tail_placed, 16 * BT)
            with pe.Fori(0, NT - 1) as i:
                body(i, False)
            body(NT - 1, True)

        @block.scalar
        def _(act):
            act.wait_ge(*w.at)

            def take_keys(i):
                for j in range(BT):
                    act.wait_ge(s.keys_done, i * BT + j + 1)
                    for m in range(DC):
                        last = nc.scalar.activation(b.key[:, j, m, :], k.ps[:, 2 * (j % 2) + m, 0:LK], ACT.Identity,
                                                    bias=w.bk[:, m:m + 1])
                    last.then_inc(s.keys_ready, 1)

            def body(i, last):
                act.wait_ge(s.max_ready, i + 1)
                nc.scalar.activation(b.p[:], k.ps[:, SB, 0:LK], ACT.Exp, bias=b.nmax[:, 0:1],
                                     accum_out=b.sums[:, 0:1]).then_inc(s.probs_ready, 1)
                if not last:
                    take_keys(i + 1)

            for u, part in ((0, w.wk), (1, w.wv)):
                nc.scalar.copy(r.w[:, 0, :, u * D:(u + 1) * D], part).then_inc(s.w_hi, 1)
            take_keys(0)
            with act.Fori(0, NT - 1) as i:
                body(i, False)
            body(NT - 1, True)

        @block.vector
        def _(dve):
            def round_context(i, first=False):
                for j in range(BT):
                    if not first:
                        dve.wait_ge(ctx_loaded[j], 16 * i)
                    nc.vector.tensor_copy(r.c[:, j], given.c[:, j]).then_inc(s.ctx_hi, 1)
                    dve.wait_ge(s.ctx_hi, i * BT + j + 1)
                    low = slice(DK - P, P)
                    nc.vector.tensor_tensor(r.c[low, j, 1, :], given.c[low, j, 1, :], r.c[low, j, 1, :],
                                            ALU.subtract).then_inc(s.ctx_low, 1)

            round_context(0, first=True)
            dve.wait_ge(*w.at)
            for u, part in ((0, w.wk), (1, w.wv)):
                at = slice(u * D, (u + 1) * D)
                dve.wait_ge(s.w_hi, u + 1)
                nc.vector.tensor_tensor(r.w[:, 1, :, at], part, r.w[:, 0, :, at], ALU.subtract).then_inc(s.w_split, 1)
            dve.wait_ge(s.tail_done, 1)
            nc.vector.tensor_tensor(b.vtail[:], k.ps[0:B, 7, 0:D], w.bv[0:B, :], ALU.add).then_inc(s.tail_ready, 1)

            def take_values(i):
                for j in range(BT):
                    dve.wait_ge(s.values_done, i * BT + j + 1)
                    nc.vector.tensor_tensor(b.val[:, j, :, :], k.ps[:, 5 - j % 2, :].rearrange("p (r c) -> p r c", r=2),
                                            spread(w.bv, 2, 1), ALU.add).then_inc(s.values_ready, 1)

            def body(i, last):
                if not last:
                    round_context(i + 1)
                dve.wait_ge(s.scores_done, i + 1)
                nc.vector.tensor_reduce(b.nmax[:], k.ps[:, SB, 0:LK], AX.X, ALU.max, negate=True).then_inc(s.max_ready, 1)
                dve.wait_ge(s.probs_ready, i + 1)
                nc.vector.tensor_scalar(b.pb[:], k.seq4, b.p[:, 2 * P:LK], None, ALU.mult).then_inc(s.tail_spread, 1)
                nc.vector.reciprocal(b.rsum[:], b.sums[:]).then_inc(s.rsum_ready, 1)
                dve.wait_ge(s.turned_done, i + 1)
                nc.vector.tensor_copy(b.pt[:], k.ps[:, PB, 0:2 * P].rearrange("p (r c) -> p r c", r=2))
                nc.vector.tensor_copy(b.ptt[:], k.ps[0:BT, PB, 2 * P:3 * P]).then_inc(s.turned_ready, 1)
                dve.wait_ge(s.rsum_ready, i + 1)
                dve.wait_ge(s.o_done, i + 1)
                tile = k.x[:, ds(i, 1), :].rearrange("p a d -> p (a d)")
                nc.vector.scalar_tensor_tensor(tile, k.ps[:, OB, 0:D], b.rsum[:, 0:1], tile, ALU.mult,
                                               ALU.add).then_inc(s.x_ready, 1)
                if not last:
                    take_values(i + 1)

            take_values(0)
            with dve.Fori(0, NT - 1) as i:
                body(i, False)
            body(NT - 1, True)


def build(nc, args, packed, fields, order):
    k = Core()
    k.nc, k.stages, k.buffers = nc, 0, 0
    k.packed, k.fields, k.order = packed, fields, order
    k.in_x, k.out = args["x"], args["out_0"]
    k.in_const = args["const"]
    k.ctx, k.ctx_t0, k.ctx_t1 = (args[n] for n in ("ctx", "ctx_t0", "ctx_t1"))
    k.args = args
    with ExitStack() as ctx:
        def sb(name, *shape):
            return ctx.enter_context(nc.sbuf_tensor(f"{name}_sb", list(shape), F32))

        k.x = sb("x", P, NT, D)
        k.z = sb("z", P, NT, D)
        k.ht = sb("ht", P, DC, T)
        k.store = sb("store", P, 2, max(int(a.shape[1]) for a in packed.values()))
        k.consts = sb("consts", P, int(k.in_const.shape[1]))
        made, at = constants(), 0
        for name, a in made.items():
            made[name] = k.consts[:, at:at + a.shape[1]]
            at += a.shape[1]
        k.ident, k.head8, k.seq4, k.causal, k.first = (
            made[n] for n in ("ident", "head8", "seq4", "causal", "first"))
        k.before, k.ones, k.down8, k.down16, k.keep, k.rcount = (
            made[n] for n in ("before", "ones", "down8", "down16", "keep", "rcount"))
        k.half4 = made["half4"].rearrange("p (c h) -> p c h", c=2)
        k.ps = ctx.enter_context(nc.psum_tensor("ps", [P, 8, BANK], F32))
        k.weights_loaded = [ctx.enter_context(nc.semaphore(f"weights_loaded{h}")) for h in range(2)]
        k.stored = ctx.enter_context(nc.semaphore("stored"))
        k.late = k.consts.shape[1] - 2 * T
        k.late_started = False
        k.late_loaded = ctx.enter_context(nc.semaphore("late_loaded"))
        k.fetched, k.fetch_to = 0, 2
        load_inputs(k)

        def begin(name):
            k.fetch_to = order.index(name) + 2
            return weights(k, name)

        for name in order:
            if name == "L2_boom":
                continue
            w = begin(name)
            if name in ("L0_xattn", "L1_xattn", "L2_xattn"):
                heads, hd = (8, 64) if name == "L2_xattn" else (16, 16)
                with buffers(k, qt=[P, heads * hd // P, T], c=[P, 2, 2, LP], t0=[P, B], t1=[DK - P, B],
                             vt=[heads // 4, B, heads * hd]) as b:
                    prepare(k, k.x, k.z, jobs=[(b.qt, w.wq, w.bq, 0.25 if hd == 16 else 0.125)], w_at=w.at,
                            early=[(b.t0[:], k.ctx_t0), (b.t1[:], k.ctx_t1), (b.c[:, 0], k.ctx[0]), (b.c[:, 1], k.ctx[1])],
                            clear_early=b.vt[:])
                    cross_attention(k, w, b.qt, b, heads, hd, clamp=1.0e4 if name == "L1_xattn" else None)
            if name in ("L1_attn", "L3_attn", "L3_gqa"):
                with buffers(k, qt=[P, DC, T], kt=[P, DC, T], v=[P, NT, D]) as b:
                    prepare(k, k.x, k.z, jobs=[(b.qt, w.wq, w.bq, 1.0), (b.kt, w.wk, w.bk, 1.0)],
                            token_major=[(b.v, w.wv, w.bv)], w_at=w.at)
                    self_attention(k, w, b.qt, b.kt, b.v, k.x if name == "L3_attn" else k.z,
                                   causal=name == "L3_attn", relu=name == "L1_attn")
                if name == "L1_attn":
                    normalize(k, k.z, k.z, gain=w.gamma, shift=w.beta, w_at=w.at, add=k.x)
            if name == "L0_attn":
                with buffers(k, qk=[P, 2, DC, T], v=[P, NT, D], sn=[P, 2, DC, T], cs=[P, 2, DC, T]) as b:
                    with buffers(k, ph=[P, 2, DC, T], amp=[P, 2, DC, T]) as f:
                        prepare(k, k.x, k.z, jobs=[(b.qk[:, 0], w.wq, None, 1.0), (b.qk[:, 1], w.wk, None, 1.0),
                                                   (f.ph[:, 0], w.wqp, None, 1.0), (f.ph[:, 1], w.wkp, None, 1.0)],
                                token_major=[(b.v, w.wv, None)], w_at=w.at)
                        phase_features(k, w, b.qk, f.ph, f.amp, b.sn, b.cs)
                    self_attention(k, w, b.qk[:, 0], b.qk[:, 1], b.v, k.x, causal=True,
                                   more=[(b.sn[:, 0], b.sn[:, 1]), (b.cs[:, 0], b.cs[:, 1])])
            if name in ("L0_ffn", "L1_ffn", "L2_ffn", "L3_ffn"):
                n_exp, hid, top, kind, func = {
                    "L0_ffn": (8, 1024, 2, "softmax", ACT.Gelu), "L1_ffn": (16, 512, 3, "masked", ACT.Relu),
                    "L2_ffn": (8, 256, 2, "sequence", ACT.Gelu), "L3_ffn": (8, 512, 2, "capacity", ACT.Gelu)}[name]
                biased = name != "L3_ffn"
                w1, w2 = args[f"{name}_w1"], args[f"{name}_w2"]
                with buffers(k, raw1=[P, DC, hid], raw2=[P, hid // P, D]) as raw:
                    early = [(raw.raw1[:], w1[0]), (raw.raw2[:], w2[0])]
                    if biased:
                        prepare(k, k.x, k.z, ht=k.ht, early=early)
                    else:
                        normalize(k, k.z, k.z, rms=True, gain=gains[0], eps=1e-6, w_at=gains[2], early=early)
                        transpose_tokens(k, k.z, k.ht)
                    with buffers(k, comb=[P, NT, n_exp]) as b, \
                            (buffers(k, t=[n_exp, T]) if biased else nullcontext(None)) as turned:
                        comb_t = turned.t if biased else None
                        gate(k, w, n_exp, top, kind, b.comb, comb_t)
                        ffn(k, w, n_exp, hid, w1, w2, func, b.comb, comb_t, k.x if biased else k.z,
                            b1=w.b1.rearrange("p e h -> p (e h)") if biased else None, raw=raw)
                if not biased:
                    normalize(k, k.z, k.z, rms=True, gain=gains[1], eps=1e-6, add=k.x)
            if name == "L3_gqa":
                gains = (w.gamma, w.gamma2, w.at)
            if name == "L3_xattn":
                with buffers(k, qt=[P, DC, T], c=[P, BT, 2, LP], t0=[P, B], t1=[DK - P, B]) as b:
                    prepare(k, k.x, k.z, jobs=[(b.qt, w.wq, w.bq, 1.0 / 16)], w_at=w.at,
                            early=[(b.t0[:], k.ctx_t0), (b.t1[:], k.ctx_t1)] + [(b.c[:, j], k.ctx[j]) for j in range(BT)])
                    wide_cross_attention(k, w, b.qt, b)
            if name == "L2_attn":
                pad = w.conv.shape[2] - 1
                with buffers(k, hn=[P, NT, D]) as b:
                    normalize(k, k.x, k.z)
                    with buffers(k, hp=[P, DC, B, S + pad], ct=[P, DC, T]) as f:
                        clear(k, f.hp[:, :, :, 0:pad])
                        prepare(k, k.z, b.hn, padded=f.hp[:, :, :, pad:], gain=w.g1, shift=w.b1, w_at=w.at)
                        convolve(k, w, f.hp, f.ct)
                        transpose_channels(k, f.ct, k.z, k.z)
                    with buffers(k, q=[P, DC, T], key=[P, DC, T], v=[P, DC, T]) as f:
                        prepare(k, k.z, b.hn, jobs=[(f.q, w.wq, w.bq, 1.0), (f.key, w.wk, w.bk, 1.0),
                                                    (f.v, w.wv, w.bv, 1.0)], gain=w.g2, shift=w.b2, w_at=w.at)
                        pool_keys(k, f.q, f.key, f.v)
                        transpose_channels(k, f.v, k.z, k.z)
                    with buffers(k, raw1=[P, DC, 1024], raw2=[P, 1024 // P, D]) as raw:
                        w1, w2 = args["L2_boom_w1"], args["L2_boom_w2"]
                        prepare(k, k.z, b.hn, ht=k.ht, gain=w.g3, shift=w.b3, w_at=w.at,
                                early=[(raw.raw1[:], w1[0]), (raw.raw2[:], w2[0])])
                        w = begin("L2_boom")
                        ffn(k, w, 1, 1024, w1, w2, ACT.Gelu, None, None, k.x, b1=w.b1, row_bias=w.bo, also=k.z, raw=raw)
        store_output(k)


def unlay(y):
    return np.ascontiguousarray(y.transpose(1, 0, 2)).reshape(B, S, D)


def kernel(**inputs):
    import concourse.bacc as _bacc
    from concourse.bass_utils import run_bass_kernel_spmd as _run

    nc = _bacc.Bacc("TRN2", target_bir_lowering=False, num_devices=1)
    i = {n: np.asarray(a) for n, a in inputs.items()}
    arrays = {"x": i["x"].reshape(NT, P, D).transpose(1, 0, 2)}
    ctx = np.zeros((B, DK, LP), np.float32)
    ctx[:, :, 0:LK] = i["ctx_768"].transpose(0, 2, 1)
    arrays["ctx"] = np.stack([ctx[:, 0:P, :], np.concatenate([ctx[:, P:DK, :]] * 2, axis=1)], axis=2)
    arrays["ctx_t0"], arrays["ctx_t1"] = ctx[:, 0:P, LK - 1].T, ctx[:, P:DK, LK - 1].T
    arrays["const"] = np.concatenate(list(constants().values()), axis=1)
    order = ORDER
    fields = {}
    for name, parts in packs(i).items():
        if name in order:
            fields[name] = [(f, a.shape) for f, a in parts]
            arrays[f"w_{name}"] = np.concatenate([a.reshape(P, -1) for _, a in parts], axis=1)
    for name, a, c in (("L0_ffn", "w1", "w2"), ("L1_ffn", "W1", "W2"), ("L2_ffn", "W1", "W2"), ("L3_ffn", "w1", "w2")):
        if name in order:
            arrays[f"{name}_w1"], arrays[f"{name}_w2"] = experts(i[f"{name}_{a}"], i[f"{name}_{c}"])
    if "L2_boom" in order:
        arrays["L2_boom_w1"], arrays["L2_boom_w2"] = experts(i["L2_attn_Wb"].T[None], i["L2_attn_Wu"].T[None])
    arrays = {n: np.ascontiguousarray(a) for n, a in arrays.items()}
    args = {n: nc.dram_tensor(f"in_{n}", a.shape, mybir.dt.from_np(a.dtype), kind="ExternalInput").ap()
            for n, a in arrays.items()}
    args["out_0"] = nc.dram_tensor("out_0", (P, NT, D), F32, kind="ExternalOutput").ap()
    build(nc, args, {n: args[f"w_{n}"] for n in order}, fields, order)
    r = _run(nc, [{f"in_{n}": a for n, a in arrays.items()}], core_ids=[0])
    return unlay(r.results[0]["out_0"])
```
